# Optimizing a Trainium2 kernel written in Bass

```python
import numpy as np
import jax
import jax.numpy as jnp

def _softmax(x, axis=-1):
    return jax.nn.softmax(x, axis=axis)

def _gelu(x):
    return jax.nn.gelu(x, approximate=True)

def _silu(x):
    return jax.nn.silu(x)

def _sigmoid(x):
    return jax.nn.sigmoid(x)

def _layernorm(x, axis=-1, eps=1e-05):
    m = jnp.mean(x, axis=axis, keepdims=True)
    v = jnp.var(x, axis=axis, keepdims=True)
    return (x - m) / jnp.sqrt(v + eps)

def _scatter_add(tgt, idx, src, axis=0):
    return tgt.at[idx].add(src)

def _segment_sum(src, seg, n):
    return jax.ops.segment_sum(src, seg, n)
kernel_name = 'mk_xattn_ffn_d1_seqx_r2_1f1e10'

def setup_inputs(seed: int=0):
    np.random.seed(seed)
    _w = jnp.asarray

    def _rec_inputs():
        import jax
        import jax.numpy as jnp
        _rk = jax.random.key(seed)
        x = -0.0002928 + 1 * jax.random.normal(jax.random.fold_in(_rk, 1), (16, 256, 512), jnp.float32)
        _lenS = 256 - jax.random.randint(jax.random.fold_in(_rk, 7), (16,), 0, max(1, 256 // 4) + 1, jnp.int32)
        _lenS2 = 256 - jax.random.randint(jax.random.fold_in(_rk, 8), (16,), 0, max(1, 256 // 4) + 1, jnp.int32)
        _ctx_1024P = jax.random.normal(jax.random.fold_in(_rk, 11), (16, 16, 512), jnp.float32)
        _ctx_1024c = jax.random.dirichlet(jax.random.fold_in(_rk, 511), 0.3 * jnp.ones((16,), jnp.float32), (16, 256))
        _ctx_1024t = jnp.einsum('bsk,bkd->bsd', _ctx_1024c, _ctx_1024P)
        _ctx_1024t = _ctx_1024t * jax.lax.rsqrt(jnp.mean(jnp.square(_ctx_1024t)) + 1e-12) * 0.953939
        ctx_1024 = -1.39393e-06 + 0.999914 * (_ctx_1024t + 0.3 * jax.random.normal(jax.random.fold_in(_rk, 611), (16, 256, 512), jnp.float32))
        _validS = jnp.arange(256)[None, :] < _lenS[:, None]
        _validS2 = jnp.arange(256)[None, :] < _lenS2[:, None]
        _causal = jnp.tril(jnp.ones((256, 256), dtype=bool))
        mask_BxSxS2_bk0 = jnp.logical_not(jnp.broadcast_to(_validS2[:, None, :], (16, 256, 256)))
        return (x, ctx_1024, mask_BxSxS2_bk0)
    x, ctx_1024, mask_BxSxS2_bk0 = _rec_inputs()

    def _L0_xattn_setup():
        import jax, jax.numpy as jnp
        import numpy as np
        from math import sqrt
        B, Q, S, D, H = (2, 1024, 1024, 512, 16)
        ADIM = D // H
        IEPS = 1e-32

        def sparse_norm(scores, nbias):
            t = jax.nn.relu(scores + nbias[0])
            t = t * t
            return t / (t.sum(-1, keepdims=True) + IEPS)
        key = jax.random.key(seed)
        ks = jax.random.split(key, 7)
        sc = 0.02
        return {'iQ': jax.random.normal(ks[0], (B, Q, D), jnp.float32), 'iK': jax.random.normal(ks[1], (B, S, D), jnp.float32), 'mask': jax.random.randint(ks[2], (B, Q, S), 0, 2) > 0, 'Wq': jax.random.normal(ks[3], (D, D), jnp.float32) * sc, 'Wkv': jax.random.normal(ks[4], (2 * D, D), jnp.float32) * sc, 'Wo': jax.random.normal(ks[5], (D, D), jnp.float32) * sc, 'nbias': jnp.zeros((1,), jnp.float32)}
    _L0_xattn_all = _L0_xattn_setup()
    _L0_xattn_in = {k: v for k, v in _L0_xattn_all.items() if k in ('Wq', 'Wkv', 'Wo', 'nbias')}
    del _L0_xattn_all

    def _L0_ffn_setup():
        import jax, jax.numpy as jnp
        import numpy as np
        B, S, H = (2, 512, 512)
        E, F = (16, 256)
        G, TOPK_G, TOPK = (4, 2, 4)
        N_SHARED = 2
        ROUTE_SCALE = 1.0
        FS = N_SHARED * F

        def _gate(x, w_gate):
            T = x.shape[0]
            scores = jax.nn.sigmoid(x @ w_gate.T)
            sv = scores.reshape(T, G, E // G)
            group_scores = jax.lax.top_k(sv, 2)[0].sum(-1)
            top_groups = jax.lax.top_k(group_scores, TOPK_G)[1]
            allowed = jnp.zeros((T, G), dtype=bool).at[jnp.arange(T)[:, None], top_groups].set(True)
            masked = jnp.where(allowed[:, :, None], sv, -jnp.inf).reshape(T, E)
            _, idx = jax.lax.top_k(masked, TOPK)
            w = jnp.take_along_axis(scores, idx, axis=1)
            w = w / (w.sum(-1, keepdims=True) + 1e-06) * ROUTE_SCALE
            return (w, idx)

        def _swiglu(x, w1, w3, w2):
            return jax.nn.silu(x @ w1.T) * (x @ w3.T) @ w2.T
        key = jax.random.key(seed)
        ks = jax.random.split(key, 8)
        scale = 0.02
        return {'hidden_states': jax.random.normal(ks[0], (B, S, H), dtype=jnp.float32), 'w_gate': jax.random.normal(ks[1], (E, H), dtype=jnp.float32) * scale, 'w1_e': jax.random.normal(ks[2], (E, F, H), dtype=jnp.float32) * scale, 'w3_e': jax.random.normal(ks[3], (E, F, H), dtype=jnp.float32) * scale, 'w2_e': jax.random.normal(ks[4], (E, H, F), dtype=jnp.float32) * scale, 'w1_s': jax.random.normal(ks[5], (FS, H), dtype=jnp.float32) * scale, 'w3_s': jax.random.normal(ks[6], (FS, H), dtype=jnp.float32) * scale, 'w2_s': jax.random.normal(ks[7], (H, FS), dtype=jnp.float32) * scale}
    _L0_ffn_all = _L0_ffn_setup()
    _L0_ffn_in = {k: v for k, v in _L0_ffn_all.items() if k in ('w_gate', 'w1_e', 'w3_e', 'w2_e', 'w1_s', 'w3_s', 'w2_s')}
    del _L0_ffn_all
    return {'x': x, 'ctx_1024': ctx_1024, 'mask_BxSxS2_bk0': mask_BxSxS2_bk0, 'L0_xattn_Wq': _L0_xattn_in['Wq'], 'L0_xattn_Wkv': _L0_xattn_in['Wkv'], 'L0_xattn_Wo': _L0_xattn_in['Wo'], 'L0_xattn_nbias': _L0_xattn_in['nbias'], 'L0_ffn_w_gate': _L0_ffn_in['w_gate'], 'L0_ffn_w1_e': _L0_ffn_in['w1_e'], 'L0_ffn_w3_e': _L0_ffn_in['w3_e'], 'L0_ffn_w2_e': _L0_ffn_in['w2_e'], 'L0_ffn_w1_s': _L0_ffn_in['w1_s'], 'L0_ffn_w3_s': _L0_ffn_in['w3_s'], 'L0_ffn_w2_s': _L0_ffn_in['w2_s']}

def reference(x, ctx_1024, mask_BxSxS2_bk0, L0_xattn_Wq, L0_xattn_Wkv, L0_xattn_Wo, L0_xattn_nbias, L0_ffn_w_gate, L0_ffn_w1_e, L0_ffn_w3_e, L0_ffn_w2_e, L0_ffn_w1_s, L0_ffn_w3_s, L0_ffn_w2_s):
    import jax
    import jax.numpy as jnp

    def _L0_xattn_ref(iQ, iK, mask, Wq, Wkv, Wo, nbias):
        import jax, jax.numpy as jnp
        import numpy as np
        from math import sqrt
        B, Q, S, D, H = (2, 1024, 1024, 512, 16)
        ADIM = D // H
        IEPS = 1e-32

        def sparse_norm(scores, nbias):
            t = jax.nn.relu(scores + nbias[0])
            t = t * t
            return t / (t.sum(-1, keepdims=True) + IEPS)
        b, q, _ = iQ.shape
        s = iK.shape[1]
        rq = (iQ @ Wq.T).reshape(b, q, H, ADIM)
        kv = (iK @ Wkv.T).reshape(b, s, 2, H, ADIM)
        rk, rv = (kv[:, :, 0], kv[:, :, 1])
        scores = jnp.einsum('bqhd,bshd->bhqs', rq, rk) / sqrt(ADIM)
        scores = jnp.where(mask[:, None, :, :], jnp.float32(-1e+32), scores)
        attn = sparse_norm(scores, nbias)
        o = jnp.einsum('bhqs,bshd->bqhd', attn, rv).reshape(b, q, H * ADIM)
        return o @ Wo.T

    def _L0_ffn_ref(hidden_states, w_gate, w1_e, w3_e, w2_e, w1_s, w3_s, w2_s):
        import jax, jax.numpy as jnp
        import numpy as np
        B, S, H = (2, 512, 512)
        E, F = (16, 256)
        G, TOPK_G, TOPK = (4, 2, 4)
        N_SHARED = 2
        ROUTE_SCALE = 1.0
        FS = N_SHARED * F

        def _gate(x, w_gate):
            T = x.shape[0]
            scores = jax.nn.sigmoid(x @ w_gate.T)
            sv = scores.reshape(T, G, E // G)
            group_scores = jax.lax.top_k(sv, 2)[0].sum(-1)
            top_groups = jax.lax.top_k(group_scores, TOPK_G)[1]
            allowed = jnp.zeros((T, G), dtype=bool).at[jnp.arange(T)[:, None], top_groups].set(True)
            masked = jnp.where(allowed[:, :, None], sv, -jnp.inf).reshape(T, E)
            _, idx = jax.lax.top_k(masked, TOPK)
            w = jnp.take_along_axis(scores, idx, axis=1)
            w = w / (w.sum(-1, keepdims=True) + 1e-06) * ROUTE_SCALE
            return (w, idx)

        def _swiglu(x, w1, w3, w2):
            return jax.nn.silu(x @ w1.T) * (x @ w3.T) @ w2.T
        shape = hidden_states.shape
        x = hidden_states.reshape(-1, H)
        weights, idx = _gate(x, w_gate)
        combine = (jax.nn.one_hot(idx, E, dtype=x.dtype) * weights[..., None]).sum(1)
        g = jax.nn.silu(jnp.einsum('th,efh->tef', x, w1_e))
        u = jnp.einsum('th,efh->tef', x, w3_e)
        routed = jnp.einsum('tef,ehf,te->th', g * u, w2_e, combine)
        shared = _swiglu(x, w1_s, w3_s, w2_s)
        return (routed + shared).reshape(shape)
    x = x + _L0_xattn_ref(_layernorm(x, axis=-1), ctx_1024, mask_BxSxS2_bk0, L0_xattn_Wq, L0_xattn_Wkv, L0_xattn_Wo, L0_xattn_nbias)
    x = x + _L0_ffn_ref(_layernorm(x, axis=-1), L0_ffn_w_gate, L0_ffn_w1_e, L0_ffn_w3_e, L0_ffn_w2_e, L0_ffn_w1_s, L0_ffn_w3_s, L0_ffn_w2_s)
    return x

_drawn_inputs = setup_inputs


def setup_inputs(seed=0):
    import zlib

    import numpy as np

    out = dict(_drawn_inputs(seed))
    spreads = {}
    factors = {'L0_ffn_w_gate': 3.747, 'L0_ffn_w1_e': 3.332, 'L0_ffn_w3_e': 3.269, 'L0_ffn_w2_e': 3.267}
    for name, (base, spread) in spreads.items():
        noise = np.random.default_rng([zlib.crc32(name.encode()), seed]).standard_normal(out[name].shape)
        drawn = base * np.exp(spread * noise) if base else spread * noise
        out[name] = jnp.asarray(drawn.astype(out[name].dtype))
    for name, factor in factors.items():
        out[name] = (out[name] * factor).astype(out[name].dtype)
    return out
```

```python
from contextlib import ExitStack

import numpy as np

import concourse.bass as bass
from concourse import mybir

ALU = mybir.AluOpType
ACT = mybir.ActivationFunctionType
F32 = mybir.dt.float32
I32 = mybir.dt.int32
U32 = mybir.dt.uint32
U8 = mybir.dt.uint8
AX_X = mybir.AxisListType.X

P = 128
HEADS = 16
HEAD_DIM = 32
LN_EPS = 1e-5
NORM_EPS = 1e-32
ROUTE_EPS = 1e-6
GROUPS = 4
GROUP_SIZE = 4
TOP_K = 4
WEIGHT_SLOTS = 4
XN2_LOADS = 4
FAR = 1.0e6


def at_least(engine, semaphore, value):
    if not isinstance(value, int) or value > 0:
        engine.wait_ge(semaphore, value)


def stage_attend(nc, T, keep):
    B, S, D = T["x"].shape
    C = D // P
    ST = S // P
    assert (D, S, HEADS * HEAD_DIM) == (512, 256, 512) and B >= 4
    scale = float(HEAD_DIM) ** -0.5

    with ExitStack() as ctx:
        def sb(name, shape, dt=F32):
            return ctx.enter_context(nc.sbuf_tensor(name, shape, dt))

        def sem(name):
            return ctx.enter_context(nc.semaphore(name))

        wq, wk, wv, wo = (sb(n, [P, C, D]) for n in ("wq", "wk", "wv", "wo"))
        ws1, ws3, ws2 = (sb(n, [P, C, D]) for n in ("ws1", "ws3", "ws2"))
        wg = sb("wg", [P, C, 16])
        ident = sb("ident", [P, P])
        ones = sb("ones", [P, HEAD_DIM])
        minus_half = sb("minus_half", [P, ST])
        nbias = sb("nbias_all", [P, 1])
        x_in = sb("x_in", [P, ST, D])
        x_res = sb("x_res", [P, ST, D])
        ctx_t = sb("ctx_t", [P, C, S])
        mask = sb("mask_t", [P, B, ST, S], U8)
        bound = sb("bound", [P, ST, S])
        stats = sb("stats", [P, 2, ST, 6])
        mean_var = sb("mean_var", [P, 2, ST, 2])
        var_eps = sb("var_eps", [P, 2, ST])
        rstd = sb("rstd", [P, 2, ST])
        spacer = sb("spacer", [P, 2])
        eps = sb("eps", [P, ST])
        xn = sb("xn", [P, ST, D])
        xn_t = sb("xn_t", [P, C, S])
        q_diag = sb("q_diag", [P, C, 4, S])
        k_t = sb("k_t", [P, C, S])
        v_nat = sb("v_nat", [P, ST, D])
        probs = sb("probs", [P, 2, ST, 4, S])
        den = sb("den", [P, S])
        rec = sb("rec", [P, S])
        o_t = sb("o_t", [P, C, S])
        x1 = sb("x1", [P, ST, D])
        xn2 = sb("xn2", [P, ST, D])
        xn2_t = sb("xn2_t", [P, C, S])
        silu_g = sb("silu_g", [P, 2, 2 * S])
        h_t = sb("h_t", [P, C, S])
        base = sb("base_sb", [P, ST, D])

        psum = ctx.enter_context(nc.psum_tensor("attend_banks", [P, 3, 512], F32))
        sc = ctx.enter_context(nc.psum_tensor("attend_scores", [P, ST, 4 * S], F32))
        av = ctx.enter_context(nc.psum_tensor("attend_av", [P, 2, S], F32))

        consts_loaded = sem("consts_loaded")
        x_loaded, ctx_loaded, mask_loaded, res_loaded = (
            sem(n) for n in ("x_loaded", "ctx_loaded", "mask_loaded", "res_loaded"))
        xn2_kept, base_stored = sem("xn2_kept"), sem("base_stored")
        zeroed, ident_ready, q_zeroed, consts_made = (
            sem(n) for n in ("zeroed", "ident_ready", "q_zeroed", "consts_made"))
        front_ready, back_ready, scores_ready, av_ready = (
            sem(n) for n in ("front_ready", "back_ready", "scores_ready", "av_ready"))
        xnt_ready, q_ready, k_ready, v_ready, xn2t_ready, gate_ready, silu_ready = (
            sem(n) for n in ("xnt_ready", "q_ready", "k_ready", "v_ready", "xn2t_ready", "gate_ready", "silu_ready"))
        stats1, var1, xn_ready, stats2, var2, xn2_ready, x1_ready, bound_ready = (
            sem(n) for n in ("stats1", "var1", "xn_ready", "stats2", "var2", "xn2_ready", "x1_ready", "bound_ready"))
        clipped, probs_ready, den_ready, rec_ready, ot_ready, h_ready, base_ready = (
            sem(n) for n in ("clipped", "probs_ready", "den_ready", "rec_ready", "ot_ready", "h_ready", "base_ready"))
        eps1, rstd1, eps2, rstd2 = (sem(n) for n in ("eps1", "rstd1", "eps2", "rstd2"))

        tokens = T["x"].rearrange("b (t p) d -> b p t d", p=P)
        base_dram = T["base"].rearrange("b (t p) d -> b p t d", p=P)
        xn2_dram = T["xn2"].rearrange("b (t p) d -> b p t d", p=P)

        block = ctx.enter_context(nc.Block())

        @block.sync
        def _(sp):
            def pick(ap, i):
                if isinstance(i, int):
                    return ap[i]
                return ap[bass.ds(i, 1)]

            def load(dst, ap, i, free, count, loaded):
                src = pick(ap, i)
                if not isinstance(i, int):
                    src = src.rearrange({3: "a p s -> (a p) s", 4: "a p t s -> (a p) t s"}[len(ap.shape)])
                at_least(sp, free, count)
                sp.dma_start(dst, src).then_inc(loaded, 16)

            consts = [(wk, "wk"), (wv, "wv"), (wq, "wq"), (wo, "wo"), (ws1, "ws1"), (ws3, "ws3"), (wg, "wg"), (ws2, "ws2")]
            load(x_in[:], tokens, 0, xn_ready, 0, x_loaded)
            load(ctx_t[:], T["ctx_t"], 0, front_ready, 0, ctx_loaded)
            for dst, name in consts:
                sp.dma_start(dst[:], T[name]).then_inc(consts_loaded, 16)
            sp.dma_start(nbias[:], T["nbias"].rearrange("(a b) -> a b", a=1).to_broadcast([P, 1])).then_inc(consts_loaded, 16)
            sp.dma_start(mask[:], T["mask_t"].rearrange("b p t s -> p b t s")).then_inc(mask_loaded, 16)
            load(x_res[:], tokens, 0, x1_ready, 0, res_loaded)

            def next_loads(i):
                load(x_in[:], tokens, i + 1, xn_ready, ST * (i + 1), x_loaded)
                load(ctx_t[:], T["ctx_t"], i + 1, front_ready, 8 * (i + 1), ctx_loaded)

            def keep_xn2(j):
                dst = pick(xn2_dram, j)
                if not isinstance(j, int):
                    dst = dst.rearrange("a p t d -> (a p) t d")
                at_least(sp, xn2_ready, ST * (j + 1))
                sp.dma_start(dst, xn2[:]).then_inc(xn2_kept, 16)

            def store_base(j):
                dst = pick(base_dram, j)
                if not isinstance(j, int):
                    dst = dst.rearrange("a p t d -> (a p) t d")
                at_least(sp, base_ready, ST * (j + 1))
                sp.dma_start(dst, base[:]).then_inc(base_stored, 16)

            def body(i, more=True):
                if more:
                    next_loads(i)
                load(x_res[:], tokens, i, x1_ready, ST * i, res_loaded)
                keep_xn2(i - 1)
                store_base(i - 1)

            next_loads(0)
            body(1)
            with sp.Fori(2, B - 1) as i:
                body(i)
            body(B - 1, more=False)
            keep_xn2(B - 1)
            store_base(B - 1)
            sp.wait_ge(xn2_kept, 16 * B)
            sp.wait_ge(base_stored, 16 * B)

        @block.gpsimd
        def _(pool):
            nc.gpsimd.memset(ident[:], 0.0).then_inc(zeroed, 1)
            nc.gpsimd.memset(minus_half[:], -0.5).then_inc(consts_made, 1)
            nc.gpsimd.memset(ones[:], 1.0).then_inc(consts_made, 1)
            nc.gpsimd.memset(eps[:], LN_EPS).then_inc(consts_made, 1)
            pool.wait_ge(zeroed, 1)
            nc.gpsimd.affine_select(out=ident[:], in_=ident[:], compare_op=ALU.not_equal, fill=1.0, base=0,
                                    pattern=[[-1, P]], channel_multiplier=1).then_inc(ident_ready, 1)
            nc.gpsimd.memset(q_diag[:], 0.0).then_inc(q_zeroed, 1)
            pool.wait_ge(consts_made, 3)

            def inverse_std(which, i, var, eps_ready, done):
                at_least(pool, var, ST * (i + 1))
                nc.gpsimd.tensor_tensor(var_eps[:, which, :], mean_var[:, which, :, 1], eps[:],
                                        ALU.add).then_inc(eps_ready, 1)
                at_least(pool, eps_ready, i + 1)
                nc.gpsimd.tensor_tensor(rstd[:, which, :], var_eps[:, which, :], minus_half[:], ALU.pow).then_inc(done, 1)

            def body(i, more=True):
                inverse_std(1, i - 1, var2, eps2, rstd2)
                if more:
                    inverse_std(0, i + 1, var1, eps1, rstd1)

            inverse_std(0, 0, var1, eps1, rstd1)
            inverse_std(0, 1, var1, eps1, rstd1)
            body(1)
            with pool.Fori(2, B - 1) as i:
                body(i)
            body(B - 1, more=False)
            inverse_std(1, B - 1, var2, eps2, rstd2)

        @block.tensor
        def _(pe):
            def transposes(i, t):
                at_least(pe, xn_ready, ST * i + t + 1)
                if t == 0:
                    at_least(pe, silu_ready, 2 * (i - 1))
                    at_least(pe, v_ready, ST * i)
                else:
                    at_least(pe, base_ready, ST * (i - 1))
                    at_least(pe, k_ready, 2 * i)
                for c in range(C):
                    last = nc.tensor.transpose(psum[:, t, c * P:(c + 1) * P], xn[:, t, c * P:(c + 1) * P], ident[:])
                last.then_inc(front_ready, 1)

            def q_unit(i, u):
                at_least(pe, xnt_ready, ST * (i + 1))
                if u == 1:
                    at_least(pe, x1_ready, ST * (i - 1) + 1)
                    at_least(pe, v_ready, ST * (i - 1) + 1)
                for cc in range(2):
                    for c in range(C):
                        last = nc.tensor.matmul(psum[:, 1 + u, cc * S:(cc + 1) * S],
                                                wq[:, c, (2 * u + cc) * P:(2 * u + cc + 1) * P], xn_t[:, c, :],
                                                start=(c == 0), stop=(c == C - 1))
                last.then_inc(front_ready, 1)

            def k_unit(i, u):
                at_least(pe, ctx_loaded, 16 * (i + 1))
                if u == 0:
                    at_least(pe, x1_ready, ST * i)
                    at_least(pe, xnt_ready, ST * i + 1)
                else:
                    at_least(pe, q_ready, 2 * i + 1)
                for cc in range(2):
                    for c in range(C):
                        last = nc.tensor.matmul(psum[:, u, cc * S:(cc + 1) * S],
                                                wk[:, c, (2 * u + cc) * P:(2 * u + cc + 1) * P], ctx_t[:, c, :],
                                                start=(c == 0), stop=(c == C - 1))
                last.then_inc(front_ready, 1)

            def v_unit(i, t):
                if t == 0:
                    at_least(pe, q_ready, 2 * i + 2)
                else:
                    at_least(pe, k_ready, 2 * i + 1)
                for c in range(C):
                    last = nc.tensor.matmul(psum[:, 2 - 2 * t, :], ctx_t[:, c, t * P:(t + 1) * P], wv[:, c, :],
                                            start=(c == 0), stop=(c == C - 1))
                last.then_inc(front_ready, 1)

            def scores(i, c):
                at_least(pe, q_ready, 2 * i + c // 2 + 1)
                at_least(pe, k_ready, 2 * i + c // 2 + 1)
                for st in range(ST):
                    at_least(pe, clipped, 8 * i + 2 * (c - 1) + st + 1)
                    for half in range(2):
                        last = nc.tensor.matmul(sc[:, st, half * 512:(half + 1) * 512], k_t[:, c, st * P:(st + 1) * P],
                                                q_diag[:, c, 2 * half:2 * half + 2, :], start=True, stop=True)
                    last.then_inc(scores_ready, 1)

            def attend(i, c):
                at_least(pe, probs_ready, 8 * i + 2 * c + 2)
                at_least(pe, v_ready, ST * (i + 1))
                at_least(pe, ot_ready, 4 * i + c)
                for what in range(2):
                    for st in range(ST):
                        for j in range(4):
                            h = 4 * c + j
                            left = ones[:] if what else v_nat[:, st, h * HEAD_DIM:(h + 1) * HEAD_DIM]
                            last = nc.tensor.matmul(av[32 * j:32 * j + 32, what, :], left, probs[:, c % 2, st, j, :],
                                                    start=(st == 0), stop=(st == ST - 1), tile_position=(0, 32 * j),
                                                    skip_group_check=True)
                last.then_inc(av_ready, 1)

            def o_unit(j, t):
                at_least(pe, ot_ready, 4 * (j + 1))
                if t == 0:
                    at_least(pe, base_ready, ST * (j - 1) + 1)
                    at_least(pe, v_ready, ST * j + 1)
                else:
                    if not (isinstance(j, int) and j == B - 1):
                        at_least(pe, xnt_ready, ST * (j + 1) + 1)
                    at_least(pe, silu_ready, 2 * j)
                    at_least(pe, v_ready, ST * (j + 1))
                for c in range(C):
                    last = nc.tensor.matmul(psum[:, 2 - 2 * t, :], o_t[:, c, t * P:(t + 1) * P], wo[:, c, :],
                                            start=(c == 0), stop=(c == C - 1))
                last.then_inc(back_ready, 1)

            def xn2t_unit(j, t, i):
                at_least(pe, xn2_ready, ST * j + t + 1)
                if t == 0:
                    at_least(pe, k_ready, 2 * i)
                else:
                    at_least(pe, v_ready, ST * (i - 1) + 1)
                    at_least(pe, x1_ready, ST * j + 1)
                for c in range(C):
                    last = nc.tensor.transpose(psum[:, 1 + t, c * P:(c + 1) * P], xn2[:, t, c * P:(c + 1) * P], ident[:])
                last.then_inc(back_ready, 1)

            def gate_unit(j, i):
                at_least(pe, xn2t_ready, ST * (j + 1))
                at_least(pe, v_ready, ST * i)
                at_least(pe, x1_ready, ST * (j + 1))
                for t in range(ST):
                    for c in range(C):
                        last = nc.tensor.matmul(psum[:, 0, 16 * t:16 * t + 16], xn2_t[:, c, t * P:(t + 1) * P], wg[:, c, :],
                                                start=(c == 0), stop=(c == C - 1))
                last.then_inc(back_ready, 1)

            def shared_up(j, u):
                for which, (w, bank) in enumerate(((ws1, (1, 0)[u]), (ws3, (2, 1)[u]))):
                    if u == 0:
                        at_least(pe, xn2t_ready, ST * (j + 1))
                    elif which == 0:
                        at_least(pe, gate_ready, j + 1)
                    else:
                        at_least(pe, silu_ready, 2 * j + 1)
                    for cc in range(2):
                        for c in range(C):
                            last = nc.tensor.matmul(psum[:, bank, cc * S:(cc + 1) * S],
                                                    w[:, c, (2 * u + cc) * P:(2 * u + cc + 1) * P], xn2_t[:, c, :],
                                                    start=(c == 0), stop=(c == C - 1))
                    last.then_inc(back_ready, 1)

            def shared_down(j, t):
                at_least(pe, h_ready, 2 * (j + 1))
                for c in range(C):
                    last = nc.tensor.matmul(psum[:, 2 - t, :], h_t[:, c, t * P:(t + 1) * P], ws2[:, c, :],
                                            start=(c == 0), stop=(c == C - 1))
                last.then_inc(back_ready, 1)

            def body(i):
                j = i - 1
                for t in range(ST):
                    transposes(i, t)
                for t in range(ST):
                    o_unit(j, t)
                for u in range(2):
                    q_unit(i, u)
                for u in range(2):
                    k_unit(i, u)
                for t in range(ST):
                    v_unit(i, t)
                scores(i, 0)
                for t in range(ST):
                    xn2t_unit(j, t, i + 1)
                scores(i, 1)
                gate_unit(j, i + 1)
                shared_up(j, 0)
                attend(i, 0)
                scores(i, 2)
                shared_up(j, 1)
                attend(i, 1)
                scores(i, 3)
                for t in range(ST):
                    shared_down(j, t)
                attend(i, 2)
                attend(i, 3)

            pe.wait_ge(consts_loaded, 16 * 9)
            pe.wait_ge(ident_ready, 1)
            pe.wait_ge(consts_made, 3)
            pe.wait_ge(q_zeroed, 1)
            for t in range(ST):
                transposes(0, t)
            for u in range(2):
                q_unit(0, u)
            for u in range(2):
                k_unit(0, u)
            for t in range(ST):
                v_unit(0, t)
            for c in range(C):
                scores(0, c)
                attend(0, c)
            body(1)
            with pe.Fori(2, B - 1) as i:
                body(i)
            body(B - 1)
            j = B - 1
            for t in range(ST):
                o_unit(j, t)
            for t in range(ST):
                xn2t_unit(j, t, B)
            gate_unit(j, B)
            for u in range(2):
                shared_up(j, u)
            for t in range(ST):
                shared_down(j, t)

        @block.scalar
        def _(act):
            copy = nc.scalar.copy

            def front(i):
                for t in range(ST):
                    at_least(act, front_ready, 8 * i + t + 1)
                    copy(xn_t[:, :, t * P:(t + 1) * P], psum[:, t, :].rearrange("p (c s) -> p c s", c=C)).then_inc(xnt_ready, 1)
                act.wait_ge(q_zeroed, 1)
                for u in range(2):
                    at_least(act, front_ready, 8 * i + 3 + u)
                    for h in range(4):
                        part = slice(32 * h, 32 * h + 32)
                        last = nc.scalar.mul(q_diag[part, 2 * u:2 * u + 2, h, :],
                                             psum[part, 1 + u, :].rearrange("p (c s) -> p c s", c=2), scale)
                    last.then_inc(q_ready, 1)
                for u in range(2):
                    at_least(act, front_ready, 8 * i + 5 + u)
                    copy(k_t[:, 2 * u:2 * u + 2, :], psum[:, u, :].rearrange("p (c s) -> p c s", c=2)).then_inc(k_ready, 1)
                for t in range(ST):
                    at_least(act, front_ready, 8 * i + 7 + t)
                    copy(v_nat[:, t, :], psum[:, 2 - 2 * t, :]).then_inc(v_ready, 1)

            def back(j):
                for t in range(ST):
                    at_least(act, back_ready, 11 * j + 3 + t)
                    copy(xn2_t[:, :, t * P:(t + 1) * P], psum[:, 1 + t, :].rearrange("p (c s) -> p c s", c=C)).then_inc(xn2t_ready, 1)
                at_least(act, back_ready, 11 * j + 5)
                copy(keep["logits"][:, bass.ds(j * ST, ST), :],
                     psum[:, 0, 0:16 * ST].rearrange("p (t e) -> p t e", t=ST)).then_inc(gate_ready, 1)
                for u in range(2):
                    at_least(act, back_ready, 11 * j + 6 + 2 * u)
                    at_least(act, h_ready, 2 * (j - 1) + u + 1)
                    nc.scalar.activation(silu_g[:, u, :], psum[:, (1, 0)[u], :], ACT.Silu).then_inc(silu_ready, 1)

            def body(i):
                front(i)
                back(i - 1)

            front(0)
            body(1)
            with act.Fori(2, B - 1) as i:
                body(i)
            body(B - 1)
            back(B - 1)

        @block.vector
        def _(dve):
            def moments(src, which, i, stats_done, var_done):
                for t in range(ST):
                    nc.vector.bn_stats(stats[:, which, t, :], src[:, t, :]).then_inc(stats_done, 1)
                at_least(dve, stats_done, ST * (i + 1))
                nc.vector.memset(spacer[:, which:which + 1], 0.0)
                for t in range(ST):
                    nc.vector.bn_aggr(mean_var[:, which, t, :], stats[:, which, t, :]).then_inc(var_done, 1)

            def normalise(dst, src, which, i, rstd_done, done):
                at_least(dve, rstd_done, i + 1)
                for t in range(ST):
                    nc.vector.tensor_scalar(dst[:, t, :], src[:, t, :], mean_var[:, which, t, 0:1], rstd[:, which, t:t + 1],
                                            ALU.subtract, ALU.mult).then_inc(done, 1)

            def moments1(i):
                at_least(dve, rstd1, i)
                at_least(dve, x_loaded, 16 * (i + 1))
                moments(x_in, 0, i, stats1, var1)

            def normalise1(i):
                at_least(dve, front_ready, 8 * (i - 1) + 2)
                normalise(xn, x_in, 0, i, rstd1, xn_ready)

            def residual(j):
                at_least(dve, res_loaded, 16 * (j + 1))
                for t in range(ST):
                    at_least(dve, back_ready, 11 * j + 1 + t)
                    nc.vector.tensor_tensor(x1[:, t, :], psum[:, 2 - 2 * t, :], x_res[:, t, :], ALU.add).then_inc(x1_ready, 1)
                at_least(dve, x1_ready, ST * (j + 1))
                moments(x1, 1, j, stats2, var2)

            def normalise2(j):
                at_least(dve, xn2_kept, 16 * j)
                normalise(xn2, x1, 1, j, rstd2, xn2_ready)

            def make_bound(i):
                big = float(np.finfo(np.float32).max)
                for t in range(ST):
                    part = mask[:, i, t, :] if isinstance(i, int) else mask[:, bass.ds(i, 1), t, :].rearrange("p a s -> p (a s)")
                    nc.vector.tensor_scalar(bound[:, t, :], part, -big, big, ALU.mult, ALU.add).then_inc(bound_ready, 1)

            def probabilities(i, c):
                at_least(dve, bound_ready, ST * (i + 1))
                at_least(dve, av_ready, 4 * i + c - 1)
                for st in range(ST):
                    at_least(dve, scores_ready, 8 * i + 2 * c + st + 1)
                    nc.vector.scalar_tensor_tensor(
                        out=probs[:, c % 2, st, :, :], in0=sc[:, st, :].rearrange("p (h s) -> p h s", h=4),
                        scalar=nbias[:, 0:1], in1=bound[:, st:st + 1, :].to_broadcast([P, 4, S]),
                        op0=ALU.add, op1=ALU.min).then_inc(clipped, 1)
                for st in range(ST):
                    at_least(dve, clipped, 8 * i + 2 * c + st + 1)
                    x = probs[:, c % 2, st, :, :].rearrange("p h s -> p (h s)")
                    nc.vector.scalar_tensor_tensor(out=x, in0=x, scalar=0.0, in1=x, op0=ALU.max,
                                                   op1=ALU.mult).then_inc(probs_ready, 1)

            def divide(i, c):
                at_least(dve, av_ready, 4 * i + c + 1)
                nc.vector.tensor_scalar(den[:], av[:, 1, :], NORM_EPS, None, ALU.add).then_inc(den_ready, 1)
                at_least(dve, den_ready, 4 * i + c + 1)
                nc.vector.reciprocal(rec[:], den[:]).then_inc(rec_ready, 1)
                at_least(dve, rec_ready, 4 * i + c + 1)
                nc.vector.tensor_tensor(o_t[:, c, :], av[:, 0, :], rec[:], ALU.mult).then_inc(ot_ready, 1)

            def hidden(j, u):
                at_least(dve, silu_ready, 2 * j + u + 1)
                at_least(dve, back_ready, 11 * j + 7 + 2 * u)
                nc.vector.tensor_tensor(h_t[:, 2 * u:2 * u + 2, :].rearrange("p c s -> p (c s)"), psum[:, 2 - u, :],
                                        silu_g[:, u, :], ALU.mult).then_inc(h_ready, 1)

            def sum_base(j):
                at_least(dve, base_stored, 16 * j)
                for t in range(ST):
                    at_least(dve, back_ready, 11 * j + 10 + t)
                    nc.vector.tensor_tensor(base[:, t, :], psum[:, 2 - t, :], x1[:, t, :], ALU.add).then_inc(base_ready, 1)

            def body(i, more=True):
                j = i - 1
                residual(j)
                make_bound(i)
                normalise2(j)
                probabilities(i, 0)
                probabilities(i, 1)
                hidden(j, 0)
                divide(i, 0)
                if more:
                    moments1(i + 1)
                probabilities(i, 2)
                hidden(j, 1)
                divide(i, 1)
                if more:
                    normalise1(i + 1)
                probabilities(i, 3)
                sum_base(j)
                divide(i, 2)
                divide(i, 3)

            dve.wait_ge(consts_loaded, 16 * 9)
            moments1(0)
            normalise1(0)
            moments1(1)
            normalise1(1)
            dve.wait_ge(mask_loaded, 16)
            make_bound(0)
            for c in range(C):
                probabilities(0, c)
                divide(0, c)
            body(1)
            with dve.Fori(2, B - 1) as i:
                body(i)
            body(B - 1, more=False)
            j = B - 1
            residual(j)
            normalise2(j)
            for u in range(2):
                hidden(j, u)
            sum_base(j)


def stage_route(nc, T, keep, plan):
    NT, BLOCKS, E = keep["tiles"], keep["blocks"], HEADS
    sorted_rows = T["sorted_x"]
    with ExitStack() as ctx:
        def sb(name, shape, dt=F32):
            return ctx.enter_context(nc.sbuf_tensor(name, shape, dt))

        def sem(name):
            return ctx.enter_context(nc.semaphore(name))

        xn2 = sb("xn2_all", [P, NT, 512])
        scores = sb("gate_scores", [P, NT, E])
        low = sb("pair_low", [P, 2, NT * GROUPS])
        high = sb("pair_high", [P, 2, NT * GROUPS])
        second = sb("second", [P, 2, NT * GROUPS])
        group = sb("group_score", [P, NT, GROUPS])
        group_beats = sb("group_beats", [P, NT, GROUPS, GROUPS])
        group_rank = sb("group_rank", [P, NT, GROUPS])
        allowed = sb("allowed", [P, NT, GROUPS])
        shut = sb("shut", [P, NT, GROUPS])
        open_scores = sb("open_scores", [P, NT, E])
        beats = sb("beats", [P, NT, E, E])
        rank = sb("expert_rank", [P, NT, E])
        chosen = sb("chosen", [P, NT, E])
        weight = sb("weight", [P, NT, E])
        weight_sum = sb("weight_sum", [P, NT])
        earlier = sb("earlier", [P, P])
        all_ones = sb("all_ones", [P, P])
        tile_counts = sb("tile_counts", [P, E, NT])
        same_expert = sb("same_expert", [P, E, NT])
        running = sb("running", [P, E, NT])
        count = sb("count", [P, E])
        count_i = sb("count_i", [P, E], I32)
        n_blocks = sb("n_blocks", [P, E])
        ends = sb("block_ends", [P, E])
        first_row = sb("first_row", [P, E])
        place = sb("place", [P, NT, E])
        picked = sb("picked", [P, NT, E])
        chosen_place = sb("chosen_place", [P, NT, E])
        place_k = sb("place_k", [P, TOP_K, NT])
        lane = sb("lane", [P, E])
        pad_place = sb("pad_place", [P, E])
        pad_over = sb("pad_over", [P, E])
        pad_index = sb("pad_index", [P, E], U32)
        zeros = sb("zero_rows", [P, 512])
        step_no = sb("block_no", [1, BLOCKS])
        passed = sb("passed", [1, BLOCKS, E])
        nonempty = sb("nonempty", [1, E])
        table_f = sb("table_f", [1, 4, BLOCKS])
        run_i = sb("run_i", [1, BLOCKS], I32)
        counts_ps = ctx.enter_context(nc.psum_tensor("counts_ps", [P, 2, NT * E], F32))

        scores_ready, step, made, counted, pads_ready, places_ready = (
            sem(n) for n in ("sigmoid_ready", "dve_step", "route_consts", "counted", "pads_ready", "places_ready"))
        xn2_loaded = sem("xn2_loaded")
        chosen_ready, constants_zeroed, pads_scattered, scattered = (
            sem(n) for n in ("chosen_ready", "constants_zeroed", "pads_scattered", "scattered"))
        block = ctx.enter_context(nc.Block())

        @block.sync
        def _(sp):
            source = T["xn2"].rearrange("b (t p) d -> p (b t) d", p=P)
            for part in range(XN2_LOADS):
                tiles = slice(part * NT // XN2_LOADS, (part + 1) * NT // XN2_LOADS)
                sp.dma_start(xn2[:, tiles, :], source[:, tiles, :]).then_inc(xn2_loaded, 16)

        @block.scalar
        def _(act):
            nc.scalar.activation(scores[:], keep["logits"][:], ACT.Sigmoid).then_inc(scores_ready, 1)

        @block.gpsimd
        def _(pool):
            nc.gpsimd.memset(all_ones[:], 1.0).then_inc(made, 1)
            nc.gpsimd.memset(earlier[:], 1.0).then_inc(constants_zeroed, 1)
            nc.gpsimd.memset(zeros[:], 0.0).then_inc(made, 1)
            nc.gpsimd.iota(lane[:], pattern=[[0, E]], base=0, channel_multiplier=1,
                           allow_small_or_imprecise_dtypes=True).then_inc(made, 1)
            nc.gpsimd.iota(step_no[:], pattern=[[1, BLOCKS]], base=0, channel_multiplier=0,
                           allow_small_or_imprecise_dtypes=True).then_inc(made, 1)
            pool.wait_ge(constants_zeroed, 1)
            nc.gpsimd.affine_select(out=earlier[:], in_=earlier[:], compare_op=ALU.is_gt, fill=0.0, base=0,
                                    pattern=[[1, P]], channel_multiplier=-1).then_inc(made, 1)
            pool.wait_ge(made, 5)
            pool.wait_ge(pads_ready, 1)
            for e in range(E):
                pool.indirect_dma_start(sorted_rows, bass.IndirectOffsetOnAxis(ap=pad_index[:, e:e + 1], axis=0),
                                        zeros[:], None, bounds_check=BLOCKS * P - 1,
                                        oob_is_err=False).then_inc(pads_scattered, 16)
            pool.wait_ge(places_ready, 1)
            pool.wait_ge(xn2_loaded, 16 * XN2_LOADS)
            for t in range(NT):
                for k in range(TOP_K):
                    pool.indirect_dma_start(sorted_rows, bass.IndirectOffsetOnAxis(ap=plan["place"][:, k, t:t + 1], axis=0),
                                            xn2[:, t, :], None, bounds_check=BLOCKS * P - 1,
                                            oob_is_err=False).then_inc(scattered, 16)
            pool.wait_ge(pads_scattered, 16 * E)
            pool.wait_ge(scattered, 16 * NT * TOP_K)

        @block.tensor
        def _(pe):
            pe.wait_ge(made, 5)
            pe.wait_ge(chosen_ready, 1)
            flat = chosen[:].rearrange("p t e -> p (t e)")
            nc.tensor.matmul(counts_ps[:, 0, :], earlier[:], flat, start=True, stop=True)
            nc.tensor.matmul(counts_ps[:, 1, :], all_ones[:], flat, start=True, stop=True).then_inc(counted, 1)

        @block.vector
        def _(dve):
            steps = [0]

            def link(instruction):
                steps[0] += 1
                instruction.then_inc(step, 1)
                dve.wait_ge(step, steps[0])

            v = nc.vector
            flat4 = "p t g -> p (t g)"
            dve.wait_ge(scores_ready, 1)
            by_group = scores[:].rearrange("p t (g k) -> p (t g) k", k=GROUP_SIZE)
            for pair in range(2):
                a, b = by_group[:, :, 2 * pair], by_group[:, :, 2 * pair + 1]
                v.tensor_tensor(high[:, pair, :], a, b, ALU.max)
                link(v.tensor_tensor(low[:, pair, :], a, b, ALU.min))
            v.tensor_tensor(second[:, 0, :], high[:, 0, :], high[:, 1, :], ALU.min)
            link(v.tensor_tensor(second[:, 1, :], low[:, 0, :], low[:, 1, :], ALU.max))
            link(v.tensor_tensor(low[:, 0, :], high[:, 0, :], high[:, 1, :], ALU.max))
            link(v.tensor_tensor(second[:, 0, :], second[:, 0, :], second[:, 1, :], ALU.max))
            link(v.tensor_tensor(group[:].rearrange(flat4), low[:, 0, :], second[:, 0, :], ALU.add))

            def ranks(values, out, work, n):
                for e in range(n):
                    if e:
                        v.tensor_tensor(work[:, :, e, 0:e], values[:, :, 0:e],
                                        values[:, :, e:e + 1].to_broadcast([P, NT, e]), ALU.is_ge)
                    last = v.memset(work[:, :, e, e:e + 1], 0.0)
                    if e < n - 1:
                        last = v.tensor_tensor(work[:, :, e, e + 1:n], values[:, :, e + 1:n],
                                               values[:, :, e:e + 1].to_broadcast([P, NT, n - 1 - e]), ALU.is_gt)
                link(last)
                link(v.tensor_reduce(out, work[:], AX_X, ALU.add))

            ranks(group[:], group_rank[:], group_beats, GROUPS)
            link(v.tensor_scalar(allowed[:], group_rank[:], 1.5, None, ALU.is_lt))
            link(v.tensor_scalar(shut[:], allowed[:], 1.0, None, ALU.subtract))
            per_expert = [P, NT * GROUPS, GROUP_SIZE]
            open_group = open_scores[:].rearrange("p t (g k) -> p (t g) k", k=GROUP_SIZE)
            link(v.tensor_tensor(open_group, by_group, allowed[:].rearrange("p t (g o) -> p (t g) o", o=1).to_broadcast(per_expert),
                                 ALU.mult))
            link(v.tensor_tensor(open_group, open_group, shut[:].rearrange("p t (g o) -> p (t g) o", o=1).to_broadcast(per_expert),
                                 ALU.add))
            ranks(open_scores[:], rank[:], beats, E)
            link(v.tensor_scalar(chosen[:], rank[:], TOP_K - 0.5, None, ALU.is_lt))
            v.tensor_scalar(picked[:], rank[:], TOP_K - 0.5, None, ALU.is_lt).then_inc(chosen_ready, 1)

            link(v.tensor_tensor(weight[:], scores[:], chosen[:], ALU.mult))
            link(v.tensor_reduce(weight_sum[:], weight[:], AX_X, ALU.add))
            link(v.tensor_scalar(weight_sum[:], weight_sum[:], ROUTE_EPS, None, ALU.add))
            link(v.reciprocal(weight_sum[:], weight_sum[:]))
            link(v.tensor_tensor(weight[:], weight[:], weight_sum[:].rearrange("p (t o) -> p t o", o=1).to_broadcast([P, NT, E]),
                                 ALU.mult))

            v.memset(same_expert[:, :, 1:NT], 1.0)
            link(v.memset(same_expert[:, :, 0:1], 0.0))
            dve.wait_ge(counted, 1)
            link(v.tensor_copy(tile_counts[:], counts_ps[:, 1, :].rearrange("p (t e) -> p e t", e=E)))
            flat_et = "p e t -> p (e t)"
            link(v.tensor_tensor_scan(running[:].rearrange(flat_et), same_expert[:].rearrange(flat_et),
                                      tile_counts[:].rearrange(flat_et), 0.0, ALU.mult, ALU.add))
            link(v.tensor_scalar(count[:], running[:, :, NT - 1], float(P - 1), None, ALU.add))
            link(v.tensor_tensor(running[:], running[:], tile_counts[:], ALU.subtract))
            link(v.tensor_copy(count_i[:], count[:]))
            link(v.tensor_scalar(count_i[:], count_i[:], 7, None, ALU.logical_shift_right))
            link(v.tensor_copy(n_blocks[:], count_i[:]))
            v.memset(pad_over[:], 1.0)
            link(v.tensor_scalar(count[:], count[:], float(P - 1), None, ALU.subtract))
            link(v.tensor_tensor_scan(ends[:], pad_over[:], n_blocks[:], 0.0, ALU.mult, ALU.add))
            link(v.tensor_tensor(first_row[:], ends[:], n_blocks[:], ALU.subtract))
            link(v.tensor_scalar(first_row[:], first_row[:], float(P), None, ALU.mult))

            dve.wait_ge(made, 5)
            link(v.tensor_tensor(pad_place[:], first_row[:], count[:], ALU.add))
            link(v.tensor_tensor(pad_place[:], pad_place[:], lane[:], ALU.add))
            link(v.scalar_tensor_tensor(out=pad_over[:], in0=ends[:], scalar=float(P), in1=pad_place[:],
                                        op0=ALU.mult, op1=ALU.is_le))
            link(v.scalar_tensor_tensor(out=pad_place[:], in0=pad_over[:], scalar=FAR, in1=pad_place[:],
                                        op0=ALU.mult, op1=ALU.add))
            v.tensor_copy(pad_index[:], pad_place[:]).then_inc(pads_ready, 1)

            link(v.tensor_tensor(place[:], counts_ps[:, 0, :].rearrange("p (t e) -> p t e", e=E),
                                 running[:].rearrange("p e t -> p t e"), ALU.add))
            link(v.tensor_tensor(place[:], place[:], first_row[:].rearrange("p (o e) -> p o e", o=1).to_broadcast([P, NT, E]),
                                 ALU.add))
            for k in range(TOP_K):
                link(v.tensor_scalar(picked[:], rank[:], float(k), None, ALU.is_equal))
                v.tensor_tensor(chosen_place[:], picked[:], place[:], ALU.mult)
                link(v.tensor_tensor(picked[:], picked[:], weight[:], ALU.mult))
                v.tensor_reduce(place_k[:, k, :], chosen_place[:], AX_X, ALU.add)
                link(v.tensor_reduce(plan["weight"][:, k, :], picked[:], AX_X, ALU.add))
            v.tensor_copy(plan["place"][:], place_k[:]).then_inc(places_ready, 1)

            link(v.tensor_tensor(passed[:], ends[0:1, :].rearrange("p (o e) -> p o e", o=1).to_broadcast([1, BLOCKS, E]),
                                 step_no[:].rearrange("p (b o) -> p b o", o=1).to_broadcast([1, BLOCKS, E]), ALU.is_le))
            v.tensor_scalar(nonempty[:], n_blocks[0:1, :], 0.5, None, ALU.is_gt)
            link(v.tensor_reduce(table_f[:, 0, :], passed[:], AX_X, ALU.add))
            link(v.tensor_tensor(passed[:], passed[:], nonempty[:].rearrange("p (o e) -> p o e", o=1).to_broadcast([1, BLOCKS, E]),
                                 ALU.mult))
            v.tensor_scalar(table_f[:, 0, :], table_f[:, 0, :], float(E - 1), None, ALU.min)
            link(v.tensor_reduce(table_f[:, 1, :], passed[:], AX_X, ALU.add))
            v.memset(table_f[:, 2, 0:1], 1.0)
            v.tensor_tensor(table_f[:, 2, 1:BLOCKS], table_f[:, 1, 1:BLOCKS], table_f[:, 1, 0:BLOCKS - 1], ALU.not_equal)
            v.tensor_scalar(nonempty[:, 0:1], ends[0:1, E - 1:E], 1.0, None, ALU.subtract)
            link(v.tensor_copy(run_i[:], table_f[:, 1, :]))
            link(v.tensor_scalar(table_f[:, 3, :], step_no[:], nonempty[:, 0:1], None, ALU.min))
            link(v.tensor_copy(plan["table"][:], table_f[:]))
            link(v.tensor_scalar(plan["table"][:, 1, :], run_i[:], WEIGHT_SLOTS - 1, None, ALU.bitwise_and))


def stage_experts(nc, T, keep, plan):
    BLOCKS = keep["blocks"]
    D, C, F = 512, 4, 256
    FC = F // P
    W = C * 2 * F + FC * D
    assert BLOCKS % 4 == 0 and WEIGHT_SLOTS == 4
    with ExitStack() as ctx:
        def sb(name, shape, dt=F32):
            return ctx.enter_context(nc.sbuf_tensor(name, shape, dt))

        def sem(name):
            return ctx.enter_context(nc.semaphore(name))

        weights = sb("expert_weights", [P, WEIGHT_SLOTS * W])
        ident = sb("ident2", [P, P])
        rows = sb("rows", [P, 2, D])
        rows_t = sb("rows_t", [P, 2, D])
        silu_g = sb("silu_g2", [P, 2, F])
        hidden = sb("hidden", [P, 2, F])
        hidden_t = sb("hidden_t", [P, 2, F])
        result = sb("result", [P, 2, D])
        rows_ps = ctx.enter_context(nc.psum_tensor("rows_ps", [P, 2, D], F32))
        up_ps = ctx.enter_context(nc.psum_tensor("up_ps", [P, 2, 2 * F], F32))
        hid_ps = ctx.enter_context(nc.psum_tensor("hid_ps", [P, 2, 512], F32))
        down_ps = ctx.enter_context(nc.psum_tensor("down_ps", [P, 2, D], F32))

        zeroed, ident_ready = sem("zeroed2"), sem("ident_ready2")
        weights_loaded = [sem(f"weights_loaded{s}") for s in range(WEIGHT_SLOTS)]
        rows_loaded = [sem(f"rows_loaded{s}") for s in range(2)]
        stored = [sem(f"result_stored{s}") for s in range(2)]
        turned, rows_ready, up_ready, silu_ready, hidden_ready, hidden_turned, hid_ready, down_ready, result_ready = (
            sem(n) for n in ("rows_turned", "rows_t_ready", "up_ready", "silu2_ready", "hidden_ready", "hidden_turned",
                             "hidden_t_ready", "down_ready", "result_ready"))
        sorted_x = T["sorted_x"].rearrange("(b p) d -> b p d", p=P)
        sorted_y = T["sorted_y"].rearrange("(b p) d -> b p d", p=P)
        table = plan["table"]
        block = ctx.enter_context(nc.Block())

        def entry(engine, line, b, top):
            return engine.value_load(table[0:1, line, bass.ds(b, 1)], min_val=0, max_val=top)

        @block.gpsimd
        def _(pool):
            nc.gpsimd.memset(ident[:], 0.0).then_inc(zeroed, 1)
            pool.wait_ge(zeroed, 1)
            nc.gpsimd.affine_select(out=ident[:], in_=ident[:], compare_op=ALU.not_equal, fill=1.0, base=0,
                                    pattern=[[-1, P]], channel_multiplier=1).then_inc(ident_ready, 1)

        @block.sync
        def _(sp):
            def load_weights(b, turn):
                expert = entry(sp, 0, b, HEADS - 1)
                slot = entry(sp, 1, b, WEIGHT_SLOTS - 1)
                new = entry(sp, 2, b, 1)
                dst = weights[:, bass.ds(slot * W, W)]
                src = T["w_experts"][bass.ds(expert, 1), :, :].rearrange("a p w -> (a p) w")
                at_least(sp, down_ready, b - WEIGHT_SLOTS + 1)
                sp.dma_start(dst, src, cond=new).then_inc(weights_loaded[turn], 16)

            def load_rows(b, s):
                row_block = entry(sp, 3, b, BLOCKS - 1)
                src = sorted_x[bass.ds(row_block, 1)].rearrange("a p d -> (a p) d")
                at_least(sp, turned, b - 1)
                sp.dma_start(rows[:, s, :], src).then_inc(rows_loaded[s], 16)

            for b in range(4):
                load_weights(b, b)
                load_rows(b, b % 2)
            with sp.Fori(1, BLOCKS // 4) as four:
                for n in range(4):
                    load_weights(4 * four + n, n)
                    load_rows(4 * four + n, n % 2)

        @block.tensor
        def _(pe):
            def turn_rows(b, s, nth):
                pe.wait_ge(rows_loaded[s], 16 * nth)
                at_least(pe, rows_ready, b - 1)
                for c in range(C):
                    last = nc.tensor.transpose(rows_ps[:, s, c * P:(c + 1) * P], rows[:, s, c * P:(c + 1) * P], ident[:])
                last.then_inc(turned, 1)

            def up(b, turn, nth):
                s = turn % 2
                slot = entry(pe, 1, b, WEIGHT_SLOTS - 1)
                pe.wait_ge(weights_loaded[turn], 16 * nth)
                pe.wait_ge(rows_ready, b + 1)
                at_least(pe, hidden_ready, b - 1)
                for c in range(C):
                    last = nc.tensor.matmul(up_ps[:, s, :], rows_t[:, s, c * P:(c + 1) * P],
                                            weights[:, bass.ds(slot * W + c * 2 * F, 2 * F)],
                                            start=(c == 0), stop=(c == C - 1))
                last.then_inc(up_ready, 1)

            def turn_hidden(b, s):
                pe.wait_ge(hidden_ready, b + 1)
                at_least(pe, hid_ready, b - 1)
                for c in range(FC):
                    last = nc.tensor.transpose(hid_ps[:, s, c * P:(c + 1) * P], hidden[:, s, c * P:(c + 1) * P], ident[:])
                last.then_inc(hidden_turned, 1)

            def down(b, s):
                slot = entry(pe, 1, b, WEIGHT_SLOTS - 1)
                pe.wait_ge(hid_ready, b + 1)
                at_least(pe, result_ready, b - 1)
                for c in range(FC):
                    last = nc.tensor.matmul(down_ps[:, s, :], hidden_t[:, s, c * P:(c + 1) * P],
                                            weights[:, bass.ds(slot * W + C * 2 * F + c * D, D)],
                                            start=(c == 0), stop=(c == FC - 1))
                last.then_inc(down_ready, 1)

            pe.wait_ge(ident_ready, 1)
            turn_rows(0, 0, 1)
            up(0, 0, 1)
            turn_rows(1, 1, 1)

            def body(b, turn, fours, more=True):
                s = turn % 2
                up(b, turn, fours + 1)
                turn_hidden(b - 1, 1 - s)
                if more:
                    turn_rows(b + 1, 1 - s, 2 * fours + (turn + 1) // 2 + 1)
                down(b - 1, 1 - s)

            for b in range(1, 4):
                body(b, b, 0)
            with pe.Fori(1, BLOCKS // 4 - 1) as four:
                for turn in range(4):
                    body(4 * four + turn, turn, four)
            for turn in range(4):
                body(BLOCKS - 4 + turn, turn, BLOCKS // 4 - 1, more=(turn < 3))
            turn_hidden(BLOCKS - 1, 1)
            down(BLOCKS - 1, 1)

        @block.scalar
        def _(act):
            def rows_out(b, s):
                act.wait_ge(turned, b + 1)
                at_least(act, up_ready, b - 1)
                nc.scalar.copy(rows_t[:, s, :], rows_ps[:, s, :]).then_inc(rows_ready, 1)

            def silu(b, s):
                act.wait_ge(up_ready, b + 1)
                at_least(act, hidden_ready, b - 1)
                nc.scalar.activation(silu_g[:, s, :], up_ps[:, s, 0:F], ACT.Silu).then_inc(silu_ready, 1)

            def body(b, s):
                silu(b, s)
                rows_out(b + 2, s)

            rows_out(0, 0)
            rows_out(1, 1)
            body(0, 0)
            body(1, 1)
            with act.Fori(1, BLOCKS // 2 - 1) as pair:
                body(2 * pair, 0)
                body(2 * pair + 1, 1)
            silu(BLOCKS - 2, 0)
            silu(BLOCKS - 1, 1)

        @block.vector
        def _(dve):
            def hide(b, s):
                dve.wait_ge(silu_ready, b + 1)
                at_least(dve, hidden_turned, b - 1)
                nc.vector.tensor_tensor(hidden[:, s, :], up_ps[:, s, F:2 * F], silu_g[:, s, :], ALU.mult).then_inc(hidden_ready, 1)

            def hidden_out(b, s):
                dve.wait_ge(hidden_turned, b + 1)
                at_least(dve, down_ready, b - 1)
                nc.vector.tensor_copy(hidden_t[:, s, :], hid_ps[:, s, 0:F]).then_inc(hid_ready, 1)

            def result_out(b, s, nth):
                dve.wait_ge(down_ready, b + 1)
                at_least(dve, stored[s], 16 * nth)
                nc.vector.tensor_copy(result[:, s, :], down_ps[:, s, :]).then_inc(result_ready, 1)

            def body(b, s, nth):
                hide(b, s)
                hidden_out(b - 1, 1 - s)
                result_out(b - 1, 1 - s, nth)

            hide(0, 0)
            body(1, 1, 0)
            body(2, 0, 0)
            with dve.Fori(1, BLOCKS // 2 - 1) as pair:
                body(2 * pair + 1, 1, pair)
                body(2 * pair + 2, 0, pair)
            body(BLOCKS - 1, 1, BLOCKS // 2 - 1)
            hidden_out(BLOCKS - 1, 1)
            result_out(BLOCKS - 1, 1, BLOCKS // 2 - 1)

        @block.gpsimd
        def _(pool):
            def store(b, s):
                dst = sorted_y[bass.ds(b, 1)].rearrange("a p d -> (a p) d") if not isinstance(b, int) else sorted_y[b]
                pool.wait_ge(result_ready, b + 1)
                pool.dma_start(dst, result[:, s, :]).then_inc(stored[s], 16)

            store(0, 0)
            store(1, 1)
            with pool.Fori(1, BLOCKS // 2) as pair:
                store(2 * pair, 0)
                store(2 * pair + 1, 1)
            for s in range(2):
                pool.wait_ge(stored[s], 16 * (BLOCKS // 2))


def stage_combine(nc, T, keep, plan):
    NT = keep["tiles"]
    D = 512
    with ExitStack() as ctx:
        def sb(name, shape, dt=F32):
            return ctx.enter_context(nc.sbuf_tensor(name, shape, dt))

        def sem(name):
            return ctx.enter_context(nc.semaphore(name))

        DEPTH = 4
        picked = sb("picked_rows", [P, DEPTH, TOP_K, D])
        total = sb("total", [P, DEPTH, D])
        gathered = [sem(f"gathered{s}") for s in range(DEPTH)]
        base_loaded = [sem(f"base_loaded{s}") for s in range(DEPTH)]
        out_stored = [sem(f"out_stored{s}") for s in range(DEPTH)]
        added = sem("added")
        base = T["base"].rearrange("b (t p) d -> (b t) p d", p=P)
        out = T["out"].rearrange("b (t p) d -> (b t) p d", p=P)
        block = ctx.enter_context(nc.Block())

        @block.gpsimd
        def _(pool):
            for t in range(NT):
                s = t % DEPTH
                at_least(pool, added, TOP_K * (t - DEPTH + 1))
                for k in range(TOP_K):
                    pool.indirect_dma_start(picked[:, s, k, :], None, T["sorted_y"],
                                            bass.IndirectOffsetOnAxis(ap=plan["place"][:, k, t:t + 1], axis=0),
                                            bounds_check=keep["blocks"] * P - 1,
                                            oob_is_err=False).then_inc(gathered[s], 16)

        @block.sync
        def _(sp):
            def load_base(t):
                at_least(sp, out_stored[t % DEPTH], 16 * (t // DEPTH))
                sp.dma_start(total[:, t % DEPTH, :], base[t]).then_inc(base_loaded[t % DEPTH], 16)

            for t in range(DEPTH):
                load_base(t)
            for t in range(NT):
                sp.wait_ge(added, TOP_K * (t + 1))
                sp.dma_start(out[t], total[:, t % DEPTH, :]).then_inc(out_stored[t % DEPTH], 16)
                if t + DEPTH < NT:
                    load_base(t + DEPTH)
            for s in range(DEPTH):
                sp.wait_ge(out_stored[s], 16 * (NT // DEPTH))

        @block.vector
        def _(dve):
            for t in range(NT):
                s = t % DEPTH
                dve.wait_ge(gathered[s], 16 * TOP_K * (t // DEPTH + 1))
                dve.wait_ge(base_loaded[s], 16 * (t // DEPTH + 1))
                for k in range(TOP_K):
                    at_least(dve, added, TOP_K * t + k)
                    nc.vector.scalar_tensor_tensor(out=total[:, s, :], in0=picked[:, s, k, :],
                                                   scalar=plan["weight"][:, k, t:t + 1], in1=total[:, s, :],
                                                   op0=ALU.mult, op1=ALU.add).then_inc(added, 1)


def program(nc, T):
    B, S, D = T["x"].shape
    NT = B * S // P
    BLOCKS = NT * TOP_K + HEADS
    T = dict(T)
    T["xn2"] = nc.dram_tensor("xn2_rows", [B, S, D], F32).ap()
    T["base"] = nc.dram_tensor("base_rows", [B, S, D], F32).ap()
    T["sorted_x"] = nc.dram_tensor("sorted_x", [BLOCKS * P, D], F32).ap()
    T["sorted_y"] = nc.dram_tensor("sorted_y", [BLOCKS * P, D], F32).ap()
    with (
        nc.sbuf_tensor("place_of", [P, TOP_K, NT], U32) as place,
        nc.sbuf_tensor("weight_of", [P, TOP_K, NT], F32) as weight,
        nc.sbuf_tensor("block_table", [1, 4, BLOCKS], I32) as table,
    ):
        plan = {"place": place, "weight": weight, "table": table}
        keep = {"tiles": NT, "blocks": BLOCKS}
        with nc.sbuf_tensor("logits_all", [P, NT, HEADS], F32) as logits:
            keep["logits"] = logits
            stage_attend(nc, T, keep)
            stage_route(nc, T, keep, plan)
        stage_experts(nc, T, keep, plan)
        stage_combine(nc, T, keep, plan)


def lay_out(inputs):
    x = np.ascontiguousarray(inputs["x"])
    B, S, D = x.shape

    def by_chunk(w):
        w = np.asarray(w)
        w = np.swapaxes(w, -1, -2)
        w = w.reshape(*w.shape[:-2], w.shape[-2] // P, P, w.shape[-1])
        return np.ascontiguousarray(np.swapaxes(w, -3, -2))

    wkv = np.asarray(inputs["L0_xattn_Wkv"])
    w1, w3, w2 = (np.asarray(inputs[f"L0_ffn_w{n}_e"]) for n in (1, 3, 2))
    E = w1.shape[0]
    up = by_chunk(np.concatenate([w1, w3], axis=1)).reshape(E, P, -1)
    down = by_chunk(w2).reshape(E, P, -1)
    return {
        "x": x,
        "ctx_t": by_chunk(inputs["ctx_1024"]),
        "mask_t": by_chunk(inputs["mask_BxSxS2_bk0"]),
        "wq": by_chunk(inputs["L0_xattn_Wq"]),
        "wk": by_chunk(wkv[:D]),
        "wv": by_chunk(wkv[D:]),
        "wo": by_chunk(inputs["L0_xattn_Wo"]),
        "nbias": np.ascontiguousarray(inputs["L0_xattn_nbias"]),
        "wg": by_chunk(inputs["L0_ffn_w_gate"]),
        "ws1": by_chunk(inputs["L0_ffn_w1_s"]),
        "ws3": by_chunk(inputs["L0_ffn_w3_s"]),
        "ws2": by_chunk(inputs["L0_ffn_w2_s"]),
        "w_experts": np.ascontiguousarray(np.concatenate([up, down], axis=2)),
    }


def kernel(**inputs):
    import concourse.bacc as bacc
    from concourse.bass_utils import run_bass_kernel_spmd

    arrays = {f"in_{name}": a for name, a in lay_out(inputs).items()}
    nc = bacc.Bacc("TRN2", target_bir_lowering=False, num_devices=1)
    T = {name[3:]: nc.dram_tensor(name, a.shape, mybir.dt.from_np(a.dtype), kind="ExternalInput").ap()
         for name, a in arrays.items()}
    T["out"] = nc.dram_tensor("out_rows", inputs["x"].shape, F32, kind="ExternalOutput").ap()
    program(nc, T)
    result = run_bass_kernel_spmd(nc, [arrays], core_ids=[0])
    return result.results[0]["out_rows"]
```

```python
from contextlib import ExitStack

import numpy as np

import concourse.bass as bass
from concourse import mybir

ALU = mybir.AluOpType
ACT = mybir.ActivationFunctionType
F32 = mybir.dt.float32
F32R = mybir.dt.float32r
BF16 = mybir.dt.bfloat16
I32 = mybir.dt.int32
U32 = mybir.dt.uint32
U8 = mybir.dt.uint8
AX_X = mybir.AxisListType.X

P = 128
HEADS = 16
HEAD_DIM = 32
LN_EPS = 1e-5
NORM_EPS = 1e-32
ROUTE_EPS = 1e-6
GROUPS = 4
GROUP_SIZE = 4
TOP_K = 4
WEIGHT_SLOTS = 4
STORE_LAG = 6
SHARED_PARTS = 2
XN2_LOADS = 4
FAR = 1.0e6


def at_least(engine, semaphore, value):
    if not isinstance(value, int) or value > 0:
        engine.wait_ge(semaphore, value)


def split_products(nc, out, pairs, first=True, last=True):
    instruction = None
    for n, (lh, ll, rh, rl) in enumerate(pairs):
        for k, (left, right) in enumerate(((lh, rh), (lh, rl), (ll, rh))):
            instruction = nc.tensor.matmul(out, left, right, start=(first and n == 0 and k == 0),
                                           stop=(last and n == len(pairs) - 1 and k == 2))
    return instruction


def stage_attend(nc, T, keep):
    B, S, D = T["x"].shape
    C = D // P
    ST = S // P
    assert (D, S, HEADS * HEAD_DIM) == (512, 256, 512) and B >= 4
    JOBS, _, W = T["w_experts"].shape
    HALF = W // 2
    assert JOBS == HEADS + SHARED_PARTS
    scale = float(HEAD_DIM) ** -0.5

    with ExitStack() as ctx:
        def sb(name, shape, dt=F32):
            return ctx.enter_context(nc.sbuf_tensor(name, shape, dt))

        def sem(name):
            return ctx.enter_context(nc.semaphore(name))

        wk, wq, wv, wo = (sb(n, [P, 2, C, D], F32R) for n in ("wk", "wq", "wv", "wo"))
        wg = sb("wg", [P, C, 16])
        ident = sb("ident", [P, P])
        ones = sb("ones", [P, HEAD_DIM])
        minus_half = sb("minus_half", [P, ST])
        nbias = sb("nbias_all", [P, 1])
        x_in = sb("x_in", [P, ST, D])
        x_res = sb("x_res", [P, ST, D])
        ctx_in = sb("ctx_in", [P, C, S])
        ctx_t = sb("ctx_t", [P, 2, C, S], F32R)
        mask = sb("mask_t", [P, B, ST, S], U8)
        bound = sb("bound", [P, ST, S])
        stats = sb("stats", [P, 2, ST, 6])
        mean_var = sb("mean_var", [P, 2, ST, 2])
        var_eps = sb("var_eps", [P, 2, ST])
        rstd = sb("rstd", [P, 2, ST])
        spacer = sb("spacer", [P, 2])
        eps = sb("eps", [P, ST])
        xn = sb("xn", [P, ST, D])
        xn_t = sb("xn_t", [P, 2, C, S], F32R)
        q_diag = sb("q_diag", [P, C, 4, S])
        k_t = sb("k_t", [P, C, S])
        v_nat = sb("v_nat", [P, ST, D])
        probs = sb("probs", [P, 2, ST, 4, S])
        den = sb("den", [P, S])
        rec = sb("rec", [P, S])
        o_all = sb("o_all", [P, C, S])
        o_t = sb("o_t", [P, 2, C, S], F32R)
        x1 = sb("x1", [P, ST, D])
        xn2 = sb("xn2", [P, ST, D])
        xn2_t = sb("xn2_t", [P, C, S])
        part = sb("expert_part", [P, HALF])
        part_high = sb("expert_part_high", [P, HALF], F32R)
        part_low = sb("expert_part_low", [P, HALF], F32R)

        psum = ctx.enter_context(nc.psum_tensor("attend_banks", [P, 3, 512], F32))
        sc = ctx.enter_context(nc.psum_tensor("attend_scores", [P, ST, 4 * S], F32))
        av = ctx.enter_context(nc.psum_tensor("attend_av", [P, 2, S], F32))

        w_loaded = [sem(f"w_loaded{n}") for n in range(4)]
        consts_loaded = sem("consts_loaded")
        x_loaded, ctx_loaded, mask_loaded, res_loaded, part_loaded = (
            sem(n) for n in ("x_loaded", "ctx_loaded", "mask_loaded", "res_loaded", "part_loaded"))
        xn2_kept, base_stored, xn2t_stored, part_stored = (
            sem(n) for n in ("xn2_kept", "base_stored", "xn2t_stored", "part_stored"))
        zeroed, ident_ready, q_zeroed, consts_made = (
            sem(n) for n in ("zeroed", "ident_ready", "q_zeroed", "consts_made"))
        xn_turned, q_done, k_done, v_done, o_done, xn2_turned, gate_done, scores_ready, av_ready = (
            sem(n) for n in ("xn_turned", "q_done", "k_done", "v_done", "o_done", "xn2_turned", "gate_done",
                             "scores_ready", "av_ready"))
        w_high, ctx_high, xn_high, q_ready, k_ready, v_ready, xn2t_ready, gate_ready, o_high, part_high_ready = (
            sem(n) for n in ("w_high", "ctx_high", "xn_high", "q_ready", "k_ready", "v_ready", "xn2t_ready",
                             "gate_ready", "o_high", "part_high_ready"))
        w_low, xn_low, stats1, var1, xn_ready, stats2, var2, xn2_ready, x1_ready, bound_ready = (
            sem(n) for n in ("w_low", "xn_low", "stats1", "var1", "xn_ready", "stats2", "var2", "xn2_ready",
                             "x1_ready", "bound_ready"))
        clipped, probs_ready, den_ready, rec_ready, o_ready = (
            sem(n) for n in ("clipped", "probs_ready", "den_ready", "rec_ready", "o_ready"))
        eps1, rstd1, eps2, rstd2, ctx_low, o_low, part_low_ready = (
            sem(n) for n in ("eps1", "rstd1", "eps2", "rstd2", "ctx_low", "o_low",
                             "part_low_ready"))

        tokens = T["x"].rearrange("b (t p) d -> b p t d", p=P)
        base_dram = T["base"].rearrange("b (t p) d -> b p t d", p=P)
        xn2_dram = T["xn2"].rearrange("b (t p) d -> b p t d", p=P)
        parts = T["w_experts"].rearrange("e p (h w) -> e h p w", h=2)
        parts_high = T["w_high"].bitcast(F32).rearrange("e p (h w) -> e h p w", h=2)
        parts_low = T["w_low"].bitcast(F32).rearrange("e p (h w) -> e h p w", h=2)

        def halves(i):
            own = [(i, 0), (i, 1)]
            if isinstance(i, int) and i < 2:
                return own + [(HEADS, i)]
            if isinstance(i, int) and i == B - 1:
                return own + [(HEADS + 1, 0), (HEADS + 1, 1)]
            return own

        def nth_half(i):
            if isinstance(i, int) and i < 2:
                return 3 * i
            return 2 * i + (4 if isinstance(i, int) and i >= B else 2)

        def pick(ap, i, *more):
            if isinstance(i, int):
                return ap[(i, *more)]
            axes = {3: "a p s -> (a p) s", 4: "a p t s -> (a p) t s"}
            ap = ap[(bass.ds(i, 1), *more)]
            return ap.rearrange(axes[len(ap.shape)])

        block = ctx.enter_context(nc.Block())

        @block.sync
        def _(sp):
            def load(dst, src, free, count, loaded):
                at_least(sp, free, count)
                sp.dma_start(dst, src).then_inc(loaded, 16)

            def load_part(e, h, nth):
                load(part[:], pick(parts, e, h), part_low_ready, nth, part_loaded)

            def store_part(e, h, nth):
                at_least(sp, part_high_ready, nth + 1)
                sp.dma_start(pick(parts_high, e, h), part_high[:].bitcast(F32)).then_inc(part_stored, 16)
                at_least(sp, part_low_ready, nth + 1)
                sp.dma_start(pick(parts_low, e, h), part_low[:].bitcast(F32)).then_inc(part_stored, 16)

            def store(dst, src, ready, count, stored):
                at_least(sp, ready, count)
                sp.dma_start(dst, src).then_inc(stored, 16)

            def back_stores(j, i):
                store(pick(base_dram, j), x1[:], x1_ready, ST * (j + 1), base_stored)
                if i is not None:
                    load(x_res[:], pick(tokens, i), x1_ready, ST * i, res_loaded)
                store(pick(xn2_dram, j), xn2[:], xn2_ready, ST * (j + 1), xn2_kept)
                store(pick(T["xn2_t"], j), xn2_t[:], xn2t_ready, ST * (j + 1), xn2t_stored)

            staged = [probs[:, n, :, :, :].rearrange("p t h s -> p (t h s)").rearrange("p (c d) -> p c d", c=C)
                      for n in range(2)]
            load(ctx_in[:], pick(T["ctx_t"], 0), ctx_low, 0, ctx_loaded)
            load(staged[0], T["wk"], w_low, 0, w_loaded[0])
            load(x_in[:], pick(tokens, 0), xn_ready, 0, x_loaded)
            load(staged[1], T["wq"], w_low, 0, w_loaded[1])
            sp.dma_start(wg[:], T["wg"]).then_inc(consts_loaded, 16)
            sp.dma_start(nbias[:], T["nbias"].rearrange("(a b) -> a b", a=1).to_broadcast([P, 1])).then_inc(consts_loaded, 16)
            load(staged[0], T["wv"], w_low, 1, w_loaded[2])
            load(staged[1], T["wo"], w_low, 2, w_loaded[3])
            sp.dma_start(mask[:], T["mask_t"].rearrange("b p t s -> p b t s")).then_inc(mask_loaded, 16)
            load(x_in[:], pick(tokens, 1), xn_ready, ST, x_loaded)
            load(ctx_in[:], pick(T["ctx_t"], 1), ctx_low, 1, ctx_loaded)
            load(x_res[:], pick(tokens, 0), x1_ready, 0, res_loaded)
            load_part(0, 0, 0)

            def body(i, back=True, ahead2=True, more=True):
                split = [(*half, nth_half(i) + n) for n, half in enumerate(halves(i))]
                if ahead2:
                    load(x_in[:], pick(tokens, i + 2), xn_ready, ST * (i + 2), x_loaded)
                    load(ctx_in[:], pick(T["ctx_t"], i + 2), ctx_low, i + 2, ctx_loaded)
                store_part(*split[0])
                load_part(*split[1])
                if back:
                    back_stores(i - 1, i)
                store_part(*split[1])
                for half in split[2:]:
                    load_part(*half)
                    store_part(*half)
                if more:
                    load_part(i + 1, 0, split[-1][2] + 1)

            body(0, back=False)
            body(1)
            with sp.Fori(2, B - 2) as i:
                body(i)
            body(B - 2, ahead2=False)
            body(B - 1, ahead2=False, more=False)
            back_stores(B - 1, None)
            for e in range(B, HEADS):
                for h in range(2):
                    load_part(e, h, nth_half(e) + h)
                    store_part(e, h, nth_half(e) + h)
            sp.wait_ge(xn2_kept, 16 * B)
            sp.wait_ge(base_stored, 16 * B)
            sp.wait_ge(xn2t_stored, 16 * B)
            sp.wait_ge(part_stored, 64 * JOBS)

        @block.gpsimd
        def _(pool):
            nc.gpsimd.memset(ident[:], 0.0).then_inc(zeroed, 1)
            nc.gpsimd.memset(minus_half[:], -0.5).then_inc(consts_made, 1)
            nc.gpsimd.memset(ones[:], 1.0).then_inc(consts_made, 1)
            nc.gpsimd.memset(eps[:], LN_EPS).then_inc(consts_made, 1)
            pool.wait_ge(zeroed, 1)
            nc.gpsimd.affine_select(out=ident[:], in_=ident[:], compare_op=ALU.not_equal, fill=1.0, base=0,
                                    pattern=[[-1, P]], channel_multiplier=1).then_inc(ident_ready, 1)
            nc.gpsimd.memset(q_diag[:], 0.0).then_inc(q_zeroed, 1)
            pool.wait_ge(consts_made, 3)

            def inverse_std(which, n, var, eps_ready, done):
                at_least(pool, var, ST * (n + 1))
                nc.gpsimd.tensor_tensor(var_eps[:, which, :], mean_var[:, which, :, 1], eps[:],
                                        ALU.add).then_inc(eps_ready, 1)
                at_least(pool, eps_ready, n + 1)
                nc.gpsimd.tensor_tensor(rstd[:, which, :], var_eps[:, which, :], minus_half[:], ALU.pow).then_inc(done, 1)

            def context_low(n):
                at_least(pool, ctx_high, n + 1)
                nc.gpsimd.tensor_tensor(ctx_t[:, 1, :, :], ctx_in[:], ctx_t[:, 0, :, :].bitcast(F32),
                                        ALU.subtract).then_inc(ctx_low, 1)

            def expert_low(nth):
                at_least(pool, part_high_ready, nth + 1)
                at_least(pool, part_stored, 32 * nth)
                nc.gpsimd.tensor_tensor(part_low[:], part[:], part_high[:].bitcast(F32),
                                        ALU.subtract).then_inc(part_low_ready, 1)

            def output_low(i, c):
                at_least(pool, o_high, 4 * i + c + 1)
                nc.gpsimd.tensor_tensor(o_t[:, 1, c, :], o_all[:, c, :], o_t[:, 0, c, :].bitcast(F32),
                                        ALU.subtract).then_inc(o_low, 1)

            def body(i, back=True, next1=True, next2=True):
                if next1:
                    context_low(i + 1)
                expert_low(nth_half(i))
                if back:
                    inverse_std(1, i - 1, var2, eps2, rstd2)
                output_low(i, 0)
                output_low(i, 1)
                if next2:
                    inverse_std(0, i + 2, var1, eps1, rstd1)
                expert_low(nth_half(i) + 1)
                output_low(i, 2)
                output_low(i, 3)
                for n in range(2, len(halves(i))):
                    expert_low(nth_half(i) + n)

            context_low(0)
            inverse_std(0, 0, var1, eps1, rstd1)
            inverse_std(0, 1, var1, eps1, rstd1)
            body(0, back=False)
            body(1)
            with pool.Fori(2, B - 2) as i:
                body(i)
            body(B - 2, next2=False)
            body(B - 1, next1=False, next2=False)
            inverse_std(1, B - 1, var2, eps2, rstd2)
            for nth in range(nth_half(B), nth_half(HEADS)):
                expert_low(nth)

        @block.tensor
        def _(pe):
            def transposes(n, t):
                at_least(pe, xn_ready, ST * n + t + 1)
                at_least(pe, v_ready, ST * (n - 1) + t + 1)
                if t == 1:
                    at_least(pe, x1_ready, ST * (n - 2) + 1)
                bank = 2 - 2 * t
                for c in range(C):
                    last = nc.tensor.transpose(psum[:, bank, c * P:(c + 1) * P], xn[:, t, c * P:(c + 1) * P], ident[:])
                last.then_inc(xn_turned, 1)

            def project(out, w, source, u):
                for cc in range(2):
                    channels = slice((2 * u + cc) * P, (2 * u + cc + 1) * P)
                    last = split_products(nc, out[:, cc * S:(cc + 1) * S],
                                          [(w[:, 0, c, channels], w[:, 1, c, channels], source[:, 0, c, :], source[:, 1, c, :])
                                           for c in range(C)])
                return last

            def q_unit(n, u):
                at_least(pe, w_low, 2)
                at_least(pe, xn_low, ST * (n + 1))
                if u == 1:
                    at_least(pe, xn2t_ready, ST * (n - 2) + 1)
                project(psum[:, (2, 0)[u], :], wq, xn_t, u).then_inc(q_done, 1)

            def k_unit(n, u):
                at_least(pe, w_low, 1)
                at_least(pe, ctx_low, n + 1)
                if u == 0:
                    at_least(pe, k_ready, 2 * n)
                    at_least(pe, x1_ready, ST * (n - 1))
                else:
                    at_least(pe, k_ready, 2 * n + 1)
                    at_least(pe, xn2t_ready, ST * (n - 1))
                project(psum[:, 1, :], wk, ctx_t, u).then_inc(k_done, 1)

            def v_unit(n, t):
                at_least(pe, w_low, 3)
                if t == 0:
                    at_least(pe, q_ready, 2 * n + 1)
                    at_least(pe, gate_ready, n - 1)
                else:
                    at_least(pe, q_ready, 2 * n + 2)
                tile = slice(t * P, (t + 1) * P)
                split_products(nc, psum[:, 2 - 2 * t, :],
                               [(ctx_t[:, 0, c, tile], ctx_t[:, 1, c, tile], wv[:, 0, c, :], wv[:, 1, c, :])
                                for c in range(C)]).then_inc(v_done, 1)

            def scores(i, c):
                at_least(pe, q_ready, 2 * i + c // 2 + 1)
                at_least(pe, k_ready, 2 * i + c // 2 + 1)
                for st in range(ST):
                    at_least(pe, clipped, 8 * i + 2 * (c - 1) + st + 1)
                    for half in range(2):
                        last = nc.tensor.matmul(sc[:, st, half * 512:(half + 1) * 512], k_t[:, c, st * P:(st + 1) * P],
                                                q_diag[:, c, 2 * half:2 * half + 2, :], start=True, stop=True)
                    last.then_inc(scores_ready, 1)

            def attend(i, c):
                at_least(pe, probs_ready, 8 * i + 2 * c + 2)
                at_least(pe, v_ready, ST * (i + 1))
                at_least(pe, o_ready, 4 * i + c)
                for what in range(2):
                    for st in range(ST):
                        for j in range(4):
                            h = 4 * c + j
                            left = ones[:] if what else v_nat[:, st, h * HEAD_DIM:(h + 1) * HEAD_DIM]
                            last = nc.tensor.matmul(av[32 * j:32 * j + 32, what, :], left, probs[:, c % 2, st, j, :],
                                                    start=(st == 0), stop=(st == ST - 1), tile_position=(0, 32 * j),
                                                    skip_group_check=True)
                last.then_inc(av_ready, 1)

            def o_unit(j, t):
                at_least(pe, o_low, 4 * (j + 1))
                at_least(pe, xn2t_ready, ST * j)
                if t == 0:
                    if isinstance(j, int) and j == B - 1:
                        at_least(pe, v_ready, ST * B)
                    else:
                        at_least(pe, v_ready, ST * (j + 2))
                    bank = 0
                else:
                    if isinstance(j, int) and j == B - 1:
                        at_least(pe, k_ready, 2 * B)
                    else:
                        at_least(pe, k_ready, 2 * (j + 2))
                    bank = 1
                tile = slice(t * P, (t + 1) * P)
                split_products(nc, psum[:, bank, :],
                               [(o_t[:, 0, c, tile], o_t[:, 1, c, tile], wo[:, 0, c, :], wo[:, 1, c, :])
                                for c in range(C)]).then_inc(o_done, 1)

            def xn2t_unit(j, t, more):
                at_least(pe, xn2_ready, ST * j + t + 1)
                if more:
                    if t == 0:
                        at_least(pe, xn_low, ST * (j + 3))
                    else:
                        at_least(pe, k_ready, 2 * (j + 2) + 1)
                for c in range(C):
                    last = nc.tensor.transpose(psum[:, t, c * P:(c + 1) * P], xn2[:, t, c * P:(c + 1) * P], ident[:])
                last.then_inc(xn2_turned, 1)

            def gate_unit(j, more):
                at_least(pe, xn2t_ready, ST * (j + 1))
                if more:
                    at_least(pe, q_ready, 2 * (j + 2) + 1)
                at_least(pe, gate_ready, j)
                for t in range(ST):
                    for c in range(C):
                        last = nc.tensor.matmul(psum[:, 2, 16 * t:16 * t + 16], xn2_t[:, c, t * P:(t + 1) * P], wg[:, c, :],
                                                start=(c == 0), stop=(c == C - 1))
                last.then_inc(gate_done, 1)

            def body(i, back=True, more=True):
                j, n = i - 1, i + 1
                scores(i, 0)
                if back:
                    o_unit(j, 0)
                    o_unit(j, 1)
                if more:
                    transposes(n, 0)
                scores(i, 1)
                if more:
                    transposes(n, 1)
                    k_unit(n, 0)
                attend(i, 0)
                if more:
                    q_unit(n, 0)
                scores(i, 2)
                if back:
                    xn2t_unit(j, 0, more)
                    xn2t_unit(j, 1, more)
                attend(i, 1)
                if back:
                    gate_unit(j, more)
                scores(i, 3)
                if more:
                    q_unit(n, 1)
                attend(i, 2)
                if more:
                    k_unit(n, 1)
                attend(i, 3)
                if more:
                    v_unit(n, 0)
                    v_unit(n, 1)

            pe.wait_ge(ident_ready, 1)
            k_unit(0, 0)
            k_unit(0, 1)
            transposes(0, 0)
            transposes(0, 1)
            q_unit(0, 0)
            q_unit(0, 1)
            v_unit(0, 0)
            v_unit(0, 1)
            pe.wait_ge(consts_loaded, 16 * 2)
            pe.wait_ge(consts_made, 3)
            pe.wait_ge(q_zeroed, 1)
            pe.wait_ge(w_low, 4)
            body(0, back=False)
            body(1)
            with pe.Fori(2, B - 1) as i:
                body(i)
            body(B - 1, more=False)
            j = B - 1
            o_unit(j, 0)
            o_unit(j, 1)
            xn2t_unit(j, 0, False)
            xn2t_unit(j, 1, False)
            gate_unit(j, False)

        @block.scalar
        def _(act):
            copy = nc.scalar.copy

            def context_high(n):
                at_least(act, ctx_loaded, 16 * (n + 1))
                at_least(act, v_done, ST * n)
                copy(ctx_t[:, 0, :, :], ctx_in[:]).then_inc(ctx_high, 1)

            def tokens_high(n, t):
                at_least(act, xn_turned, ST * n + t + 1)
                at_least(act, q_done, 2 * n)
                copy(xn_t[:, 0, :, t * P:(t + 1) * P],
                     psum[:, 2 - 2 * t, :].rearrange("p (c s) -> p c s", c=C)).then_inc(xn_high, 1)

            def q_out(n, u):
                at_least(act, q_done, 2 * n + u + 1)
                at_least(act, scores_ready, 8 * (n - 1) + 4 * (u + 1))
                for h in range(4):
                    part = slice(32 * h, 32 * h + 32)
                    last = nc.scalar.mul(q_diag[part, 2 * u:2 * u + 2, h, :],
                                         psum[part, (2, 0)[u], :].rearrange("p (c s) -> p c s", c=2), scale)
                last.then_inc(q_ready, 1)

            def k_out(n, u):
                at_least(act, k_done, 2 * n + u + 1)
                at_least(act, scores_ready, 8 * (n - 1) + 4 * (u + 1))
                copy(k_t[:, 2 * u:2 * u + 2, :], psum[:, 1, :].rearrange("p (c s) -> p c s", c=2)).then_inc(k_ready, 1)

            def v_out(n, t):
                at_least(act, v_done, ST * n + t + 1)
                at_least(act, av_ready, 4 * n)
                copy(v_nat[:, t, :], psum[:, 2 - 2 * t, :]).then_inc(v_ready, 1)

            def xn2t_out(j, t):
                at_least(act, xn2_turned, ST * j + t + 1)
                at_least(act, xn2t_stored, 16 * j)
                at_least(act, gate_done, j)
                copy(xn2_t[:, :, t * P:(t + 1) * P], psum[:, t, :].rearrange("p (c s) -> p c s", c=C)).then_inc(xn2t_ready, 1)

            def gate_out(j):
                at_least(act, gate_done, j + 1)
                copy(keep["logits"][:, bass.ds(j * ST, ST), :],
                     psum[:, 2, 0:16 * ST].rearrange("p (t e) -> p t e", t=ST)).then_inc(gate_ready, 1)

            def output_high(i, c):
                at_least(act, o_ready, 4 * i + c + 1)
                if c == 0:
                    at_least(act, o_done, ST * i)
                copy(o_t[:, 0, c, :], o_all[:, c, :]).then_inc(o_high, 1)

            def expert_high(nth):
                at_least(act, part_loaded, 16 * (nth + 1))
                at_least(act, part_stored, 32 * nth)
                copy(part_high[:], part[:]).then_inc(part_high_ready, 1)

            def body(i, back=True, more=True):
                j, n = i - 1, i + 1
                if more:
                    context_high(n)
                expert_high(nth_half(i))
                if more:
                    tokens_high(n, 0)
                    tokens_high(n, 1)
                    k_out(n, 0)
                output_high(i, 0)
                if more:
                    q_out(n, 0)
                if back:
                    xn2t_out(j, 0)
                    xn2t_out(j, 1)
                output_high(i, 1)
                if back:
                    gate_out(j)
                expert_high(nth_half(i) + 1)
                if more:
                    q_out(n, 1)
                output_high(i, 2)
                if more:
                    k_out(n, 1)
                output_high(i, 3)
                if more:
                    v_out(n, 0)
                    v_out(n, 1)
                for n in range(2, len(halves(i))):
                    expert_high(nth_half(i) + n)

            staged = [probs[:, n, :, :, :].rearrange("p t h s -> p (t h s)").rearrange("p (c d) -> p c d", c=C)
                      for n in range(2)]

            def weight_high(n):
                act.wait_ge(w_loaded[n], 16)
                copy((wk, wq, wv, wo)[n][:, 0, :, :], staged[n % 2]).then_inc(w_high, 1)

            context_high(0)
            weight_high(0)
            weight_high(1)
            k_out(0, 0)
            k_out(0, 1)
            weight_high(2)
            tokens_high(0, 0)
            tokens_high(0, 1)
            act.wait_ge(q_zeroed, 1)
            q_out(0, 0)
            weight_high(3)
            q_out(0, 1)
            v_out(0, 0)
            v_out(0, 1)
            body(0, back=False)
            body(1)
            with act.Fori(2, B - 1) as i:
                body(i)
            body(B - 1, more=False)
            xn2t_out(B - 1, 0)
            xn2t_out(B - 1, 1)
            gate_out(B - 1)
            for nth in range(nth_half(B), nth_half(HEADS)):
                expert_high(nth)

        @block.vector
        def _(dve):
            def moments(src, which, n, stats_done, var_done):
                for t in range(ST):
                    nc.vector.bn_stats(stats[:, which, t, :], src[:, t, :]).then_inc(stats_done, 1)
                at_least(dve, stats_done, ST * (n + 1))
                nc.vector.memset(spacer[:, which:which + 1], 0.0)
                for t in range(ST):
                    nc.vector.bn_aggr(mean_var[:, which, t, :], stats[:, which, t, :]).then_inc(var_done, 1)

            def normalise(dst, src, which, n, rstd_done, done):
                at_least(dve, rstd_done, n + 1)
                for t in range(ST):
                    nc.vector.tensor_scalar(dst[:, t, :], src[:, t, :], mean_var[:, which, t, 0:1], rstd[:, which, t:t + 1],
                                            ALU.subtract, ALU.mult).then_inc(done, 1)

            def moments1(n):
                at_least(dve, rstd1, n)
                at_least(dve, x_loaded, 16 * (n + 1))
                moments(x_in, 0, n, stats1, var1)

            def normalise1(n):
                at_least(dve, xn_turned, ST * n)
                normalise(xn, x_in, 0, n, rstd1, xn_ready)

            def tokens_low(n, t):
                at_least(dve, xn_high, ST * n + t + 1)
                tile = slice(t * P, (t + 1) * P)
                nc.vector.tensor_tensor(xn_t[:, 1, :, tile], psum[:, 2 - 2 * t, :].rearrange("p (c s) -> p c s", c=C),
                                        xn_t[:, 0, :, tile].bitcast(F32), ALU.subtract).then_inc(xn_low, 1)

            def residual(j):
                at_least(dve, res_loaded, 16 * (j + 1))
                at_least(dve, base_stored, 16 * j)
                for t in range(ST):
                    at_least(dve, o_done, ST * j + t + 1)
                    nc.vector.tensor_tensor(x1[:, t, :], psum[:, t, :], x_res[:, t, :], ALU.add).then_inc(x1_ready, 1)
                at_least(dve, x1_ready, ST * (j + 1))
                moments(x1, 1, j, stats2, var2)

            def normalise2(j):
                at_least(dve, xn2_kept, 16 * j)
                normalise(xn2, x1, 1, j, rstd2, xn2_ready)

            def make_bound(i):
                at_least(dve, clipped, 8 * i)
                big = float(np.finfo(np.float32).max)
                for t in range(ST):
                    part = mask[:, i, t, :] if isinstance(i, int) else mask[:, bass.ds(i, 1), t, :].rearrange("p a s -> p (a s)")
                    nc.vector.tensor_scalar(bound[:, t, :], part, -big, big, ALU.mult, ALU.add).then_inc(bound_ready, 1)

            def probabilities(i, c):
                at_least(dve, bound_ready, ST * (i + 1))
                at_least(dve, av_ready, 4 * i + c - 1)
                for st in range(ST):
                    at_least(dve, scores_ready, 8 * i + 2 * c + st + 1)
                    nc.vector.scalar_tensor_tensor(
                        out=probs[:, c % 2, st, :, :], in0=sc[:, st, :].rearrange("p (h s) -> p h s", h=4),
                        scalar=nbias[:, 0:1], in1=bound[:, st:st + 1, :].to_broadcast([P, 4, S]),
                        op0=ALU.add, op1=ALU.min).then_inc(clipped, 1)
                for st in range(ST):
                    at_least(dve, clipped, 8 * i + 2 * c + st + 1)
                    x = probs[:, c % 2, st, :, :].rearrange("p h s -> p (h s)")
                    nc.vector.scalar_tensor_tensor(out=x, in0=x, scalar=0.0, in1=x, op0=ALU.max,
                                                   op1=ALU.mult).then_inc(probs_ready, 1)

            def divide(i, c):
                at_least(dve, av_ready, 4 * i + c + 1)
                nc.vector.tensor_scalar(den[:], av[:, 1, :], NORM_EPS, None, ALU.add).then_inc(den_ready, 1)
                at_least(dve, den_ready, 4 * i + c + 1)
                nc.vector.reciprocal(rec[:], den[:]).then_inc(rec_ready, 1)
                at_least(dve, rec_ready, 4 * i + c + 1)
                nc.vector.tensor_tensor(o_all[:, c, :], av[:, 0, :], rec[:], ALU.mult).then_inc(o_ready, 1)

            def body(i, back=True, more=True, more2=True):
                j, n = i - 1, i + 1
                probabilities(i, 0)
                if back:
                    residual(j)
                if more:
                    tokens_low(n, 0)
                probabilities(i, 1)
                if more:
                    tokens_low(n, 1)
                divide(i, 0)
                if back:
                    normalise2(j)
                if more2:
                    moments1(n + 1)
                probabilities(i, 2)
                divide(i, 1)
                if more2:
                    normalise1(n + 1)
                probabilities(i, 3)
                divide(i, 2)
                if more:
                    make_bound(n)
                divide(i, 3)

            staged = [probs[:, n, :, :, :].rearrange("p t h s -> p (t h s)").rearrange("p (c d) -> p c d", c=C)
                      for n in range(2)]

            def weight_low(n):
                w = (wk, wq, wv, wo)[n]
                dve.wait_ge(w_high, n + 1)
                nc.vector.tensor_tensor(w[:, 1, :, :], staged[n % 2], w[:, 0, :, :].bitcast(F32),
                                        ALU.subtract).then_inc(w_low, 1)

            weight_low(0)
            moments1(0)
            normalise1(0)
            weight_low(1)
            weight_low(2)
            tokens_low(0, 0)
            tokens_low(0, 1)
            weight_low(3)
            moments1(1)
            normalise1(1)
            dve.wait_ge(mask_loaded, 16)
            dve.wait_ge(consts_loaded, 16 * 2)
            make_bound(0)
            dve.wait_ge(w_low, 4)
            body(0, back=False)
            body(1)
            with dve.Fori(2, B - 2) as i:
                body(i)
            body(B - 2, more2=False)
            body(B - 1, more=False, more2=False)
            residual(B - 1)
            normalise2(B - 1)


class SharedExpertSteps:
    pass


def shared_expert(nc, T, ctx, w, name, first, count):
    _, P_, C, S = T["xn2_t"].shape
    D, ST = C * P, S // P
    assert count % 2 == 0 and SHARED_PARTS * T["w_high"].shape[2] == 3 * C * D

    def sb(part, shape, dt=F32):
        return ctx.enter_context(nc.sbuf_tensor(f"{name}_{part}", shape, dt))

    def sem(part):
        return ctx.enter_context(nc.semaphore(f"{name}_{part}"))

    x = sb("tokens", [P, C, S])
    x_t = sb("tokens_split", [P, 2, 2, C, S], F32R)
    silu_g = sb("silu", [P, 2, 2, S])
    h_t = sb("hidden", [P, 2, C, S], F32R)
    total = sb("base", [P, ST, D])
    up_ps = ctx.enter_context(nc.psum_tensor(f"{name}_up_ps", [P, 2, 2, 2, S], F32))
    down_ps = ctx.enter_context(nc.psum_tensor(f"{name}_down_ps", [P, ST, D], F32))

    x_loaded, base_loaded, base_stored = (sem(n) for n in ("x_loaded", "base_loaded", "base_stored"))
    up_done, down_done, x_high, x_low, silu_ready, hidden, h_high, h_low, summed = (
        sem(n) for n in ("up_done", "down_done", "x_high", "x_low", "silu_ready", "hidden_ready", "h_high", "h_low",
                         "summed"))
    base = T["base"].rearrange("b (t p) d -> b p t d", p=P)

    def load_tokens(queue, n):
        at_least(queue, x_low, n)
        queue.dma_start(x[:], T["xn2_t"][first + n]).then_inc(x_loaded, 16)

    def load_base(queue, n):
        at_least(queue, base_stored, 16 * n)
        queue.dma_start(total[:], base[first + n]).then_inc(base_loaded, 16)

    def first_loads(queue):
        load_tokens(queue, 0)
        load_base(queue, 0)

    def transfers(queue, step):
        n, quarter = step // 4, step % 4
        if step == 0:
            load_tokens(queue, 1)
        if quarter == 1 and n + 2 < count:
            load_tokens(queue, n + 2)
        done = n - 1 if quarter == 1 else n if step == 4 * count - 1 else -1
        if done >= 0:
            queue.wait_ge(summed, ST * (done + 1))
            queue.dma_start(base[first + done], total[:]).then_inc(base_stored, 16)
            if done + 1 < count:
                load_base(queue, done + 1)

    def up(pe, n, buffer, half):
        for which in range(2):
            if which == 0:
                at_least(pe, x_low, n + 1)
                at_least(pe, silu_ready, 2 * (n - 1) + half + 1)
            else:
                at_least(pe, hidden, 2 * (n - 1) + half + 1)
            for cc in range(2):
                channels = slice((2 * half + cc) * P, (2 * half + cc + 1) * P)
                last = split_products(nc, up_ps[:, half, which, cc, :],
                                      [(w[:, 0, which, c, channels], w[:, 1, which, c, channels],
                                        x_t[:, buffer, 0, c, :], x_t[:, buffer, 1, c, :]) for c in range(C)])
            last.then_inc(up_done, 1)

    def down(pe, n):
        at_least(pe, h_low, 2 * (n + 1))
        at_least(pe, summed, ST * n)
        for t in range(ST):
            tile = slice(t * P, (t + 1) * P)
            split_products(nc, down_ps[:, t, :], [(h_t[:, 0, c, tile], h_t[:, 1, c, tile], w[:, 0, 2, c, :], w[:, 1, 2, c, :])
                                                  for c in range(C)]).then_inc(down_done, 1)

    def tensor_start(pe):
        up(pe, 0, 0, 0)
        up(pe, 0, 0, 1)
        up(pe, 1, 1, 0)
        down(pe, 0)

    def tensor_rest(pe):
        up(pe, 1, 1, 1)
        if count > 2:
            with pe.Fori(1, count // 2) as pair:
                for s in range(2):
                    up(pe, 2 * pair + s, s, 0)
                    down(pe, 2 * pair + s - 1)
                    up(pe, 2 * pair + s, s, 1)
        down(pe, count - 1)

    def tokens_high(act, n, buffer):
        at_least(act, x_loaded, 16 * (n + 1))
        at_least(act, up_done, 4 * (n - 1))
        nc.scalar.copy(x_t[:, buffer, 0, :, :], x[:]).then_inc(x_high, 1)

    def silu(act, n, half):
        at_least(act, up_done, 4 * n + 2 * half + 1)
        at_least(act, h_low, 2 * (n - 1) + half + 1)
        nc.scalar.activation(silu_g[:, half, :, :], up_ps[:, half, 0, :, :], ACT.Silu).then_inc(silu_ready, 1)

    def hidden_high(act, n, half):
        at_least(act, hidden, 2 * n + half + 1)
        at_least(act, down_done, ST * n)
        nc.scalar.copy(h_t[:, 0, 2 * half:2 * half + 2, :], silu_g[:, half, :, :]).then_inc(h_high, 1)

    def scalar(act):
        def step(n, buffer, more=True):
            silu(act, n, 0)
            hidden_high(act, n, 0)
            silu(act, n, 1)
            if more:
                tokens_high(act, n + 1, 1 - buffer)
            hidden_high(act, n, 1)

        tokens_high(act, 0, 0)
        step(0, 0)
        if count > 2:
            step(1, 1)
            if count > 4:
                with act.Fori(1, count // 2 - 1) as pair:
                    step(2 * pair, 0)
                    step(2 * pair + 1, 1)
            step(count - 2, 0)
        step(count - 1, 1, more=False)

    def tokens_low(dve, n):
        at_least(dve, x_high, n + 1)
        nc.vector.tensor_tensor(x_t[:, n % 2, 1, :, :], x[:], x_t[:, n % 2, 0, :, :].bitcast(F32),
                                ALU.subtract).then_inc(x_low, 1)

    def hide(dve, n, half):
        at_least(dve, silu_ready, 2 * n + half + 1)
        at_least(dve, up_done, 4 * n + 2 * half + 2)
        nc.vector.tensor_tensor(silu_g[:, half, :, :], up_ps[:, half, 1, :, :], silu_g[:, half, :, :],
                                ALU.mult).then_inc(hidden, 1)

    def hidden_low(dve, n, half):
        at_least(dve, h_high, 2 * n + half + 1)
        nc.vector.tensor_tensor(h_t[:, 1, 2 * half:2 * half + 2, :], silu_g[:, half, :, :],
                                h_t[:, 0, 2 * half:2 * half + 2, :].bitcast(F32), ALU.subtract).then_inc(h_low, 1)

    def add_base(dve, n):
        at_least(dve, base_loaded, 16 * (n + 1))
        for t in range(ST):
            at_least(dve, down_done, ST * n + t + 1)
            nc.vector.tensor_tensor(total[:, t, :], down_ps[:, t, :], total[:, t, :], ALU.add).then_inc(summed, 1)

    def vector_step(dve, step):
        n, quarter = step // 4, step % 4
        if step == 0:
            tokens_low(dve, 0)
        if quarter == 0:
            hide(dve, n, 0)
        elif quarter == 1:
            if n + 1 < count:
                tokens_low(dve, n + 1)
            if n:
                add_base(dve, n - 1)
        elif quarter == 2:
            hidden_low(dve, n, 0)
            hide(dve, n, 1)
        else:
            hidden_low(dve, n, 1)
            if n + 1 == count:
                add_base(dve, n)

    steps = SharedExpertSteps()
    steps.count, steps.vector_steps, steps.base_stored = count, 4 * count, base_stored
    steps.first_loads, steps.transfers = first_loads, transfers
    steps.tensor_start, steps.tensor_rest, steps.scalar, steps.vector_step = tensor_start, tensor_rest, scalar, vector_step
    return steps


def stage_route(nc, T, keep, plan, shared_w, batches):
    NT, BLOCKS, E = keep["tiles"], keep["blocks"], HEADS
    sorted_rows = T["sorted_x"]
    with ExitStack() as ctx:
        def sb(name, shape, dt=F32):
            return ctx.enter_context(nc.sbuf_tensor(name, shape, dt))

        def sem(name):
            return ctx.enter_context(nc.semaphore(name))

        xn2 = sb("xn2_all", [P, NT, 512])
        scores = sb("gate_scores", [P, NT, E])
        low = sb("pair_low", [P, 2, NT * GROUPS])
        high = sb("pair_high", [P, 2, NT * GROUPS])
        second = sb("second", [P, 2, NT * GROUPS])
        group = sb("group_score", [P, NT, GROUPS])
        group_beats = sb("group_beats", [P, NT, GROUPS, GROUPS])
        group_rank = sb("group_rank", [P, NT, GROUPS])
        allowed = sb("allowed", [P, NT, GROUPS])
        shut = sb("shut", [P, NT, GROUPS])
        open_scores = sb("open_scores", [P, NT, E])
        beats = sb("beats", [P, NT, E, E], BF16)
        rank = sb("expert_rank", [P, NT, E])
        chosen = sb("chosen", [P, NT, E])
        weight = sb("weight", [P, NT, E])
        weight_sum = sb("weight_sum", [P, NT])
        earlier = sb("earlier", [P, P])
        all_ones = sb("all_ones", [P, P])
        tile_counts = sb("tile_counts", [P, E, NT])
        same_expert = group_beats[:].rearrange("p t (a g) h -> p (t a g h)", a=1).rearrange("p (e t) -> p e t", e=E)
        running = sb("running", [P, E, NT])
        count = sb("count", [P, E])
        count_i = sb("count_i", [P, E], I32)
        n_blocks = sb("n_blocks", [P, E])
        ends = sb("block_ends", [P, E])
        first_row = sb("first_row", [P, E])
        place = sb("place", [P, NT, E])
        picked = sb("picked", [P, NT, E])
        chosen_place = open_scores
        place_k = sb("place_k", [P, TOP_K, NT])
        lane = sb("lane", [P, E])
        pad_place = sb("pad_place", [P, E])
        pad_over = sb("pad_over", [P, E])
        pad_index = sb("pad_index", [P, E], U32)
        zeros = sb("zero_rows", [P, 512])
        step_no = sb("block_no", [1, BLOCKS])
        passed = sb("passed", [1, BLOCKS, E], BF16)
        nonempty = sb("nonempty", [1, E])
        table_f = sb("table_f", [1, 4, BLOCKS])
        run_i = sb("run_i", [1, BLOCKS], I32)
        counts_ps = ctx.enter_context(nc.psum_tensor("counts_ps", [P, 2, NT * E], F32))
        shared = shared_expert(nc, T, ctx, shared_w, "shared", 0, batches)

        scores_ready, step, made, counted, pads_ready, places_ready = (
            sem(n) for n in ("sigmoid_ready", "dve_step", "route_consts", "counted", "pads_ready", "places_ready"))
        shared_w_loaded = sem("shared_w_loaded")
        xn2_loaded = [sem(f"xn2_loaded{part}") for part in range(XN2_LOADS)]
        chosen_ready, constants_zeroed, pads_scattered, scattered = (
            sem(n) for n in ("chosen_ready", "constants_zeroed", "pads_scattered", "scattered"))
        block = ctx.enter_context(nc.Block())

        @block.sync
        def _(sp):
            source = T["xn2"].rearrange("b (t p) d -> p (b t) d", p=P)
            shared.first_loads(sp)
            for step in range(shared.vector_steps):
                shared.transfers(sp, step)
                if step < XN2_LOADS:
                    tiles = slice(step * NT // XN2_LOADS, (step + 1) * NT // XN2_LOADS)
                    sp.dma_start(xn2[:, tiles, :], source[:, tiles, :]).then_inc(xn2_loaded[step], 16)
            sp.wait_ge(shared.base_stored, 16 * shared.count)

        @block.scalar
        def _(act):
            nc.scalar.activation(scores[:], keep["logits"][:], ACT.Sigmoid).then_inc(scores_ready, 1)
            shared.scalar(act)

        @block.gpsimd
        def _(pool):
            for part, source in enumerate((T["w_high"], T["w_low"])):
                dst = shared_w[:, part, :, :, :].rearrange("p m c d -> p (m c d)").rearrange("p (e w) -> p e w", e=SHARED_PARTS)
                for e in range(SHARED_PARTS):
                    pool.dma_start(dst[:, e, :], source[HEADS + e]).then_inc(shared_w_loaded, 16)
            nc.gpsimd.memset(all_ones[:], 1.0).then_inc(made, 1)
            nc.gpsimd.memset(earlier[:], 1.0).then_inc(constants_zeroed, 1)
            nc.gpsimd.memset(zeros[:], 0.0).then_inc(made, 1)
            nc.gpsimd.iota(lane[:], pattern=[[0, E]], base=0, channel_multiplier=1,
                           allow_small_or_imprecise_dtypes=True).then_inc(made, 1)
            nc.gpsimd.iota(step_no[:], pattern=[[1, BLOCKS]], base=0, channel_multiplier=0,
                           allow_small_or_imprecise_dtypes=True).then_inc(made, 1)
            pool.wait_ge(constants_zeroed, 1)
            nc.gpsimd.affine_select(out=earlier[:], in_=earlier[:], compare_op=ALU.is_gt, fill=0.0, base=0,
                                    pattern=[[1, P]], channel_multiplier=-1).then_inc(made, 1)
            pool.wait_ge(made, 5)
            pool.wait_ge(pads_ready, 1)
            for e in range(E):
                pool.indirect_dma_start(sorted_rows, bass.IndirectOffsetOnAxis(ap=pad_index[:, e:e + 1], axis=0),
                                        zeros[:], None, bounds_check=BLOCKS * P - 1,
                                        oob_is_err=False).then_inc(pads_scattered, 16)
            pool.wait_ge(places_ready, 1)
            for t in range(NT):
                pool.wait_ge(xn2_loaded[t * XN2_LOADS // NT], 16)
                for k in range(TOP_K):
                    pool.indirect_dma_start(sorted_rows, bass.IndirectOffsetOnAxis(ap=plan["place"][:, k, t:t + 1], axis=0),
                                            xn2[:, t, :], None, bounds_check=BLOCKS * P - 1,
                                            oob_is_err=False).then_inc(scattered, 16)
            pool.wait_ge(pads_scattered, 16 * E)
            pool.wait_ge(scattered, 16 * NT * TOP_K)

        @block.tensor
        def _(pe):
            pe.wait_ge(shared_w_loaded, 16 * 2 * SHARED_PARTS)
            shared.tensor_start(pe)
            pe.wait_ge(made, 5)
            pe.wait_ge(chosen_ready, 1)
            flat = chosen[:].rearrange("p t e -> p (t e)")
            nc.tensor.matmul(counts_ps[:, 0, :], earlier[:], flat, start=True, stop=True)
            nc.tensor.matmul(counts_ps[:, 1, :], all_ones[:], flat, start=True, stop=True).then_inc(counted, 1)
            shared.tensor_rest(pe)

        @block.vector
        def _(dve):
            steps = [0]

            def link(instruction):
                steps[0] += 1
                instruction.then_inc(step, 1)
                dve.wait_ge(step, steps[0])

            v = nc.vector
            flat4 = "p t g -> p (t g)"
            dve.wait_ge(scores_ready, 1)
            by_group = scores[:].rearrange("p t (g k) -> p (t g) k", k=GROUP_SIZE)
            for pair in range(2):
                a, b = by_group[:, :, 2 * pair], by_group[:, :, 2 * pair + 1]
                v.tensor_tensor(high[:, pair, :], a, b, ALU.max)
                link(v.tensor_tensor(low[:, pair, :], a, b, ALU.min))
            v.tensor_tensor(second[:, 0, :], high[:, 0, :], high[:, 1, :], ALU.min)
            link(v.tensor_tensor(second[:, 1, :], low[:, 0, :], low[:, 1, :], ALU.max))
            link(v.tensor_tensor(low[:, 0, :], high[:, 0, :], high[:, 1, :], ALU.max))
            link(v.tensor_tensor(second[:, 0, :], second[:, 0, :], second[:, 1, :], ALU.max))
            link(v.tensor_tensor(group[:].rearrange(flat4), low[:, 0, :], second[:, 0, :], ALU.add))

            def ranks(values, out, work, n):
                for e in range(n):
                    if e:
                        v.tensor_tensor(work[:, :, e, 0:e], values[:, :, 0:e],
                                        values[:, :, e:e + 1].to_broadcast([P, NT, e]), ALU.is_ge)
                    last = v.memset(work[:, :, e, e:e + 1], 0.0)
                    if e < n - 1:
                        last = v.tensor_tensor(work[:, :, e, e + 1:n], values[:, :, e + 1:n],
                                               values[:, :, e:e + 1].to_broadcast([P, NT, n - 1 - e]), ALU.is_gt)
                link(last)
                link(v.tensor_reduce(out, work[:], AX_X, ALU.add))

            shared_steps = [0]

            def shared_next(n):
                for _ in range(n):
                    if shared_steps[0] < shared.vector_steps:
                        shared.vector_step(dve, shared_steps[0])
                        shared_steps[0] += 1

            shared_next(1)
            ranks(group[:], group_rank[:], group_beats, GROUPS)
            link(v.tensor_scalar(allowed[:], group_rank[:], 1.5, None, ALU.is_lt))
            link(v.tensor_scalar(shut[:], allowed[:], 1.0, None, ALU.subtract))
            per_expert = [P, NT * GROUPS, GROUP_SIZE]
            open_group = open_scores[:].rearrange("p t (g k) -> p (t g) k", k=GROUP_SIZE)
            link(v.tensor_tensor(open_group, by_group, allowed[:].rearrange("p t (g o) -> p (t g) o", o=1).to_broadcast(per_expert),
                                 ALU.mult))
            link(v.tensor_tensor(open_group, open_group, shut[:].rearrange("p t (g o) -> p (t g) o", o=1).to_broadcast(per_expert),
                                 ALU.add))
            shared_next(1)
            ranks(open_scores[:], rank[:], beats, E)
            shared_next(2)
            link(v.tensor_scalar(chosen[:], rank[:], TOP_K - 0.5, None, ALU.is_lt))
            v.tensor_scalar(picked[:], rank[:], TOP_K - 0.5, None, ALU.is_lt).then_inc(chosen_ready, 1)

            link(v.tensor_tensor(weight[:], scores[:], chosen[:], ALU.mult))
            link(v.tensor_reduce(weight_sum[:], weight[:], AX_X, ALU.add))
            link(v.tensor_scalar(weight_sum[:], weight_sum[:], ROUTE_EPS, None, ALU.add))
            link(v.reciprocal(weight_sum[:], weight_sum[:]))
            link(v.tensor_tensor(weight[:], weight[:], weight_sum[:].rearrange("p (t o) -> p t o", o=1).to_broadcast([P, NT, E]),
                                 ALU.mult))

            shared_next(1)
            v.memset(same_expert[:, :, 1:NT], 1.0)
            link(v.memset(same_expert[:, :, 0:1], 0.0))
            dve.wait_ge(counted, 1)
            link(v.tensor_copy(tile_counts[:], counts_ps[:, 1, :].rearrange("p (t e) -> p e t", e=E)))
            flat_et = "p e t -> p (e t)"
            link(v.tensor_tensor_scan(running[:].rearrange(flat_et), same_expert.rearrange(flat_et),
                                      tile_counts[:].rearrange(flat_et), 0.0, ALU.mult, ALU.add))
            link(v.tensor_scalar(count[:], running[:, :, NT - 1], float(P - 1), None, ALU.add))
            link(v.tensor_tensor(running[:], running[:], tile_counts[:], ALU.subtract))
            link(v.tensor_copy(count_i[:], count[:]))
            link(v.tensor_scalar(count_i[:], count_i[:], 7, None, ALU.logical_shift_right))
            link(v.tensor_copy(n_blocks[:], count_i[:]))
            v.memset(pad_over[:], 1.0)
            link(v.tensor_scalar(count[:], count[:], float(P - 1), None, ALU.subtract))
            link(v.tensor_tensor_scan(ends[:], pad_over[:], n_blocks[:], 0.0, ALU.mult, ALU.add))
            link(v.tensor_tensor(first_row[:], ends[:], n_blocks[:], ALU.subtract))
            link(v.tensor_scalar(first_row[:], first_row[:], float(P), None, ALU.mult))

            shared_next(1)
            dve.wait_ge(made, 5)
            link(v.tensor_tensor(pad_place[:], first_row[:], count[:], ALU.add))
            link(v.tensor_tensor(pad_place[:], pad_place[:], lane[:], ALU.add))
            link(v.scalar_tensor_tensor(out=pad_over[:], in0=ends[:], scalar=float(P), in1=pad_place[:],
                                        op0=ALU.mult, op1=ALU.is_le))
            link(v.scalar_tensor_tensor(out=pad_place[:], in0=pad_over[:], scalar=FAR, in1=pad_place[:],
                                        op0=ALU.mult, op1=ALU.add))
            v.tensor_copy(pad_index[:], pad_place[:]).then_inc(pads_ready, 1)

            link(v.tensor_tensor(place[:], counts_ps[:, 0, :].rearrange("p (t e) -> p t e", e=E),
                                 running[:].rearrange("p e t -> p t e"), ALU.add))
            link(v.tensor_tensor(place[:], place[:], first_row[:].rearrange("p (o e) -> p o e", o=1).to_broadcast([P, NT, E]),
                                 ALU.add))
            for k in range(TOP_K):
                link(v.tensor_scalar(picked[:], rank[:], float(k), None, ALU.is_equal))
                v.tensor_tensor(chosen_place[:], picked[:], place[:], ALU.mult)
                link(v.tensor_tensor(picked[:], picked[:], weight[:], ALU.mult))
                v.tensor_reduce(place_k[:, k, :], chosen_place[:], AX_X, ALU.add)
                link(v.tensor_reduce(plan["weight"][:, k, :], picked[:], AX_X, ALU.add))
            v.tensor_copy(plan["place"][:], place_k[:]).then_inc(places_ready, 1)

            shared_next(4)
            link(v.tensor_tensor(passed[:], ends[0:1, :].rearrange("p (o e) -> p o e", o=1).to_broadcast([1, BLOCKS, E]),
                                 step_no[:].rearrange("p (b o) -> p b o", o=1).to_broadcast([1, BLOCKS, E]), ALU.is_le))
            v.tensor_scalar(nonempty[:], n_blocks[0:1, :], 0.5, None, ALU.is_gt)
            link(v.tensor_reduce(table_f[:, 0, :], passed[:], AX_X, ALU.add))
            link(v.tensor_tensor(passed[:], passed[:], nonempty[:].rearrange("p (o e) -> p o e", o=1).to_broadcast([1, BLOCKS, E]),
                                 ALU.mult))
            v.tensor_scalar(table_f[:, 0, :], table_f[:, 0, :], float(E - 1), None, ALU.min)
            link(v.tensor_reduce(table_f[:, 1, :], passed[:], AX_X, ALU.add))
            v.memset(table_f[:, 2, 0:1], 1.0)
            v.tensor_tensor(table_f[:, 2, 1:BLOCKS], table_f[:, 1, 1:BLOCKS], table_f[:, 1, 0:BLOCKS - 1], ALU.not_equal)
            v.tensor_scalar(nonempty[:, 0:1], ends[0:1, E - 1:E], 1.0, None, ALU.subtract)
            link(v.tensor_copy(run_i[:], table_f[:, 1, :]))
            link(v.tensor_scalar(table_f[:, 3, :], step_no[:], nonempty[:, 0:1], None, ALU.min))
            link(v.tensor_copy(plan["table"][:], table_f[:]))
            link(v.tensor_scalar(plan["table"][:, 1, :], run_i[:], WEIGHT_SLOTS - 1, None, ALU.bitwise_and))
            shared_next(shared.vector_steps)


def stage_experts(nc, T, keep, plan):
    BLOCKS = keep["blocks"]
    D, C, F = 512, 4, 256
    FC = F // P
    W = C * 2 * F + FC * D
    assert BLOCKS % 4 == 0 and WEIGHT_SLOTS == 4
    with ExitStack() as ctx:
        def sb(name, shape, dt=F32):
            return ctx.enter_context(nc.sbuf_tensor(name, shape, dt))

        def sem(name):
            return ctx.enter_context(nc.semaphore(name))

        weights = sb("expert_weights", [P, 2, WEIGHT_SLOTS * W], F32R)
        ident = sb("ident2", [P, P])
        rows = sb("rows", [P, 4, D])
        rows_t = sb("rows_t", [P, 2, 2, D], F32R)
        silu_g = sb("silu_g2", [P, 2, F])
        hidden = sb("hidden", [P, 2, F])
        hidden_t = sb("hidden_t", [P, 2, 2, F], F32R)
        result = sb("result", [P, 4, D])
        rows_ps = ctx.enter_context(nc.psum_tensor("rows_ps", [P, 2, D], F32))
        up_ps = ctx.enter_context(nc.psum_tensor("up_ps", [P, 2, 2 * F], F32))
        hid_ps = ctx.enter_context(nc.psum_tensor("hid_ps", [P, 2, 512], F32))
        down_ps = ctx.enter_context(nc.psum_tensor("down_ps", [P, 2, D], F32))

        zeroed, ident_ready = sem("zeroed2"), sem("ident_ready2")
        weights_loaded = [sem(f"weights_loaded{s}") for s in range(WEIGHT_SLOTS)]
        rows_loaded = [sem(f"rows_loaded{turn}") for turn in range(4)]
        stored = [sem(f"result_stored{turn}") for turn in range(4)]
        turned, up_ready, hidden_turned, down_ready = (
            sem(n) for n in ("rows_turned", "up_ready", "hidden_turned", "down_ready"))
        rows_high, rows_ready, silu_ready, hidden_ready, hid_high, hid_ready, result_ready = (
            sem(n) for n in ("rows_high", "rows_ready", "silu2_ready", "hidden_ready", "hid_high", "hid_ready",
                             "result_ready"))
        sorted_x = T["sorted_x"].rearrange("(b p) d -> b p d", p=P)
        sorted_y = T["sorted_y"].rearrange("(b p) d -> b p d", p=P)
        table = plan["table"]
        block = ctx.enter_context(nc.Block())

        def entry(engine, line, b, top):
            return engine.value_load(table[0:1, line, bass.ds(b, 1)], min_val=0, max_val=top)

        @block.gpsimd
        def _(pool):
            nc.gpsimd.memset(ident[:], 0.0).then_inc(zeroed, 1)
            pool.wait_ge(zeroed, 1)
            nc.gpsimd.affine_select(out=ident[:], in_=ident[:], compare_op=ALU.not_equal, fill=1.0, base=0,
                                    pattern=[[-1, P]], channel_multiplier=1).then_inc(ident_ready, 1)

            def load_weights(b, turn):
                expert = entry(pool, 0, b, HEADS - 1)
                slot = entry(pool, 1, b, WEIGHT_SLOTS - 1)
                new = entry(pool, 2, b, 1)
                at_least(pool, down_ready, b - WEIGHT_SLOTS + 1)
                for part, source in enumerate((T["w_high"], T["w_low"])):
                    src = source[bass.ds(expert, 1), :, :].rearrange("a p w -> (a p) w")
                    pool.dma_start(weights[:, part, bass.ds(slot * W, W)], src, cond=new).then_inc(weights_loaded[turn], 16)

            for b in range(4):
                load_weights(b, b)
            with pool.Fori(1, BLOCKS // 4) as four:
                for n in range(4):
                    load_weights(4 * four + n, n)

        @block.sync
        def _(sp):
            def load_rows(b, turn):
                row_block = entry(sp, 3, b, BLOCKS - 1)
                src = sorted_x[bass.ds(row_block, 1)].rearrange("a p d -> (a p) d")
                at_least(sp, turned, b - 3)
                sp.dma_start(rows[:, turn, :], src).then_inc(rows_loaded[turn], 16)

            def store(b, turn):
                dst = sorted_y[bass.ds(b, 1)].rearrange("a p d -> (a p) d") if not isinstance(b, int) else sorted_y[b]
                sp.wait_ge(result_ready, b + 1)
                sp.dma_start(dst, result[:, turn, :]).then_inc(stored[turn], 16)

            for b in range(8):
                load_rows(b, b % 4)
                if b >= STORE_LAG:
                    store(b - STORE_LAG, (b - STORE_LAG) % 4)
            with sp.Fori(2, BLOCKS // 4) as four:
                for n in range(4):
                    load_rows(4 * four + n, n)
                    store(4 * four + n - STORE_LAG, (n - STORE_LAG) % 4)
            for b in range(BLOCKS - STORE_LAG, BLOCKS):
                store(b, b % 4)
            for turn in range(4):
                sp.wait_ge(stored[turn], 16 * (BLOCKS // 4))

        @block.tensor
        def _(pe):
            def turn_rows(b, turn, nth):
                s = turn % 2
                pe.wait_ge(rows_loaded[turn], 16 * nth)
                at_least(pe, rows_ready, b - 1)
                for c in range(C):
                    last = nc.tensor.transpose(rows_ps[:, s, c * P:(c + 1) * P], rows[:, turn, c * P:(c + 1) * P], ident[:])
                last.then_inc(turned, 1)

            def up(b, turn, nth, half):
                s = turn % 2
                slot = entry(pe, 1, b, WEIGHT_SLOTS - 1)
                if half == 0:
                    pe.wait_ge(weights_loaded[turn], 32 * nth)
                    pe.wait_ge(rows_ready, b + 1)
                    at_least(pe, hidden_ready, b - 1)
                chunks = range(half * C // 2, (half + 1) * C // 2)
                last = split_products(nc, up_ps[:, s, :],
                                      [(rows_t[:, s, 0, c * P:(c + 1) * P], rows_t[:, s, 1, c * P:(c + 1) * P],
                                        weights[:, 0, bass.ds(slot * W + c * 2 * F, 2 * F)],
                                        weights[:, 1, bass.ds(slot * W + c * 2 * F, 2 * F)]) for c in chunks],
                                      first=(half == 0), last=(half == 1))
                if half == 1:
                    last.then_inc(up_ready, 1)

            def turn_hidden(b, s):
                pe.wait_ge(hidden_ready, b + 1)
                at_least(pe, hid_ready, b - 1)
                for c in range(FC):
                    last = nc.tensor.transpose(hid_ps[:, s, c * P:(c + 1) * P], hidden[:, s, c * P:(c + 1) * P], ident[:])
                last.then_inc(hidden_turned, 1)

            def down(b, s):
                slot = entry(pe, 1, b, WEIGHT_SLOTS - 1)
                pe.wait_ge(hid_ready, b + 1)
                at_least(pe, result_ready, b - 1)
                split_products(nc, down_ps[:, s, :],
                               [(hidden_t[:, s, 0, c * P:(c + 1) * P], hidden_t[:, s, 1, c * P:(c + 1) * P],
                                 weights[:, 0, bass.ds(slot * W + C * 2 * F + c * D, D)],
                                 weights[:, 1, bass.ds(slot * W + C * 2 * F + c * D, D)])
                                for c in range(FC)]).then_inc(down_ready, 1)

            pe.wait_ge(ident_ready, 1)
            turn_rows(0, 0, 1)
            turn_rows(1, 1, 1)
            up(0, 0, 1, 0)
            up(0, 0, 1, 1)

            def body(b, turn, fours, more=True):
                s = turn % 2
                if more:
                    turn_rows(b + 1, (turn + 1) % 4, fours + (turn + 1) // 4 + 1)
                up(b, turn, fours + 1, 0)
                turn_hidden(b - 1, 1 - s)
                up(b, turn, fours + 1, 1)
                down(b - 1, 1 - s)

            for b in range(1, 4):
                body(b, b, 0)
            with pe.Fori(1, BLOCKS // 4 - 1) as four:
                for turn in range(4):
                    body(4 * four + turn, turn, four)
            for turn in range(4):
                body(BLOCKS - 4 + turn, turn, BLOCKS // 4 - 1, more=(turn < 3))
            turn_hidden(BLOCKS - 1, 1)
            down(BLOCKS - 1, 1)

        @block.scalar
        def _(act):
            def rows_out(b, s):
                act.wait_ge(turned, b + 1)
                at_least(act, up_ready, b - 1)
                nc.scalar.copy(rows_t[:, s, 0, :], rows_ps[:, s, :]).then_inc(rows_high, 1)

            def hidden_out(b, s):
                act.wait_ge(hidden_turned, b + 1)
                at_least(act, down_ready, b - 1)
                nc.scalar.copy(hidden_t[:, s, 0, :], hid_ps[:, s, 0:F]).then_inc(hid_high, 1)

            def silu(b, s):
                act.wait_ge(up_ready, b + 1)
                at_least(act, hidden_ready, b - 1)
                nc.scalar.activation(silu_g[:, s, :], up_ps[:, s, 0:F], ACT.Silu).then_inc(silu_ready, 1)

            def body(b, s):
                rows_out(b + 1, 1 - s)
                hidden_out(b - 1, 1 - s)
                silu(b, s)

            rows_out(0, 0)
            rows_out(1, 1)
            silu(0, 0)
            body(1, 1)
            with act.Fori(1, BLOCKS // 2 - 1) as pair:
                body(2 * pair, 0)
                body(2 * pair + 1, 1)
            body(BLOCKS - 2, 0)
            hidden_out(BLOCKS - 2, 0)
            silu(BLOCKS - 1, 1)
            hidden_out(BLOCKS - 1, 1)

        @block.vector
        def _(dve):
            def rows_low(b, s):
                dve.wait_ge(rows_high, b + 1)
                nc.vector.tensor_tensor(rows_t[:, s, 1, :], rows_ps[:, s, :], rows_t[:, s, 0, :].bitcast(F32),
                                        ALU.subtract).then_inc(rows_ready, 1)

            def hide(b, s):
                dve.wait_ge(silu_ready, b + 1)
                at_least(dve, hidden_turned, b - 1)
                nc.vector.tensor_tensor(hidden[:, s, :], up_ps[:, s, F:2 * F], silu_g[:, s, :], ALU.mult).then_inc(hidden_ready, 1)

            def hidden_low(b, s):
                dve.wait_ge(hid_high, b + 1)
                nc.vector.tensor_tensor(hidden_t[:, s, 1, :], hid_ps[:, s, 0:F], hidden_t[:, s, 0, :].bitcast(F32),
                                        ALU.subtract).then_inc(hid_ready, 1)

            def result_out(b, turn, nth):
                dve.wait_ge(down_ready, b + 1)
                at_least(dve, stored[turn], 16 * nth)
                nc.vector.tensor_copy(result[:, turn, :], down_ps[:, turn % 2, :]).then_inc(result_ready, 1)

            def body(b, turn, fours, more=True):
                s = turn % 2
                if more:
                    rows_low(b + 1, 1 - s)
                hidden_low(b - 1, 1 - s)
                hide(b, s)
                result_out(b - 1, (turn - 1) % 4, fours if turn else fours - 1)

            rows_low(0, 0)
            rows_low(1, 1)
            hide(0, 0)
            for b in range(1, 4):
                body(b, b, 0)
            for b in range(4, 8):
                body(b, b - 4, 1)
            with dve.Fori(2, BLOCKS // 4 - 1) as four:
                for turn in range(4):
                    body(4 * four + turn, turn, four)
            for turn in range(4):
                body(BLOCKS - 4 + turn, turn, BLOCKS // 4 - 1, more=(turn < 3))
            hidden_low(BLOCKS - 1, 1)
            result_out(BLOCKS - 1, 3, BLOCKS // 4 - 1)


def stage_combine(nc, T, keep, plan, shared_w, batches):
    NT = keep["tiles"]
    D = 512
    with ExitStack() as ctx:
        def sb(name, shape, dt=F32):
            return ctx.enter_context(nc.sbuf_tensor(name, shape, dt))

        def sem(name):
            return ctx.enter_context(nc.semaphore(name))

        DEPTH = 4
        picked = sb("picked_rows", [P, DEPTH, TOP_K, D])
        total = sb("total", [P, DEPTH, D])
        gathered = [sem(f"gathered{s}") for s in range(DEPTH)]
        base_loaded = [sem(f"base_loaded{s}") for s in range(DEPTH)]
        out_stored = [sem(f"out_stored{s}") for s in range(DEPTH)]
        added = sem("added")
        B, S, _ = T["x"].shape
        first = B - batches
        shared = shared_expert(nc, T, ctx, shared_w, "shared_last", first, batches)
        shared_tiles = NT - 6

        def shared_steps(t):
            return range(min(t, shared_tiles) * shared.vector_steps // shared_tiles,
                         min(t + 1, shared_tiles) * shared.vector_steps // shared_tiles)

        base = T["base"].rearrange("b (t p) d -> (b t) p d", p=P)
        out = T["out"].rearrange("b (t p) d -> (b t) p d", p=P)
        block = ctx.enter_context(nc.Block())

        @block.gpsimd
        def _(pool):
            for t in range(NT):
                s = t % DEPTH
                at_least(pool, added, TOP_K * (t - DEPTH + 1))
                for k in range(TOP_K):
                    pool.indirect_dma_start(picked[:, s, k, :], None, T["sorted_y"],
                                            bass.IndirectOffsetOnAxis(ap=plan["place"][:, k, t:t + 1], axis=0),
                                            bounds_check=keep["blocks"] * P - 1,
                                            oob_is_err=False).then_inc(gathered[s], 16)

        @block.sync
        def _(sp):
            def load_base(t):
                at_least(sp, out_stored[t % DEPTH], 16 * (t // DEPTH))
                at_least(sp, shared.base_stored, 16 * (t // (S // P) - first + 1))
                sp.dma_start(total[:, t % DEPTH, :], base[t]).then_inc(base_loaded[t % DEPTH], 16)

            shared.first_loads(sp)
            for t in range(DEPTH):
                load_base(t)
            for t in range(NT):
                for step in shared_steps(t):
                    shared.transfers(sp, step)
                sp.wait_ge(added, TOP_K * (t + 1))
                sp.dma_start(out[t], total[:, t % DEPTH, :]).then_inc(out_stored[t % DEPTH], 16)
                if t + DEPTH < NT:
                    load_base(t + DEPTH)
            for s in range(DEPTH):
                sp.wait_ge(out_stored[s], 16 * (NT // DEPTH))

        @block.tensor
        def _(pe):
            shared.tensor_start(pe)
            shared.tensor_rest(pe)

        @block.scalar
        def _(act):
            shared.scalar(act)

        @block.vector
        def _(dve):
            for t in range(NT):
                s = t % DEPTH
                for step in shared_steps(t):
                    shared.vector_step(dve, step)
                dve.wait_ge(gathered[s], 16 * TOP_K * (t // DEPTH + 1))
                dve.wait_ge(base_loaded[s], 16 * (t // DEPTH + 1))
                for k in range(TOP_K):
                    at_least(dve, added, TOP_K * t + k)
                    nc.vector.scalar_tensor_tensor(out=total[:, s, :], in0=picked[:, s, k, :],
                                                   scalar=plan["weight"][:, k, t:t + 1], in1=total[:, s, :],
                                                   op0=ALU.mult, op1=ALU.add).then_inc(added, 1)


def program(nc, T):
    B, S, D = T["x"].shape
    NT = B * S // P
    BLOCKS = NT * TOP_K + HEADS
    last = 2 * (3 * B // 16)
    T = dict(T)
    T["xn2"] = nc.dram_tensor("xn2_rows", [B, S, D], F32).ap()
    T["xn2_t"] = nc.dram_tensor("xn2_columns", [B, P, D // P, S], F32).ap()
    T["w_high"] = nc.dram_tensor("weights_high", T["w_experts"].shape, F32R).ap()
    T["w_low"] = nc.dram_tensor("weights_low", T["w_experts"].shape, F32R).ap()
    T["base"] = nc.dram_tensor("base_rows", [B, S, D], F32).ap()
    T["sorted_x"] = nc.dram_tensor("sorted_x", [BLOCKS * P, D], F32).ap()
    T["sorted_y"] = nc.dram_tensor("sorted_y", [BLOCKS * P, D], F32).ap()
    with (
        nc.sbuf_tensor("place_of", [P, TOP_K, NT], U32) as place,
        nc.sbuf_tensor("weight_of", [P, TOP_K, NT], F32) as weight,
        nc.sbuf_tensor("block_table", [1, 4, BLOCKS], I32) as table,
    ):
        plan = {"place": place, "weight": weight, "table": table}
        keep = {"tiles": NT, "blocks": BLOCKS}
        with nc.sbuf_tensor("logits_all", [P, NT, HEADS], F32) as logits, ExitStack() as ctx:
            keep["logits"] = logits
            stage_attend(nc, T, keep)
            shared_w = ctx.enter_context(nc.sbuf_tensor("shared_weights", [P, 2, 3, D // P, D], F32R))
            stage_route(nc, T, keep, plan, shared_w, B - last)
            stage_experts(nc, T, keep, plan)
            stage_combine(nc, T, keep, plan, shared_w, last)


def lay_out(inputs):
    x = np.ascontiguousarray(inputs["x"])
    B, S, D = x.shape

    def by_chunk(w):
        w = np.asarray(w)
        w = np.swapaxes(w, -1, -2)
        w = w.reshape(*w.shape[:-2], w.shape[-2] // P, P, w.shape[-1])
        return np.ascontiguousarray(np.swapaxes(w, -3, -2))

    wkv = np.asarray(inputs["L0_xattn_Wkv"])
    w1, w3, w2 = (np.asarray(inputs[f"L0_ffn_w{n}_e"]) for n in (1, 3, 2))
    E = w1.shape[0]
    up = by_chunk(np.concatenate([w1, w3], axis=1)).reshape(E, P, -1)
    down = by_chunk(w2).reshape(E, P, -1)
    shared = np.concatenate([by_chunk(inputs[f"L0_ffn_w{n}_s"]).reshape(P, -1) for n in (1, 3, 2)], axis=1)
    shared = shared.reshape(P, SHARED_PARTS, -1).swapaxes(0, 1)
    return {
        "x": x,
        "ctx_t": by_chunk(inputs["ctx_1024"]),
        "mask_t": by_chunk(inputs["mask_BxSxS2_bk0"]),
        "wq": by_chunk(inputs["L0_xattn_Wq"]),
        "wk": by_chunk(wkv[:D]),
        "wv": by_chunk(wkv[D:]),
        "wo": by_chunk(inputs["L0_xattn_Wo"]),
        "nbias": np.ascontiguousarray(inputs["L0_xattn_nbias"]),
        "wg": by_chunk(inputs["L0_ffn_w_gate"]),
        "w_experts": np.ascontiguousarray(np.concatenate([np.concatenate([up, down], axis=2), shared])),
    }


def kernel(**inputs):
    import concourse.bacc as bacc
    from concourse.bass_utils import run_bass_kernel_spmd

    arrays = {f"in_{name}": a for name, a in lay_out(inputs).items()}
    nc = bacc.Bacc("TRN2", target_bir_lowering=False, num_devices=1)
    T = {name[3:]: nc.dram_tensor(name, a.shape, mybir.dt.from_np(a.dtype), kind="ExternalInput").ap()
         for name, a in arrays.items()}
    T["out"] = nc.dram_tensor("out_rows", inputs["x"].shape, F32, kind="ExternalOutput").ap()
    program(nc, T)
    result = run_bass_kernel_spmd(nc, [arrays], core_ids=[0])
    return result.results[0]["out_rows"]
```

```python
from contextlib import ExitStack

import numpy as np

import concourse.bass as bass
from concourse import mybir

ALU = mybir.AluOpType
ACT = mybir.ActivationFunctionType
F32 = mybir.dt.float32
F32R = mybir.dt.float32r
BF16 = mybir.dt.bfloat16
I32 = mybir.dt.int32
U32 = mybir.dt.uint32
U8 = mybir.dt.uint8
AX_X = mybir.AxisListType.X

P = 128
HEADS = 16
HEAD_DIM = 32
LN_EPS = 1e-5
NORM_EPS = 1e-32
ROUTE_EPS = 1e-6
GROUPS = 4
GROUP_SIZE = 4
TOP_K = 4
WEIGHT_SLOTS = 4
ROUTE_CONSTS = 7
SHARED_PARTS = 2


def at_least(engine, semaphore, value):
    if not isinstance(value, int) or value > 0:
        engine.wait_ge(semaphore, value)


def split_products(nc, out, pairs, first=True, last=True):
    instruction = None
    for n, (lh, ll, rh, rl) in enumerate(pairs):
        for k, (left, right) in enumerate(((lh, rh), (lh, rl), (ll, rh))):
            instruction = nc.tensor.matmul(out, left, right, start=(first and n == 0 and k == 0),
                                           stop=(last and n == len(pairs) - 1 and k == 2))
    return instruction


def stage_attend(nc, T, keep):
    B, S, D = T["x"].shape
    C = D // P
    ST = S // P
    assert (D, S, HEADS * HEAD_DIM) == (512, 256, 512) and B >= 4
    JOBS, _, W = T["w_experts"].shape
    HALF = W // 2
    assert JOBS == HEADS + SHARED_PARTS
    scale = float(HEAD_DIM) ** -0.5

    with ExitStack() as ctx:
        def sb(name, shape, dt=F32):
            return ctx.enter_context(nc.sbuf_tensor(name, shape, dt))

        def sem(name):
            return ctx.enter_context(nc.semaphore(name))

        wk, wq, wv, wo = (sb(n, [P, 2, C, D], F32R) for n in ("wk", "wq", "wv", "wo"))
        wg = sb("wg", [P, C, 16])
        ident = sb("ident", [P, P])
        ones = sb("ones", [P, HEAD_DIM])
        minus_half = sb("minus_half", [P, ST])
        nbias = sb("nbias_all", [P, 1])
        x_in = sb("x_in", [P, ST, D])
        x_res = sb("x_res", [P, ST, D])
        ctx_in = sb("ctx_in", [P, C, S])
        ctx_t = sb("ctx_t", [P, 2, C, S], F32R)
        mask = sb("mask_t", [P, ST, S], U8)
        bound = sb("bound", [P, ST, S])
        stats = sb("stats", [P, 2, ST, 6])
        mean_var = sb("mean_var", [P, 2, ST, 2])
        var_eps = sb("var_eps", [P, 2, ST])
        rstd = sb("rstd", [P, 2, ST])
        spacer = sb("spacer", [P, 2])
        eps = sb("eps", [P, ST])
        xn = sb("xn", [P, ST, D])
        xn_t = sb("xn_t", [P, 2, C, S], F32R)
        q_diag = sb("q_diag", [P, 2, C, 4, S], F32R)
        k_t = sb("k_t", [P, 2, C, S], F32R)
        v_nat = sb("v_nat", [P, ST, D])
        probs = sb("probs", [P, 2, ST, 4, S])
        den = sb("den", [P, S])
        rec = sb("rec", [P, S])
        o_all = sb("o_all", [P, 2, S])
        o_t = sb("o_t", [P, 2, C, S], F32R)
        x1 = sb("x1", [P, ST, D])
        xn2 = sb("xn2", [P, ST, D])
        xn2_t = sb("xn2_t", [P, C, S])
        part = sb("expert_part", [P, HALF])
        part_high = sb("expert_part_high", [P, HALF], F32R)
        part_low = sb("expert_part_low", [P, HALF], F32R)

        psum = ctx.enter_context(nc.psum_tensor("attend_banks", [P, 3, 512], F32))
        sc = ctx.enter_context(nc.psum_tensor("attend_scores", [P, ST, 4 * S], F32))
        av = ctx.enter_context(nc.psum_tensor("attend_av", [P, 2, S], F32))

        w_loaded = [sem(f"w_loaded{n}") for n in range(4)]
        consts_loaded = sem("consts_loaded")
        x_loaded, ctx_loaded, mask_loaded, res_loaded, part_loaded = (
            sem(n) for n in ("x_loaded", "ctx_loaded", "mask_loaded", "res_loaded", "part_loaded"))
        xn2_kept, base_stored, xn2t_stored, part_stored = (
            sem(n) for n in ("xn2_kept", "base_stored", "xn2t_stored", "part_stored"))
        zeroed, ident_ready, q_zeroed, consts_made = (
            sem(n) for n in ("zeroed", "ident_ready", "q_zeroed", "consts_made"))
        xn_turned, q_done, k_done, v_done, o_done, xn2_turned, gate_done, scores_ready, av_ready = (
            sem(n) for n in ("xn_turned", "q_done", "k_done", "v_done", "o_done", "xn2_turned", "gate_done",
                             "scores_ready", "av_ready"))
        w_high, ctx_high, xn_high, q_high, k_high, v_ready, xn2t_ready, gate_ready, o_high, part_high_ready = (
            sem(n) for n in ("w_high", "ctx_high", "xn_high", "q_high", "k_high", "v_ready", "xn2t_ready",
                             "gate_ready", "o_high", "part_high_ready"))
        positive, probs_ready = sem("positive"), sem("probs_ready")
        w_low, xn_low, stats1, var1, xn_ready, stats2, var2, xn2_ready, x1_ready, bound_ready = (
            sem(n) for n in ("w_low", "xn_low", "stats1", "var1", "xn_ready", "stats2", "var2", "xn2_ready",
                             "x1_ready", "bound_ready"))
        q_ready, k_ready, masked, den_ready, rec_ready, o_ready = (
            sem(n) for n in ("q_ready", "k_ready", "masked", "den_ready", "rec_ready", "o_ready"))
        eps1, rstd1, eps2, rstd2, ctx_low, o_low, part_low_ready = (
            sem(n) for n in ("eps1", "rstd1", "eps2", "rstd2", "ctx_low", "o_low",
                             "part_low_ready"))

        tokens = T["x"].rearrange("b (t p) d -> b p t d", p=P)
        base_dram = T["base"].rearrange("b (t p) d -> b p t d", p=P)
        xn2_dram = T["xn2"].rearrange("b (t p) d -> b p t d", p=P)
        parts = T["w_experts"].rearrange("e p (h w) -> e h p w", h=2)
        parts_high = T["w_high"].bitcast(F32).rearrange("e p (h w) -> e h p w", h=2)
        parts_low = T["w_low"].bitcast(F32).rearrange("e p (h w) -> e h p w", h=2)

        def halves(i):
            own = [(i, 0), (i, 1)]
            if isinstance(i, int) and i < 2:
                return own + [(HEADS, i)]
            if isinstance(i, int) and B - 2 <= i < B:
                return own + [(HEADS + 1, i - (B - 2))]
            return own

        def nth_half(i):
            if isinstance(i, int) and i < 2:
                return 3 * i
            return 2 * i + 2 + (min(i - (B - 2), 2) if isinstance(i, int) and i >= B - 2 else 0)

        def pick(ap, i, *more):
            if isinstance(i, int):
                return ap[(i, *more)]
            axes = {3: "a p s -> (a p) s", 4: "a p t s -> (a p) t s"}
            ap = ap[(bass.ds(i, 1), *more)]
            return ap.rearrange(axes[len(ap.shape)])

        block = ctx.enter_context(nc.Block())

        @block.sync
        def _(sp):
            def load(dst, src, free, count, loaded):
                at_least(sp, free, count)
                sp.dma_start(dst, src).then_inc(loaded, 16)

            def load_part(e, h, nth):
                load(part[:], pick(parts, e, h), part_low_ready, nth, part_loaded)

            def store_part(e, h, nth):
                at_least(sp, part_high_ready, nth + 1)
                sp.dma_start(pick(parts_high, e, h), part_high[:].bitcast(F32)).then_inc(part_stored, 16)
                at_least(sp, part_low_ready, nth + 1)
                sp.dma_start(pick(parts_low, e, h), part_low[:].bitcast(F32)).then_inc(part_stored, 16)

            def store(dst, src, ready, count, stored):
                at_least(sp, ready, count)
                sp.dma_start(dst, src).then_inc(stored, 16)

            def back_stores(j, i):
                store(pick(base_dram, j), x1[:], x1_ready, ST * (j + 1), base_stored)
                if i is not None:
                    load(x_res[:], pick(tokens, i), x1_ready, ST * i, res_loaded)
                store(pick(xn2_dram, j), xn2[:], xn2_ready, ST * (j + 1), xn2_kept)
                store(pick(T["xn2_t"], j), xn2_t[:], xn2t_ready, ST * (j + 1), xn2t_stored)

            staged = [probs[:, n, :, :, :].rearrange("p t h s -> p (t h s)").rearrange("p (c d) -> p c d", c=C)
                      for n in range(2)]
            load(ctx_in[:], pick(T["ctx_t"], 0), ctx_low, 0, ctx_loaded)
            load(staged[0], T["wk"], w_low, 0, w_loaded[0])
            load(x_in[:], pick(tokens, 0), xn_ready, 0, x_loaded)
            load(staged[1], T["wq"], w_low, 0, w_loaded[1])
            sp.dma_start(wg[:], T["wg"]).then_inc(consts_loaded, 16)
            sp.dma_start(nbias[:], T["nbias"].rearrange("(a b) -> a b", a=1).to_broadcast([P, 1])).then_inc(consts_loaded, 16)
            load(staged[0], T["wv"], w_low, 1, w_loaded[2])
            load(staged[1], T["wo"], w_low, 2, w_loaded[3])
            load(mask[:], pick(T["mask_t"], 0), bound_ready, 0, mask_loaded)
            load(x_in[:], pick(tokens, 1), xn_ready, ST, x_loaded)
            load(ctx_in[:], pick(T["ctx_t"], 1), ctx_low, 1, ctx_loaded)
            load(x_res[:], pick(tokens, 0), x1_ready, 0, res_loaded)
            load_part(0, 0, 0)

            def body(i, back=True, ahead2=True, more=True):
                split = [(*half, nth_half(i) + n) for n, half in enumerate(halves(i))]
                if ahead2:
                    load(x_in[:], pick(tokens, i + 2), xn_ready, ST * (i + 2), x_loaded)
                    load(ctx_in[:], pick(T["ctx_t"], i + 2), ctx_low, i + 2, ctx_loaded)
                store_part(*split[0])
                load_part(*split[1])
                if back:
                    back_stores(i - 1, i)
                else:
                    at_least(sp, bound_ready, ST)
                if more:
                    sp.dma_start(mask[:], pick(T["mask_t"], i + 1)).then_inc(mask_loaded, 16)
                store_part(*split[1])
                for half in split[2:]:
                    load_part(*half)
                    store_part(*half)
                if more:
                    load_part(i + 1, 0, split[-1][2] + 1)

            body(0, back=False)
            body(1)
            with sp.Fori(2, B - 2) as i:
                body(i)
            body(B - 2, ahead2=False)
            body(B - 1, ahead2=False, more=False)
            back_stores(B - 1, None)
            for e in range(B, HEADS):
                for h in range(2):
                    load_part(e, h, nth_half(e) + h)
                    store_part(e, h, nth_half(e) + h)
            sp.wait_ge(xn2_kept, 16 * B)
            sp.wait_ge(base_stored, 16 * B)
            sp.wait_ge(xn2t_stored, 16 * B)
            sp.wait_ge(part_stored, 64 * JOBS)

        @block.gpsimd
        def _(pool):
            nc.gpsimd.memset(ident[:], 0.0).then_inc(zeroed, 1)
            nc.gpsimd.memset(minus_half[:], -0.5).then_inc(consts_made, 1)
            nc.gpsimd.memset(ones[:], 1.0).then_inc(consts_made, 1)
            nc.gpsimd.memset(eps[:], LN_EPS).then_inc(consts_made, 1)
            pool.wait_ge(zeroed, 1)
            nc.gpsimd.affine_select(out=ident[:], in_=ident[:], compare_op=ALU.not_equal, fill=1.0, base=0,
                                    pattern=[[-1, P]], channel_multiplier=1).then_inc(ident_ready, 1)
            nc.gpsimd.memset(q_diag[:].bitcast(F32), 0.0).then_inc(q_zeroed, 1)
            pool.wait_ge(consts_made, 3)

            def inverse_std(which, n, var, eps_ready, done):
                at_least(pool, var, ST * (n + 1))
                nc.gpsimd.tensor_tensor(var_eps[:, which, :], mean_var[:, which, :, 1], eps[:],
                                        ALU.add).then_inc(eps_ready, 1)
                at_least(pool, eps_ready, n + 1)
                nc.gpsimd.tensor_tensor(rstd[:, which, :], var_eps[:, which, :], minus_half[:], ALU.pow).then_inc(done, 1)

            def context_low(n):
                at_least(pool, ctx_high, n + 1)
                nc.gpsimd.tensor_tensor(ctx_t[:, 1, :, :], ctx_in[:], ctx_t[:, 0, :, :].bitcast(F32),
                                        ALU.subtract).then_inc(ctx_low, 1)

            def expert_low(nth):
                at_least(pool, part_high_ready, nth + 1)
                at_least(pool, part_stored, 32 * nth)
                nc.gpsimd.tensor_tensor(part_low[:], part[:], part_high[:].bitcast(F32),
                                        ALU.subtract).then_inc(part_low_ready, 1)

            def output_low(i, c):
                at_least(pool, o_high, 4 * i + c + 1)
                nc.gpsimd.tensor_tensor(o_t[:, 1, c, :], o_all[:, c % 2, :], o_t[:, 0, c, :].bitcast(F32),
                                        ALU.subtract).then_inc(o_low, 1)

            def body(i, back=True, next1=True, next2=True):
                if next1:
                    context_low(i + 1)
                expert_low(nth_half(i))
                if back:
                    inverse_std(1, i - 1, var2, eps2, rstd2)
                output_low(i, 0)
                output_low(i, 1)
                if next2:
                    inverse_std(0, i + 2, var1, eps1, rstd1)
                expert_low(nth_half(i) + 1)
                output_low(i, 2)
                output_low(i, 3)
                for n in range(2, len(halves(i))):
                    expert_low(nth_half(i) + n)

            context_low(0)
            inverse_std(0, 0, var1, eps1, rstd1)
            inverse_std(0, 1, var1, eps1, rstd1)
            body(0, back=False)
            body(1)
            with pool.Fori(2, B - 2) as i:
                body(i)
            body(B - 2, next2=False)
            body(B - 1, next1=False, next2=False)
            inverse_std(1, B - 1, var2, eps2, rstd2)
            for nth in range(nth_half(B), nth_half(HEADS)):
                expert_low(nth)

        @block.tensor
        def _(pe):
            def transposes(n, t):
                at_least(pe, xn_ready, ST * n + t + 1)
                at_least(pe, v_ready, ST * (n - 1) + t + 1)
                if t == 1:
                    at_least(pe, x1_ready, ST * (n - 2) + 1)
                bank = 2 - 2 * t
                for c in range(C):
                    last = nc.tensor.transpose(psum[:, bank, c * P:(c + 1) * P], xn[:, t, c * P:(c + 1) * P], ident[:])
                last.then_inc(xn_turned, 1)

            def project(out, w, source, u):
                for cc in range(2):
                    channels = slice((2 * u + cc) * P, (2 * u + cc + 1) * P)
                    last = split_products(nc, out[:, cc * S:(cc + 1) * S],
                                          [(w[:, 0, c, channels], w[:, 1, c, channels], source[:, 0, c, :], source[:, 1, c, :])
                                           for c in range(C)])
                return last

            def q_unit(n, u):
                at_least(pe, w_low, 2)
                at_least(pe, xn_low, ST * (n + 1))
                if u == 1:
                    at_least(pe, xn2t_ready, ST * (n - 2) + 1)
                project(psum[:, (2, 0)[u], :], wq, xn_t, u).then_inc(q_done, 1)

            def k_unit(n, u):
                at_least(pe, w_low, 1)
                at_least(pe, ctx_low, n + 1)
                if u == 0:
                    at_least(pe, k_ready, 2 * n)
                    at_least(pe, x1_ready, ST * (n - 1))
                else:
                    at_least(pe, k_ready, 2 * n + 1)
                    at_least(pe, xn2t_ready, ST * (n - 1))
                project(psum[:, 1, :], wk, ctx_t, u).then_inc(k_done, 1)

            def v_unit(n, t):
                at_least(pe, w_low, 3)
                if t == 0:
                    at_least(pe, q_ready, 2 * n + 1)
                    at_least(pe, gate_ready, n - 1)
                else:
                    at_least(pe, q_ready, 2 * n + 2)
                tile = slice(t * P, (t + 1) * P)
                split_products(nc, psum[:, 2 - 2 * t, :],
                               [(ctx_t[:, 0, c, tile], ctx_t[:, 1, c, tile], wv[:, 0, c, :], wv[:, 1, c, :])
                                for c in range(C)]).then_inc(v_done, 1)

            def scores(i, c):
                at_least(pe, q_ready, 2 * i + c // 2 + 1)
                at_least(pe, k_ready, 2 * i + c // 2 + 1)
                for st in range(ST):
                    at_least(pe, positive, 8 * i + 2 * (c - 1) + st + 1)
                    for half in range(2):
                        tile, heads = slice(st * P, (st + 1) * P), slice(2 * half, 2 * half + 2)
                        last = split_products(nc, sc[:, st, half * 512:(half + 1) * 512],
                                              [(k_t[:, 0, c, tile], k_t[:, 1, c, tile],
                                                q_diag[:, 0, c, heads, :], q_diag[:, 1, c, heads, :])])
                    last.then_inc(scores_ready, 1)

            def attend(i, c):
                at_least(pe, probs_ready, 8 * i + 2 * c + 2)
                at_least(pe, v_ready, ST * (i + 1))
                at_least(pe, o_ready, 4 * i + c)
                for what in range(2):
                    for st in range(ST):
                        for j in range(4):
                            h = 4 * c + j
                            left = ones[:] if what else v_nat[:, st, h * HEAD_DIM:(h + 1) * HEAD_DIM]
                            last = nc.tensor.matmul(av[32 * j:32 * j + 32, what, :], left, probs[:, c % 2, st, j, :],
                                                    start=(st == 0), stop=(st == ST - 1), tile_position=(0, 32 * j),
                                                    skip_group_check=True)
                last.then_inc(av_ready, 1)

            def o_unit(j, t):
                at_least(pe, o_low, 4 * (j + 1))
                at_least(pe, xn2t_ready, ST * j)
                if t == 0:
                    if isinstance(j, int) and j == B - 1:
                        at_least(pe, v_ready, ST * B)
                    else:
                        at_least(pe, v_ready, ST * (j + 2))
                    bank = 0
                else:
                    if isinstance(j, int) and j == B - 1:
                        at_least(pe, k_ready, 2 * B)
                    else:
                        at_least(pe, k_ready, 2 * (j + 2))
                    bank = 1
                tile = slice(t * P, (t + 1) * P)
                split_products(nc, psum[:, bank, :],
                               [(o_t[:, 0, c, tile], o_t[:, 1, c, tile], wo[:, 0, c, :], wo[:, 1, c, :])
                                for c in range(C)]).then_inc(o_done, 1)

            def xn2t_unit(j, t, more):
                at_least(pe, xn2_ready, ST * j + t + 1)
                if more:
                    if t == 0:
                        at_least(pe, xn_low, ST * (j + 3))
                    else:
                        at_least(pe, k_ready, 2 * (j + 2) + 1)
                for c in range(C):
                    last = nc.tensor.transpose(psum[:, t, c * P:(c + 1) * P], xn2[:, t, c * P:(c + 1) * P], ident[:])
                last.then_inc(xn2_turned, 1)

            def gate_unit(j, more):
                at_least(pe, xn2t_ready, ST * (j + 1))
                if more:
                    at_least(pe, q_ready, 2 * (j + 2) + 1)
                at_least(pe, gate_ready, j)
                for t in range(ST):
                    for c in range(C):
                        last = nc.tensor.matmul(psum[:, 2, 16 * t:16 * t + 16], xn2_t[:, c, t * P:(t + 1) * P], wg[:, c, :],
                                                start=(c == 0), stop=(c == C - 1))
                last.then_inc(gate_done, 1)

            def body(i, back=True, more=True):
                j, n = i - 1, i + 1
                scores(i, 0)
                if back:
                    o_unit(j, 0)
                    o_unit(j, 1)
                if more:
                    transposes(n, 0)
                scores(i, 1)
                if more:
                    transposes(n, 1)
                    k_unit(n, 0)
                attend(i, 0)
                if more:
                    q_unit(n, 0)
                scores(i, 2)
                if back:
                    xn2t_unit(j, 0, more)
                    xn2t_unit(j, 1, more)
                attend(i, 1)
                if back:
                    gate_unit(j, more)
                scores(i, 3)
                if more:
                    q_unit(n, 1)
                attend(i, 2)
                if more:
                    k_unit(n, 1)
                attend(i, 3)
                if more:
                    v_unit(n, 0)
                    v_unit(n, 1)

            pe.wait_ge(ident_ready, 1)
            k_unit(0, 0)
            k_unit(0, 1)
            transposes(0, 0)
            transposes(0, 1)
            q_unit(0, 0)
            q_unit(0, 1)
            v_unit(0, 0)
            v_unit(0, 1)
            pe.wait_ge(consts_loaded, 16 * 2)
            pe.wait_ge(consts_made, 3)
            pe.wait_ge(q_zeroed, 1)
            pe.wait_ge(w_low, 4)
            body(0, back=False)
            body(1)
            with pe.Fori(2, B - 1) as i:
                body(i)
            body(B - 1, more=False)
            j = B - 1
            o_unit(j, 0)
            o_unit(j, 1)
            xn2t_unit(j, 0, False)
            xn2t_unit(j, 1, False)
            gate_unit(j, False)

        @block.scalar
        def _(act):
            copy = nc.scalar.copy

            def context_high(n):
                at_least(act, ctx_loaded, 16 * (n + 1))
                at_least(act, v_done, ST * n)
                copy(ctx_t[:, 0, :, :], ctx_in[:]).then_inc(ctx_high, 1)

            def tokens_high(n, t):
                at_least(act, xn_turned, ST * n + t + 1)
                at_least(act, q_done, 2 * n)
                copy(xn_t[:, 0, :, t * P:(t + 1) * P],
                     psum[:, 2 - 2 * t, :].rearrange("p (c s) -> p c s", c=C)).then_inc(xn_high, 1)

            def queries_high(n, u):
                at_least(act, q_done, 2 * n + u + 1)
                at_least(act, scores_ready, 8 * (n - 1) + 4 * (u + 1))
                for h in range(4):
                    part = slice(32 * h, 32 * h + 32)
                    last = copy(q_diag[part, 0, 2 * u:2 * u + 2, h, :],
                                psum[part, (2, 0)[u], :].rearrange("p (c s) -> p c s", c=2))
                last.then_inc(q_high, 1)

            def keys_high(n, u):
                at_least(act, k_done, 2 * n + u + 1)
                at_least(act, scores_ready, 8 * (n - 1) + 4 * (u + 1))
                copy(k_t[:, 0, 2 * u:2 * u + 2, :], psum[:, 1, :].rearrange("p (c s) -> p c s", c=2)).then_inc(k_high, 1)

            def relu(i, c):
                at_least(act, av_ready, 4 * i + c - 1)
                for st in range(ST):
                    at_least(act, scores_ready, 8 * i + 2 * c + st + 1)
                    nc.scalar.activation(probs[:, c % 2, st, :, :].rearrange("p h s -> p (h s)"), sc[:, st, :], ACT.Relu,
                                         bias=nbias[:, 0:1], scale=scale).then_inc(positive, 1)

            def square(i, c):
                for st in range(ST):
                    at_least(act, masked, 8 * i + 2 * c + st + 1)
                    x = probs[:, c % 2, st, :, :].rearrange("p h s -> p (h s)")
                    nc.scalar.activation(x, x, ACT.Square).then_inc(probs_ready, 1)

            def v_out(n, t):
                at_least(act, v_done, ST * n + t + 1)
                at_least(act, av_ready, 4 * n)
                copy(v_nat[:, t, :], psum[:, 2 - 2 * t, :]).then_inc(v_ready, 1)

            def xn2t_out(j, t):
                at_least(act, xn2_turned, ST * j + t + 1)
                at_least(act, xn2t_stored, 16 * j)
                at_least(act, gate_done, j)
                copy(xn2_t[:, :, t * P:(t + 1) * P], psum[:, t, :].rearrange("p (c s) -> p c s", c=C)).then_inc(xn2t_ready, 1)

            def gate_out(j):
                at_least(act, gate_done, j + 1)
                copy(keep["logits"][:, bass.ds(j * ST, ST), :],
                     psum[:, 2, 0:16 * ST].rearrange("p (t e) -> p t e", t=ST)).then_inc(gate_ready, 1)

            def output_high(i, c):
                at_least(act, o_ready, 4 * i + c + 1)
                if c == 0:
                    at_least(act, o_done, ST * i)
                copy(o_t[:, 0, c, :], o_all[:, c % 2, :]).then_inc(o_high, 1)

            def expert_high(nth):
                at_least(act, part_loaded, 16 * (nth + 1))
                at_least(act, part_stored, 32 * nth)
                copy(part_high[:], part[:]).then_inc(part_high_ready, 1)

            def body(i, back=True, more=True):
                j, n = i - 1, i + 1
                relu(i, 0)
                if more:
                    context_high(n)
                square(i, 0)
                expert_high(nth_half(i))
                if more:
                    tokens_high(n, 0)
                relu(i, 1)
                if more:
                    tokens_high(n, 1)
                square(i, 1)
                if more:
                    keys_high(n, 0)
                    queries_high(n, 0)
                output_high(i, 0)
                relu(i, 2)
                if back:
                    xn2t_out(j, 0)
                    xn2t_out(j, 1)
                square(i, 2)
                output_high(i, 1)
                if back:
                    gate_out(j)
                relu(i, 3)
                expert_high(nth_half(i) + 1)
                square(i, 3)
                if more:
                    queries_high(n, 1)
                output_high(i, 2)
                if more:
                    keys_high(n, 1)
                    v_out(n, 0)
                output_high(i, 3)
                if more:
                    v_out(n, 1)
                for n in range(2, len(halves(i))):
                    expert_high(nth_half(i) + n)

            staged = [probs[:, n, :, :, :].rearrange("p t h s -> p (t h s)").rearrange("p (c d) -> p c d", c=C)
                      for n in range(2)]

            def weight_high(n):
                act.wait_ge(w_loaded[n], 16)
                copy((wk, wq, wv, wo)[n][:, 0, :, :], staged[n % 2]).then_inc(w_high, 1)

            context_high(0)
            weight_high(0)
            weight_high(1)
            keys_high(0, 0)
            keys_high(0, 1)
            weight_high(2)
            tokens_high(0, 0)
            tokens_high(0, 1)
            act.wait_ge(q_zeroed, 1)
            queries_high(0, 0)
            weight_high(3)
            queries_high(0, 1)
            v_out(0, 0)
            v_out(0, 1)
            act.wait_ge(consts_loaded, 16 * 2)
            act.wait_ge(w_low, 4)
            body(0, back=False)
            body(1)
            with act.Fori(2, B - 2) as i:
                body(i)
            body(B - 2)
            body(B - 1, more=False)
            xn2t_out(B - 1, 0)
            xn2t_out(B - 1, 1)
            gate_out(B - 1)
            for nth in range(nth_half(B), nth_half(HEADS)):
                expert_high(nth)

        @block.vector
        def _(dve):
            def moments(src, which, n, stats_done, var_done):
                for t in range(ST):
                    nc.vector.bn_stats(stats[:, which, t, :], src[:, t, :]).then_inc(stats_done, 1)
                at_least(dve, stats_done, ST * (n + 1))
                nc.vector.memset(spacer[:, which:which + 1], 0.0)
                for t in range(ST):
                    nc.vector.bn_aggr(mean_var[:, which, t, :], stats[:, which, t, :]).then_inc(var_done, 1)

            def normalise(dst, src, which, n, rstd_done, done):
                at_least(dve, rstd_done, n + 1)
                for t in range(ST):
                    nc.vector.tensor_scalar(dst[:, t, :], src[:, t, :], mean_var[:, which, t, 0:1], rstd[:, which, t:t + 1],
                                            ALU.subtract, ALU.mult).then_inc(done, 1)

            def moments1(n):
                at_least(dve, rstd1, n)
                at_least(dve, x_loaded, 16 * (n + 1))
                moments(x_in, 0, n, stats1, var1)

            def normalise1(n):
                at_least(dve, xn_turned, ST * n)
                normalise(xn, x_in, 0, n, rstd1, xn_ready)

            def tokens_low(n, t):
                at_least(dve, xn_high, ST * n + t + 1)
                tile = slice(t * P, (t + 1) * P)
                nc.vector.tensor_tensor(xn_t[:, 1, :, tile], psum[:, 2 - 2 * t, :].rearrange("p (c s) -> p c s", c=C),
                                        xn_t[:, 0, :, tile].bitcast(F32), ALU.subtract).then_inc(xn_low, 1)

            def residual(j):
                at_least(dve, res_loaded, 16 * (j + 1))
                at_least(dve, base_stored, 16 * j)
                for t in range(ST):
                    at_least(dve, o_done, ST * j + t + 1)
                    nc.vector.tensor_tensor(x1[:, t, :], psum[:, t, :], x_res[:, t, :], ALU.add).then_inc(x1_ready, 1)
                at_least(dve, x1_ready, ST * (j + 1))
                moments(x1, 1, j, stats2, var2)

            def normalise2(j):
                at_least(dve, xn2_kept, 16 * j)
                normalise(xn2, x1, 1, j, rstd2, xn2_ready)

            def make_bound(i):
                at_least(dve, mask_loaded, 16 * (i + 1))
                at_least(dve, masked, 8 * i)
                big = float(np.finfo(np.float32).max)
                for t in range(ST):
                    nc.vector.tensor_scalar(bound[:, t, :], mask[:, t, :], -big, big, ALU.mult, ALU.add).then_inc(bound_ready, 1)

            def queries_low(n, u):
                at_least(dve, q_high, 2 * n + u + 1)
                for h in range(4):
                    part = slice(32 * h, 32 * h + 32)
                    last = nc.vector.tensor_tensor(q_diag[part, 1, 2 * u:2 * u + 2, h, :],
                                                   psum[part, (2, 0)[u], :].rearrange("p (c s) -> p c s", c=2),
                                                   q_diag[part, 0, 2 * u:2 * u + 2, h, :].bitcast(F32), ALU.subtract)
                last.then_inc(q_ready, 1)

            def keys_low(n, u):
                at_least(dve, k_high, 2 * n + u + 1)
                nc.vector.tensor_tensor(k_t[:, 1, 2 * u:2 * u + 2, :], psum[:, 1, :].rearrange("p (c s) -> p c s", c=2),
                                        k_t[:, 0, 2 * u:2 * u + 2, :].bitcast(F32), ALU.subtract).then_inc(k_ready, 1)

            def apply_mask(i, c):
                at_least(dve, bound_ready, ST * (i + 1))
                for st in range(ST):
                    at_least(dve, positive, 8 * i + 2 * c + st + 1)
                    x = probs[:, c % 2, st, :, :]
                    nc.vector.tensor_tensor(x, x, bound[:, st:st + 1, :].to_broadcast([P, 4, S]), ALU.min).then_inc(masked, 1)

            def divide(i, c):
                at_least(dve, av_ready, 4 * i + c + 1)
                nc.vector.tensor_scalar(den[:], av[:, 1, :], NORM_EPS, None, ALU.add).then_inc(den_ready, 1)
                at_least(dve, den_ready, 4 * i + c + 1)
                nc.vector.reciprocal(rec[:], den[:]).then_inc(rec_ready, 1)
                at_least(dve, rec_ready, 4 * i + c + 1)
                at_least(dve, o_low, 4 * i + c - 1)
                nc.vector.tensor_tensor(o_all[:, c % 2, :], av[:, 0, :], rec[:], ALU.mult).then_inc(o_ready, 1)

            def body(i, back=True, more=True, more2=True):
                j, n = i - 1, i + 1
                apply_mask(i, 0)
                if back:
                    residual(j)
                if more:
                    tokens_low(n, 0)
                apply_mask(i, 1)
                if more:
                    tokens_low(n, 1)
                    keys_low(n, 0)
                if back:
                    normalise2(j)
                divide(i, 0)
                if more:
                    queries_low(n, 0)
                if more2:
                    moments1(n + 1)
                apply_mask(i, 2)
                divide(i, 1)
                if more2:
                    normalise1(n + 1)
                apply_mask(i, 3)
                divide(i, 2)
                if more:
                    queries_low(n, 1)
                    keys_low(n, 1)
                    make_bound(n)
                divide(i, 3)

            staged = [probs[:, n, :, :, :].rearrange("p t h s -> p (t h s)").rearrange("p (c d) -> p c d", c=C)
                      for n in range(2)]

            def weight_low(n):
                w = (wk, wq, wv, wo)[n]
                dve.wait_ge(w_high, n + 1)
                nc.vector.tensor_tensor(w[:, 1, :, :], staged[n % 2], w[:, 0, :, :].bitcast(F32),
                                        ALU.subtract).then_inc(w_low, 1)

            weight_low(0)
            moments1(0)
            normalise1(0)
            weight_low(1)
            keys_low(0, 0)
            keys_low(0, 1)
            weight_low(2)
            tokens_low(0, 0)
            tokens_low(0, 1)
            queries_low(0, 0)
            weight_low(3)
            queries_low(0, 1)
            moments1(1)
            normalise1(1)
            make_bound(0)
            body(0, back=False)
            body(1)
            with dve.Fori(2, B - 2) as i:
                body(i)
            body(B - 2, more2=False)
            body(B - 1, more=False, more2=False)
            residual(B - 1)
            normalise2(B - 1)


class SharedExpertSteps:
    pass


def shared_expert(nc, T, ctx, w, name, first, count, store_sums):
    _, P_, C, S = T["xn2_t"].shape
    D, ST = C * P, S // P
    assert count % 2 == 0 and SHARED_PARTS * T["w_high"].shape[2] == 3 * C * D

    def sb(part, shape, dt=F32):
        return ctx.enter_context(nc.sbuf_tensor(f"{name}_{part}", shape, dt))

    def sem(part):
        return ctx.enter_context(nc.semaphore(f"{name}_{part}"))

    x = sb("tokens", [P, C, S])
    x_t = sb("tokens_split", [P, 2, 2, C, S], F32R)
    silu_g = sb("silu", [P, 2, 2, S])
    h_t = sb("hidden", [P, 2, C, S], F32R)
    total = sb("base", [P, 1 if store_sums else count, ST, D])
    up_ps = ctx.enter_context(nc.psum_tensor(f"{name}_up_ps", [P, 2, 2, 2, S], F32))
    down_ps = ctx.enter_context(nc.psum_tensor(f"{name}_down_ps", [P, ST, D], F32))

    x_loaded, base_loaded, base_stored = (sem(n) for n in ("x_loaded", "base_loaded", "base_stored"))
    up_done, down_done, x_high, x_low, silu_ready, hidden, h_high, h_low, summed = (
        sem(n) for n in ("up_done", "down_done", "x_high", "x_low", "silu_ready", "hidden_ready", "h_high", "h_low",
                         "summed"))
    base = T["base"].rearrange("b (t p) d -> b p t d", p=P)

    def sums(n):
        return total[:, 0 if store_sums else n, :, :]

    def load_tokens(queue, n):
        at_least(queue, x_low, n)
        queue.dma_start(x[:], T["xn2_t"][first + n]).then_inc(x_loaded, 16)

    def load_base(queue, n):
        if store_sums:
            at_least(queue, base_stored, 16 * n)
        queue.dma_start(sums(n), base[first + n]).then_inc(base_loaded, 16)

    def first_loads(queue):
        load_tokens(queue, 0)
        load_base(queue, 0)

    def transfers(queue, step):
        n, quarter = step // 4, step % 4
        if step == 0:
            load_tokens(queue, 1)
        if quarter == 1 and n + 2 < count:
            load_tokens(queue, n + 2)
        done = n - 1 if quarter == 1 else n if step == 4 * count - 1 else -1
        if done >= 0:
            queue.wait_ge(summed, ST * (done + 1))
            if store_sums:
                queue.dma_start(base[first + done], sums(done)).then_inc(base_stored, 16)
            if done + 1 < count:
                load_base(queue, done + 1)

    def up(pe, n, buffer, half):
        for which in range(2):
            if which == 0:
                at_least(pe, x_low, n + 1)
                at_least(pe, silu_ready, 2 * (n - 1) + half + 1)
            else:
                at_least(pe, hidden, 2 * (n - 1) + half + 1)
            for cc in range(2):
                channels = slice((2 * half + cc) * P, (2 * half + cc + 1) * P)
                last = split_products(nc, up_ps[:, half, which, cc, :],
                                      [(w[:, 0, which, c, channels], w[:, 1, which, c, channels],
                                        x_t[:, buffer, 0, c, :], x_t[:, buffer, 1, c, :]) for c in range(C)])
            last.then_inc(up_done, 1)

    def down(pe, n):
        at_least(pe, h_low, 2 * (n + 1))
        at_least(pe, summed, ST * n)
        for t in range(ST):
            tile = slice(t * P, (t + 1) * P)
            split_products(nc, down_ps[:, t, :], [(h_t[:, 0, c, tile], h_t[:, 1, c, tile], w[:, 0, 2, c, :], w[:, 1, 2, c, :])
                                                  for c in range(C)]).then_inc(down_done, 1)

    def tensor_step(pe, n, buffer):
        up(pe, n, buffer, 0)
        if not (isinstance(n, int) and n == 0):
            down(pe, n - 1)
        up(pe, n, buffer, 1)

    def tensor_end(pe):
        down(pe, count - 1)

    def tokens_high(act, n, buffer):
        at_least(act, x_loaded, 16 * (n + 1))
        at_least(act, up_done, 4 * (n - 1))
        nc.scalar.copy(x_t[:, buffer, 0, :, :], x[:]).then_inc(x_high, 1)

    def silu(act, n, half):
        at_least(act, up_done, 4 * n + 2 * half + 1)
        at_least(act, h_low, 2 * (n - 1) + half + 1)
        nc.scalar.activation(silu_g[:, half, :, :], up_ps[:, half, 0, :, :], ACT.Silu).then_inc(silu_ready, 1)

    def hidden_high(act, n, half):
        at_least(act, hidden, 2 * n + half + 1)
        at_least(act, down_done, ST * n)
        nc.scalar.copy(h_t[:, 0, 2 * half:2 * half + 2, :], silu_g[:, half, :, :]).then_inc(h_high, 1)

    def scalar(act):
        def step(n, buffer, more=True):
            if more:
                tokens_high(act, n + 1, 1 - buffer)
            for half in range(2):
                silu(act, n, half)
                hidden_high(act, n, half)

        tokens_high(act, 0, 0)
        step(0, 0)
        if count > 2:
            step(1, 1)
            if count > 4:
                with act.Fori(1, count // 2 - 1) as pair:
                    step(2 * pair, 0)
                    step(2 * pair + 1, 1)
            step(count - 2, 0)
        step(count - 1, 1, more=False)

    def tokens_low(dve, n):
        at_least(dve, x_high, n + 1)
        nc.vector.tensor_tensor(x_t[:, n % 2, 1, :, :], x[:], x_t[:, n % 2, 0, :, :].bitcast(F32),
                                ALU.subtract).then_inc(x_low, 1)

    def hide(dve, n, half):
        at_least(dve, silu_ready, 2 * n + half + 1)
        at_least(dve, up_done, 4 * n + 2 * half + 2)
        nc.vector.tensor_tensor(silu_g[:, half, :, :], up_ps[:, half, 1, :, :], silu_g[:, half, :, :],
                                ALU.mult).then_inc(hidden, 1)

    def hidden_low(dve, n, half):
        at_least(dve, h_high, 2 * n + half + 1)
        nc.vector.tensor_tensor(h_t[:, 1, 2 * half:2 * half + 2, :], silu_g[:, half, :, :],
                                h_t[:, 0, 2 * half:2 * half + 2, :].bitcast(F32), ALU.subtract).then_inc(h_low, 1)

    def add_base(dve, n):
        at_least(dve, base_loaded, 16 * (n + 1))
        for t in range(ST):
            at_least(dve, down_done, ST * n + t + 1)
            nc.vector.tensor_tensor(sums(n)[:, t, :], down_ps[:, t, :], sums(n)[:, t, :], ALU.add).then_inc(summed, 1)

    def vector_start(dve):
        tokens_low(dve, 0)

    def vector_step(dve, step):
        n, quarter = step // 4, step % 4
        if quarter == 0:
            hide(dve, n, 0)
        elif quarter == 1:
            if n + 1 < count:
                tokens_low(dve, n + 1)
            if n:
                add_base(dve, n - 1)
        elif quarter == 2:
            hidden_low(dve, n, 0)
            hide(dve, n, 1)
        else:
            hidden_low(dve, n, 1)
            if n + 1 == count:
                add_base(dve, n)

    steps = SharedExpertSteps()
    steps.count, steps.vector_steps, steps.base_stored = count, 4 * count, base_stored
    steps.summed, steps.total, steps.vector_start = summed, total, vector_start
    steps.first_loads, steps.transfers = first_loads, transfers
    steps.tensor_step, steps.tensor_end, steps.scalar, steps.vector_step = tensor_step, tensor_end, scalar, vector_step
    return steps


def stage_route(nc, T, keep, plan, shared_w, batches):
    NT, BLOCKS, E = keep["tiles"], keep["blocks"], HEADS
    PAIRS = NT * TOP_K
    GROUPS_OF_SETS = batches - 3
    assert GROUPS_OF_SETS > 0
    group_ends = [PAIRS * (g + 1) // GROUPS_OF_SETS for g in range(GROUPS_OF_SETS)]
    RING = 2 * max(end - start for start, end in zip([0] + group_ends, group_ends))
    with ExitStack() as ctx:
        def sb(name, shape, dt=F32):
            return ctx.enter_context(nc.sbuf_tensor(name, shape, dt))

        def sem(name):
            return ctx.enter_context(nc.semaphore(name))

        scores = sb("gate_scores", [P, NT, E])
        low = sb("pair_low", [P, 2, NT * GROUPS])
        high = sb("pair_high", [P, 2, NT * GROUPS])
        second = sb("second", [P, 2, NT * GROUPS])
        group = sb("group_score", [P, NT, GROUPS])
        group_beats = sb("group_beats", [P, NT, GROUPS, GROUPS])
        group_rank = sb("group_rank", [P, NT, GROUPS])
        allowed = sb("allowed", [P, NT, GROUPS])
        shut = sb("shut", [P, NT, GROUPS])
        open_scores = sb("open_scores", [P, NT, E])
        beats = sb("beats", [P, NT, E, E], BF16)
        rank = sb("expert_rank", [P, NT, E])
        chosen = sb("chosen", [P, NT, E])
        weight = sb("weight", [P, NT, E])
        weight_sum = sb("weight_sum", [P, NT])
        earlier = sb("earlier", [P, P])
        all_ones = sb("all_ones", [P, P])
        tile_counts = sb("tile_counts", [P, E, NT])
        same_expert = group_beats[:].rearrange("p t (a g) h -> p (t a g h)", a=1).rearrange("p (e t) -> p e t", e=E)
        running = sb("running", [P, E, NT])
        count = sb("count", [P, E])
        count_i = sb("count_i", [P, E], I32)
        n_blocks = sb("n_blocks", [P, E])
        ends = sb("block_ends", [P, E])
        first_row = sb("first_row", [P, E])
        place = sb("place", [P, NT, E])
        picked = sb("picked", [P, NT, E])
        chosen_place = open_scores
        place_k = sb("place_k", [P, TOP_K, NT])
        all_one = sb("all_one", [P, E])
        place_part = sb("place_part", [P, TOP_K, NT], I32)
        lane_of = sb("lane_of", [P, TOP_K, NT])
        block_of = sb("block_of", [P, TOP_K, NT])
        lanes = sb("lanes", [P, P])
        blocks = sb("blocks", [P, BLOCKS])
        token_parts = sb("token_parts", [P, NT, 2])
        lane_hot = sb("lane_hot", [P, RING, P], BF16)
        block_hot = sb("block_hot", [P, RING, 2, BLOCKS], BF16)
        token_high = sb("token_high", [P, BLOCKS])
        token_of = sb("token_of", [P, BLOCKS])
        step_no = sb("block_no", [1, BLOCKS])
        passed = sb("passed", [1, BLOCKS, E], BF16)
        nonempty = sb("nonempty", [1, E])
        table_f = sb("table_f", [1, 4, BLOCKS])
        number = sb("number", [1, E])
        run_i = sb("run_i", [1, BLOCKS], I32)
        counts_ps = ctx.enter_context(nc.psum_tensor("counts_ps", [P, 2, NT * E], F32))
        tokens_ps = counts_ps
        shared = shared_expert(nc, T, ctx, shared_w, "shared", 0, batches, store_sums=True)

        scores_ready, step, made, counted, places_ready, places_split, lane_hot_ready, block_hot_ready, pairs_summed = (
            sem(n) for n in ("sigmoid_ready", "dve_step", "route_consts", "counted", "places_ready", "places_split",
                             "lane_hot_ready", "block_hot_ready", "pairs_summed"))
        shared_w_loaded = sem("shared_w_loaded")
        chosen_ready, constants_zeroed = sem("chosen_ready"), sem("constants_zeroed")
        block = ctx.enter_context(nc.Block())

        @block.sync
        def _(sp):
            shared.first_loads(sp)
            for step in range(shared.vector_steps):
                shared.transfers(sp, step)
            sp.wait_ge(shared.base_stored, 16 * shared.count)

        @block.scalar
        def _(act):
            nc.scalar.activation(scores[:], keep["logits"][:], ACT.Sigmoid).then_inc(scores_ready, 1)
            shared.scalar(act)

        @block.gpsimd
        def _(pool):
            for part, source in enumerate((T["w_high"], T["w_low"])):
                dst = shared_w[:, part, :, :, :].rearrange("p m c d -> p (m c d)").rearrange("p (e w) -> p e w", e=SHARED_PARTS)
                for e in range(SHARED_PARTS):
                    pool.dma_start(dst[:, e, :], source[HEADS + e]).then_inc(shared_w_loaded, 16)
            nc.gpsimd.memset(all_ones[:], 1.0).then_inc(made, 1)
            nc.gpsimd.memset(earlier[:], 1.0).then_inc(constants_zeroed, 1)
            for out, pattern, lane_step in ((lanes[:], [[1, P]], 0), (blocks[:], [[1, BLOCKS]], 0),
                                            (token_parts[:, :, 0], [[1, NT]], 0), (token_parts[:, :, 1], [[0, NT]], 1)):
                nc.gpsimd.iota(out, pattern=pattern, base=0, channel_multiplier=lane_step,
                               allow_small_or_imprecise_dtypes=True).then_inc(made, 1)
            nc.gpsimd.iota(step_no[:], pattern=[[1, BLOCKS]], base=0, channel_multiplier=0,
                           allow_small_or_imprecise_dtypes=True).then_inc(made, 1)
            pool.wait_ge(constants_zeroed, 1)
            nc.gpsimd.affine_select(out=earlier[:], in_=earlier[:], compare_op=ALU.is_gt, fill=0.0, base=0,
                                    pattern=[[1, P]], channel_multiplier=-1).then_inc(made, 1)
            pool.wait_ge(made, ROUTE_CONSTS)
            pool.wait_ge(places_split, 1)
            for n in range(PAIRS):
                at_least(pool, pairs_summed, n - RING + 1)
                nc.gpsimd.tensor_scalar(lane_hot[:, n % RING, :], lanes[:], lane_of[:, n // NT, n % NT:n % NT + 1], None,
                                        ALU.is_equal).then_inc(lane_hot_ready, 1)

        @block.tensor
        def _(pe):
            pe.wait_ge(shared_w_loaded, 16 * 2 * SHARED_PARTS)
            shared.tensor_step(pe, 0, 0)
            pe.wait_ge(made, ROUTE_CONSTS)
            pe.wait_ge(chosen_ready, 1)
            flat = chosen[:].rearrange("p t e -> p (t e)")
            nc.tensor.matmul(counts_ps[:, 0, :], earlier[:], flat, start=True, stop=True)
            nc.tensor.matmul(counts_ps[:, 1, :], all_ones[:], flat, start=True, stop=True).then_inc(counted, 1)
            shared.tensor_step(pe, 1, 1)
            shared.tensor_step(pe, 2, 0)
            pe.wait_ge(places_ready, 1)
            for g in range(GROUPS_OF_SETS):
                for n in range(([0] + group_ends)[g], group_ends[g]):
                    pe.wait_ge(lane_hot_ready, n + 1)
                    pe.wait_ge(block_hot_ready, n + 1)
                    nc.tensor.matmul(tokens_ps[:, 0, 0:2 * BLOCKS], lane_hot[:, n % RING, :],
                                     block_hot[:, n % RING, :, :].rearrange("p h b -> p (h b)"),
                                     start=(n == 0), stop=(n == PAIRS - 1)).then_inc(pairs_summed, 1)
                shared.tensor_step(pe, g + 3, (g + 3) % 2)
            shared.tensor_end(pe)

        @block.vector
        def _(dve):
            steps = [0]

            def link(instruction):
                steps[0] += 1
                instruction.then_inc(step, 1)
                dve.wait_ge(step, steps[0])

            v = nc.vector
            flat4 = "p t g -> p (t g)"
            shared.vector_start(dve)
            dve.wait_ge(scores_ready, 1)
            by_group = scores[:].rearrange("p t (g k) -> p (t g) k", k=GROUP_SIZE)
            for pair in range(2):
                a, b = by_group[:, :, 2 * pair], by_group[:, :, 2 * pair + 1]
                v.tensor_tensor(high[:, pair, :], a, b, ALU.max)
                link(v.tensor_tensor(low[:, pair, :], a, b, ALU.min))
            v.tensor_tensor(second[:, 0, :], high[:, 0, :], high[:, 1, :], ALU.min)
            link(v.tensor_tensor(second[:, 1, :], low[:, 0, :], low[:, 1, :], ALU.max))
            link(v.tensor_tensor(low[:, 0, :], high[:, 0, :], high[:, 1, :], ALU.max))
            link(v.tensor_tensor(second[:, 0, :], second[:, 0, :], second[:, 1, :], ALU.max))
            link(v.tensor_tensor(group[:].rearrange(flat4), low[:, 0, :], second[:, 0, :], ALU.add))

            def ranks(values, out, work, n):
                for e in range(n):
                    if e:
                        v.tensor_tensor(work[:, :, e, 0:e], values[:, :, 0:e],
                                        values[:, :, e:e + 1].to_broadcast([P, NT, e]), ALU.is_ge)
                    last = v.memset(work[:, :, e, e:e + 1], 0.0)
                    if e < n - 1:
                        last = v.tensor_tensor(work[:, :, e, e + 1:n], values[:, :, e + 1:n],
                                               values[:, :, e:e + 1].to_broadcast([P, NT, n - 1 - e]), ALU.is_gt)
                link(last)
                link(v.tensor_reduce(out, work[:], AX_X, ALU.add))

            ranks(group[:], group_rank[:], group_beats, GROUPS)
            link(v.tensor_scalar(allowed[:], group_rank[:], 1.5, None, ALU.is_lt))
            link(v.tensor_scalar(shut[:], allowed[:], 1.0, None, ALU.subtract))
            per_expert = [P, NT * GROUPS, GROUP_SIZE]
            open_group = open_scores[:].rearrange("p t (g k) -> p (t g) k", k=GROUP_SIZE)
            link(v.tensor_tensor(open_group, by_group, allowed[:].rearrange("p t (g o) -> p (t g) o", o=1).to_broadcast(per_expert),
                                 ALU.mult))
            link(v.tensor_tensor(open_group, open_group, shut[:].rearrange("p t (g o) -> p (t g) o", o=1).to_broadcast(per_expert),
                                 ALU.add))
            ranks(open_scores[:], rank[:], beats, E)
            link(v.tensor_scalar(chosen[:], rank[:], TOP_K - 0.5, None, ALU.is_lt))
            v.tensor_scalar(picked[:], rank[:], TOP_K - 0.5, None, ALU.is_lt).then_inc(chosen_ready, 1)

            for quarter in range(4):
                shared.vector_step(dve, quarter)

            link(v.tensor_tensor(weight[:], scores[:], chosen[:], ALU.mult))
            link(v.tensor_reduce(weight_sum[:], weight[:], AX_X, ALU.add))
            link(v.tensor_scalar(weight_sum[:], weight_sum[:], ROUTE_EPS, None, ALU.add))
            link(v.reciprocal(weight_sum[:], weight_sum[:]))
            link(v.tensor_tensor(weight[:], weight[:], weight_sum[:].rearrange("p (t o) -> p t o", o=1).to_broadcast([P, NT, E]),
                                 ALU.mult))

            v.memset(same_expert[:, :, 1:NT], 1.0)
            link(v.memset(same_expert[:, :, 0:1], 0.0))
            dve.wait_ge(counted, 1)
            link(v.tensor_copy(tile_counts[:], counts_ps[:, 1, :].rearrange("p (t e) -> p e t", e=E)))
            flat_et = "p e t -> p (e t)"
            link(v.tensor_tensor_scan(running[:].rearrange(flat_et), same_expert.rearrange(flat_et),
                                      tile_counts[:].rearrange(flat_et), 0.0, ALU.mult, ALU.add))
            link(v.tensor_scalar(count[:], running[:, :, NT - 1], float(P - 1), None, ALU.add))
            link(v.tensor_tensor(running[:], running[:], tile_counts[:], ALU.subtract))
            link(v.tensor_copy(count_i[:], count[:]))
            link(v.tensor_scalar(count_i[:], count_i[:], 7, None, ALU.logical_shift_right))
            link(v.tensor_copy(n_blocks[:], count_i[:]))
            v.memset(all_one[:], 1.0)
            link(v.tensor_scalar(count[:], count[:], float(P - 1), None, ALU.subtract))
            link(v.tensor_tensor_scan(ends[:], all_one[:], n_blocks[:], 0.0, ALU.mult, ALU.add))
            link(v.tensor_tensor(first_row[:], ends[:], n_blocks[:], ALU.subtract))
            link(v.tensor_scalar(first_row[:], first_row[:], float(P), None, ALU.mult))

            shared.vector_step(dve, 4)
            shared.vector_step(dve, 5)

            link(v.tensor_tensor(place[:], counts_ps[:, 0, :].rearrange("p (t e) -> p t e", e=E),
                                 running[:].rearrange("p e t -> p t e"), ALU.add))
            link(v.tensor_tensor(place[:], place[:], first_row[:].rearrange("p (o e) -> p o e", o=1).to_broadcast([P, NT, E]),
                                 ALU.add))
            for k in range(TOP_K):
                link(v.tensor_scalar(picked[:], rank[:], float(k), None, ALU.is_equal))
                link(v.tensor_tensor(chosen_place[:], picked[:], place[:], ALU.mult))
                link(v.tensor_reduce(place_k[:, k, :], chosen_place[:], AX_X, ALU.add))
            v.tensor_copy(plan["place"][:], place_k[:]).then_inc(places_ready, 1)
            link(v.tensor_copy(place_part[:], place_k[:]))
            link(v.tensor_scalar(place_part[:], place_part[:], P - 1, None, ALU.bitwise_and))
            link(v.tensor_copy(lane_of[:], place_part[:]))
            link(v.tensor_tensor(block_of[:], place_k[:], lane_of[:], ALU.subtract))
            v.tensor_scalar(block_of[:], block_of[:], 1.0 / P, None, ALU.mult).then_inc(places_split, 1)
            dve.wait_ge(places_split, 1)
            shared.vector_step(dve, 6)
            shared.vector_step(dve, 7)

            def choice_weight(k):
                link(v.tensor_scalar(picked[:], rank[:], float(k), None, ALU.is_equal))
                link(v.tensor_tensor(picked[:], picked[:], weight[:], ALU.mult))
                link(v.tensor_reduce(plan["weight"][:, k, :], picked[:], AX_X, ALU.add))

            def block_hots(start, end):
                for n in range(start, end):
                    k, t = n // NT, n % NT
                    at_least(dve, pairs_summed, n - RING + 1)
                    v.scalar_tensor_tensor(out=block_hot[:, n % RING, :, :],
                                           in0=blocks[:].rearrange("p (o b) -> p o b", o=1).to_broadcast([P, 2, BLOCKS]),
                                           scalar=block_of[:, k, t:t + 1],
                                           in1=token_parts[:, t, :].rearrange("p (h o) -> p h o", o=1).to_broadcast([P, 2, BLOCKS]),
                                           op0=ALU.is_equal, op1=ALU.mult).then_inc(block_hot_ready, 1)

            def per_block(row):
                return row.rearrange("p (o e) -> p o e", o=1).to_broadcast([1, BLOCKS, E])

            def per_expert_of(line):
                return line.rearrange("p (b o) -> p b o", o=1).to_broadcast([1, BLOCKS, E])

            def block_experts():
                link(v.tensor_tensor(passed[:], per_block(ends[0:1, :]), per_expert_of(step_no[:]), ALU.is_le))
                v.tensor_scalar(nonempty[:], n_blocks[0:1, :], 0.5, None, ALU.is_gt)
                link(v.tensor_reduce(table_f[:, 0, :], passed[:], AX_X, ALU.add))
                link(v.tensor_tensor(passed[:], passed[:], per_block(nonempty[:]), ALU.mult))
                v.tensor_scalar(table_f[:, 0, :], table_f[:, 0, :], float(E - 1), None, ALU.min)
                link(v.tensor_reduce(table_f[:, 1, :], passed[:], AX_X, ALU.add))
                v.memset(table_f[:, 2, 0:1], 1.0)
                link(v.tensor_tensor(table_f[:, 2, 1:BLOCKS], table_f[:, 1, 1:BLOCKS], table_f[:, 1, 0:BLOCKS - 1],
                                     ALU.not_equal))

            def slots_free():
                link(v.tensor_tensor_scan(number[:], all_one[0:1, :], nonempty[:], 0.0, ALU.mult, ALU.add))
                link(v.tensor_tensor(number[:], number[:], nonempty[:], ALU.subtract))
                link(v.tensor_scalar(number[:], number[:], float(WEIGHT_SLOTS), None, ALU.add))
                link(v.tensor_tensor(passed[:], per_block(number[:]), per_expert_of(table_f[:, 1, :]), ALU.is_le))
                link(v.tensor_tensor(passed[:], passed[:], per_block(n_blocks[0:1, :]), ALU.mult))
                link(v.tensor_reduce(table_f[:, 3, :], passed[:], AX_X, ALU.add))
                link(v.tensor_scalar(table_f[:, 3, :], table_f[:, 3, :], 1.0, None, ALU.max))
                link(v.tensor_copy(run_i[:], table_f[:, 1, :]))
                link(v.tensor_copy(plan["table"][:], table_f[:]))
                link(v.tensor_scalar(plan["table"][:, 1, :], run_i[:], WEIGHT_SLOTS - 1, None, ALU.bitwise_and))

            block_hots(0, group_ends[0])
            for n in range(2, batches):
                start, end = (group_ends[min(g, GROUPS_OF_SETS - 1)] for g in (n - 2, n - 1))
                for quarter in range(4):
                    block_hots(start + (end - start) * quarter // 4, start + (end - start) * (quarter + 1) // 4)
                    shared.vector_step(dve, 4 * n + quarter)
                    if n == 2:
                        choice_weight(quarter)
                    if n == batches - 2 and quarter == 1:
                        block_experts()
                    if n == batches - 1 and quarter == 1:
                        slots_free()
                    if n == batches - 1 and quarter == 0:
                        dve.wait_ge(pairs_summed, PAIRS)
                        link(v.tensor_copy(token_of[:], tokens_ps[:, 0, BLOCKS:2 * BLOCKS]))
                        link(v.scalar_tensor_tensor(out=token_high[:], in0=tokens_ps[:, 0, 0:BLOCKS], scalar=float(P),
                                                    in1=token_of[:], op0=ALU.mult, op1=ALU.add))
                        link(v.tensor_copy(plan["token"][:], token_high[:]))


def stage_experts(nc, T, keep, plan):
    BLOCKS = keep["blocks"]
    D, C, F = 512, 4, 256
    FC = F // P
    W = C * 2 * F + FC * D
    TURNS = 8
    assert BLOCKS % TURNS == 0 and WEIGHT_SLOTS == 4
    with ExitStack() as ctx:
        def sb(name, shape, dt=F32):
            return ctx.enter_context(nc.sbuf_tensor(name, shape, dt))

        def sem(name):
            return ctx.enter_context(nc.semaphore(name))

        weights = sb("expert_weights", [P, 2, WEIGHT_SLOTS * W], F32R)
        ident = sb("ident2", [P, P])
        rows = sb("rows", [P, 4, D])
        rows_t = sb("rows_t", [P, 2, 2, D], F32R)
        silu_g = sb("silu_g2", [P, 2, F])
        hidden = sb("hidden", [P, 2, F])
        hidden_t = sb("hidden_t", [P, 2, 2, F], F32R)
        result = sb("result", [P, 4, D])
        rows_ps = ctx.enter_context(nc.psum_tensor("rows_ps", [P, 2, D], F32))
        up_ps = ctx.enter_context(nc.psum_tensor("up_ps", [P, 2, 2 * F], F32))
        hid_ps = ctx.enter_context(nc.psum_tensor("hid_ps", [P, 2, 512], F32))
        down_ps = ctx.enter_context(nc.psum_tensor("down_ps", [P, 2, D], F32))

        zeroed, ident_ready = sem("zeroed2"), sem("ident_ready2")
        weights_loaded = [sem(f"weights_loaded{turn}") for turn in range(TURNS)]
        rows_loaded = [sem(f"rows_loaded{turn}") for turn in range(4)]
        stored = [sem(f"result_stored{turn}") for turn in range(4)]
        turned, up_ready, hidden_turned, down_ready = (
            sem(n) for n in ("rows_turned", "up_ready", "hidden_turned", "down_ready"))
        rows_high, rows_ready, silu_ready, hidden_ready, hid_high, hid_ready, result_ready = (
            sem(n) for n in ("rows_high", "rows_ready", "silu2_ready", "hidden_ready", "hid_high", "hid_ready",
                             "result_ready"))
        xn2_rows = T["xn2"].rearrange("b s d -> (b s) d")
        sorted_y = T["sorted_y"].rearrange("(b p) d -> b p d", p=P)
        table = plan["table"]
        block = ctx.enter_context(nc.Block())

        def entry(engine, line, b, top):
            return engine.value_load(table[0:1, line, bass.ds(b, 1)], min_val=0, max_val=top)

        @block.gpsimd
        def _(pool):
            nc.gpsimd.memset(ident[:], 0.0).then_inc(zeroed, 1)
            pool.wait_ge(zeroed, 1)
            nc.gpsimd.affine_select(out=ident[:], in_=ident[:], compare_op=ALU.not_equal, fill=1.0, base=0,
                                    pattern=[[-1, P]], channel_multiplier=1).then_inc(ident_ready, 1)

            def load_weights(b):
                expert = entry(pool, 0, b, HEADS - 1)
                slot = entry(pool, 1, b, WEIGHT_SLOTS - 1)
                new = entry(pool, 2, b, 1)
                free_at = pool.value_load(table[0:1, 3, bass.ds(b, 1)], min_val=1, max_val=BLOCKS)
                if b >= WEIGHT_SLOTS:
                    pool.wait_ge(down_ready, free_at)
                for part, source in enumerate((T["w_high"], T["w_low"])):
                    src = source[bass.ds(expert, 1), :, :].rearrange("a p w -> (a p) w")
                    pool.dma_start(weights[:, part, bass.ds(slot * W, W)], src,
                                   cond=new).then_inc(weights_loaded[b % TURNS], 16)

            def load_rows(b):
                at_least(pool, turned, b - 3)
                pool.indirect_dma_start(rows[:, b % 4, :], None, xn2_rows,
                                        bass.IndirectOffsetOnAxis(ap=plan["token"][:, b:b + 1], axis=0),
                                        bounds_check=keep["tiles"] * P - 1, oob_is_err=False).then_inc(rows_loaded[b % 4], 16)

            for b in range(3):
                load_rows(b)
            for b in range(WEIGHT_SLOTS):
                load_weights(b)
            for b in range(BLOCKS):
                if b + 3 < BLOCKS:
                    load_rows(b + 3)
                if b + WEIGHT_SLOTS < BLOCKS:
                    load_weights(b + WEIGHT_SLOTS)

        @block.sync
        def _(sp):
            def store(b, turn):
                dst = sorted_y[bass.ds(b, 1)].rearrange("a p d -> (a p) d") if not isinstance(b, int) else sorted_y[b]
                sp.wait_ge(result_ready, b + 1)
                sp.dma_start(dst, result[:, turn, :]).then_inc(stored[turn], 16)

            for b in range(4):
                store(b, b)
            with sp.Fori(1, BLOCKS // 4) as four:
                for turn in range(4):
                    store(4 * four + turn, turn)
            for turn in range(4):
                sp.wait_ge(stored[turn], 16 * (BLOCKS // 4))

        @block.tensor
        def _(pe):
            def turn_rows(b, turn, nth):
                s = turn % 2
                pe.wait_ge(rows_loaded[turn], 16 * nth)
                at_least(pe, rows_ready, b - 1)
                for c in range(C):
                    last = nc.tensor.transpose(rows_ps[:, s, c * P:(c + 1) * P], rows[:, turn, c * P:(c + 1) * P], ident[:])
                last.then_inc(turned, 1)

            def up(b, turn, nth, half):
                s = turn % 2
                slot = entry(pe, 1, b, WEIGHT_SLOTS - 1)
                if half == 0:
                    pe.wait_ge(weights_loaded[turn % TURNS], 32 * nth)
                    pe.wait_ge(rows_ready, b + 1)
                    at_least(pe, hidden_ready, b - 1)
                chunks = range(half * C // 2, (half + 1) * C // 2)
                last = split_products(nc, up_ps[:, s, :],
                                      [(rows_t[:, s, 0, c * P:(c + 1) * P], rows_t[:, s, 1, c * P:(c + 1) * P],
                                        weights[:, 0, bass.ds(slot * W + c * 2 * F, 2 * F)],
                                        weights[:, 1, bass.ds(slot * W + c * 2 * F, 2 * F)]) for c in chunks],
                                      first=(half == 0), last=(half == 1))
                if half == 1:
                    last.then_inc(up_ready, 1)

            def turn_hidden(b, s):
                pe.wait_ge(hidden_ready, b + 1)
                at_least(pe, hid_ready, b - 1)
                for c in range(FC):
                    last = nc.tensor.transpose(hid_ps[:, s, c * P:(c + 1) * P], hidden[:, s, c * P:(c + 1) * P], ident[:])
                last.then_inc(hidden_turned, 1)

            def down(b, s):
                slot = entry(pe, 1, b, WEIGHT_SLOTS - 1)
                pe.wait_ge(hid_ready, b + 1)
                at_least(pe, result_ready, b - 1)
                split_products(nc, down_ps[:, s, :],
                               [(hidden_t[:, s, 0, c * P:(c + 1) * P], hidden_t[:, s, 1, c * P:(c + 1) * P],
                                 weights[:, 0, bass.ds(slot * W + C * 2 * F + c * D, D)],
                                 weights[:, 1, bass.ds(slot * W + C * 2 * F + c * D, D)])
                                for c in range(FC)]).then_inc(down_ready, 1)

            pe.wait_ge(ident_ready, 1)
            turn_rows(0, 0, 1)
            turn_rows(1, 1, 1)
            up(0, 0, 1, 0)
            up(0, 0, 1, 1)

            def body(b, turn, rounds, more=True):
                s = turn % 2
                if more:
                    turn_rows(b + 1, (turn + 1) % 4, 2 * rounds + (turn + 1) // 4 + 1)
                up(b, turn, rounds + 1, 0)
                turn_hidden(b - 1, 1 - s)
                up(b, turn, rounds + 1, 1)
                down(b - 1, 1 - s)

            for b in range(1, TURNS):
                body(b, b, 0)
            with pe.Fori(1, BLOCKS // TURNS - 1) as rounds:
                for turn in range(TURNS):
                    body(TURNS * rounds + turn, turn, rounds)
            for turn in range(TURNS):
                body(BLOCKS - TURNS + turn, turn, BLOCKS // TURNS - 1, more=(turn < TURNS - 1))
            turn_hidden(BLOCKS - 1, 1)
            down(BLOCKS - 1, 1)

        @block.scalar
        def _(act):
            def rows_out(b, s):
                act.wait_ge(turned, b + 1)
                at_least(act, up_ready, b - 1)
                nc.scalar.copy(rows_t[:, s, 0, :], rows_ps[:, s, :]).then_inc(rows_high, 1)

            def hidden_out(b, s):
                act.wait_ge(hidden_turned, b + 1)
                at_least(act, down_ready, b - 1)
                nc.scalar.copy(hidden_t[:, s, 0, :], hid_ps[:, s, 0:F]).then_inc(hid_high, 1)

            def silu(b, s):
                act.wait_ge(up_ready, b + 1)
                at_least(act, hidden_ready, b - 1)
                nc.scalar.activation(silu_g[:, s, :], up_ps[:, s, 0:F], ACT.Silu).then_inc(silu_ready, 1)

            def body(b, s):
                rows_out(b + 1, 1 - s)
                hidden_out(b - 1, 1 - s)
                silu(b, s)

            rows_out(0, 0)
            rows_out(1, 1)
            silu(0, 0)
            body(1, 1)
            with act.Fori(1, BLOCKS // 2 - 1) as pair:
                body(2 * pair, 0)
                body(2 * pair + 1, 1)
            body(BLOCKS - 2, 0)
            hidden_out(BLOCKS - 2, 0)
            silu(BLOCKS - 1, 1)
            hidden_out(BLOCKS - 1, 1)

        @block.vector
        def _(dve):
            def rows_low(b, s):
                dve.wait_ge(rows_high, b + 1)
                nc.vector.tensor_tensor(rows_t[:, s, 1, :], rows_ps[:, s, :], rows_t[:, s, 0, :].bitcast(F32),
                                        ALU.subtract).then_inc(rows_ready, 1)

            def hide(b, s):
                dve.wait_ge(silu_ready, b + 1)
                at_least(dve, hidden_turned, b - 1)
                nc.vector.tensor_tensor(hidden[:, s, :], up_ps[:, s, F:2 * F], silu_g[:, s, :], ALU.mult).then_inc(hidden_ready, 1)

            def hidden_low(b, s):
                dve.wait_ge(hid_high, b + 1)
                nc.vector.tensor_tensor(hidden_t[:, s, 1, :], hid_ps[:, s, 0:F], hidden_t[:, s, 0, :].bitcast(F32),
                                        ALU.subtract).then_inc(hid_ready, 1)

            def result_out(b, turn, nth):
                dve.wait_ge(down_ready, b + 1)
                at_least(dve, stored[turn], 16 * nth)
                nc.vector.tensor_copy(result[:, turn, :], down_ps[:, turn % 2, :]).then_inc(result_ready, 1)

            def body(b, turn, fours, more=True):
                s = turn % 2
                if more:
                    rows_low(b + 1, 1 - s)
                hidden_low(b - 1, 1 - s)
                hide(b, s)
                result_out(b - 1, (turn - 1) % 4, fours if turn else fours - 1)

            rows_low(0, 0)
            rows_low(1, 1)
            hide(0, 0)
            for b in range(1, 4):
                body(b, b, 0)
            for b in range(4, 8):
                body(b, b - 4, 1)
            with dve.Fori(2, BLOCKS // 4 - 1) as four:
                for turn in range(4):
                    body(4 * four + turn, turn, four)
            for turn in range(4):
                body(BLOCKS - 4 + turn, turn, BLOCKS // 4 - 1, more=(turn < 3))
            hidden_low(BLOCKS - 1, 1)
            result_out(BLOCKS - 1, 3, BLOCKS // 4 - 1)


def stage_combine(nc, T, keep, plan, shared_w, batches):
    NT = keep["tiles"]
    D = 512
    with ExitStack() as ctx:
        def sb(name, shape, dt=F32):
            return ctx.enter_context(nc.sbuf_tensor(name, shape, dt))

        def sem(name):
            return ctx.enter_context(nc.semaphore(name))

        DEPTH = 8
        LOOK = 4
        picked = sb("picked_rows", [P, DEPTH, TOP_K, D])
        total = sb("total", [P, DEPTH, D])
        gathered = [sem(f"gathered{s}") for s in range(DEPTH)]
        base_loaded = [sem(f"base_loaded{s}") for s in range(DEPTH)]
        out_stored = [sem(f"out_stored{s}") for s in range(DEPTH)]
        last_stored = sem("last_stored")
        added = sem("added")
        B, S, _ = T["x"].shape
        first = B - batches
        shared = shared_expert(nc, T, ctx, shared_w, "shared_last", first, batches, store_sums=False)
        ST = S // P
        stored_tiles = first * ST
        shared_tiles = NT - 6

        def shared_steps(t):
            return range(min(t, shared_tiles) * shared.vector_steps // shared_tiles,
                         min(t + 1, shared_tiles) * shared.vector_steps // shared_tiles)

        def sum_of(t):
            if t < stored_tiles:
                return total[:, t % DEPTH, :]
            return shared.total[:, t // ST - first, t % ST, :]

        base = T["base"].rearrange("b (t p) d -> (b t) p d", p=P)
        out = T["out"].rearrange("b (t p) d -> (b t) p d", p=P)
        block = ctx.enter_context(nc.Block())

        @block.gpsimd
        def _(pool):
            for t in range(NT):
                s = t % DEPTH
                at_least(pool, added, TOP_K * (t - DEPTH + 1))
                for k in range(TOP_K):
                    pool.indirect_dma_start(picked[:, s, k, :], None, T["sorted_y"],
                                            bass.IndirectOffsetOnAxis(ap=plan["place"][:, k, t:t + 1], axis=0),
                                            bounds_check=keep["blocks"] * P - 1,
                                            oob_is_err=False).then_inc(gathered[s], 16)

        @block.sync
        def _(sp):
            def load_base(t):
                at_least(sp, out_stored[t % DEPTH], 16 * (t // DEPTH))
                sp.dma_start(total[:, t % DEPTH, :], base[t]).then_inc(base_loaded[t % DEPTH], 16)

            shared.first_loads(sp)
            for t in range(LOOK):
                load_base(t)
            for t in range(NT):
                for step in shared_steps(t):
                    shared.transfers(sp, step)
                sp.wait_ge(added, TOP_K * (t + 1))
                sp.dma_start(out[t], sum_of(t)).then_inc(out_stored[t % DEPTH] if t < stored_tiles else last_stored, 16)
                if t + LOOK < stored_tiles:
                    load_base(t + LOOK)
            for s in range(DEPTH):
                sp.wait_ge(out_stored[s], 16 * len(range(s, stored_tiles, DEPTH)))
            sp.wait_ge(last_stored, 16 * (NT - stored_tiles))

        @block.tensor
        def _(pe):
            shared.tensor_step(pe, 0, 0)
            shared.tensor_step(pe, 1, 1)
            if batches > 2:
                with pe.Fori(1, batches // 2) as pair:
                    shared.tensor_step(pe, 2 * pair, 0)
                    shared.tensor_step(pe, 2 * pair + 1, 1)
            shared.tensor_end(pe)

        @block.scalar
        def _(act):
            shared.scalar(act)

        @block.vector
        def _(dve):
            shared.vector_start(dve)
            for t in range(NT):
                s = t % DEPTH
                for step in shared_steps(t):
                    shared.vector_step(dve, step)
                dve.wait_ge(gathered[s], 16 * TOP_K * (t // DEPTH + 1))
                if t < stored_tiles:
                    dve.wait_ge(base_loaded[s], 16 * (t // DEPTH + 1))
                else:
                    dve.wait_ge(shared.summed, t - stored_tiles + 1)
                for k in range(TOP_K):
                    at_least(dve, added, TOP_K * t + k)
                    nc.vector.scalar_tensor_tensor(out=sum_of(t), in0=picked[:, s, k, :],
                                                   scalar=plan["weight"][:, k, t:t + 1], in1=sum_of(t),
                                                   op0=ALU.mult, op1=ALU.add).then_inc(added, 1)


def program(nc, T):
    B, S, D = T["x"].shape
    NT = B * S // P
    BLOCKS = NT * TOP_K + HEADS
    last = 2 * (4 * B // 16)
    T = dict(T)
    T["xn2"] = nc.dram_tensor("xn2_rows", [B, S, D], F32).ap()
    T["xn2_t"] = nc.dram_tensor("xn2_columns", [B, P, D // P, S], F32).ap()
    T["w_high"] = nc.dram_tensor("weights_high", T["w_experts"].shape, F32R).ap()
    T["w_low"] = nc.dram_tensor("weights_low", T["w_experts"].shape, F32R).ap()
    T["base"] = nc.dram_tensor("base_rows", [B, S, D], F32).ap()
    T["sorted_y"] = nc.dram_tensor("sorted_y", [BLOCKS * P, D], F32).ap()
    with (
        nc.sbuf_tensor("place_of", [P, TOP_K, NT], U32) as place,
        nc.sbuf_tensor("weight_of", [P, TOP_K, NT], F32) as weight,
        nc.sbuf_tensor("block_table", [1, 4, BLOCKS], I32) as table,
        nc.sbuf_tensor("token_of_place", [P, BLOCKS], U32) as token,
    ):
        plan = {"place": place, "weight": weight, "table": table, "token": token}
        keep = {"tiles": NT, "blocks": BLOCKS}
        with nc.sbuf_tensor("logits_all", [P, NT, HEADS], F32) as logits, ExitStack() as ctx:
            keep["logits"] = logits
            stage_attend(nc, T, keep)
            shared_w = ctx.enter_context(nc.sbuf_tensor("shared_weights", [P, 2, 3, D // P, D], F32R))
            stage_route(nc, T, keep, plan, shared_w, B - last)
            stage_experts(nc, T, keep, plan)
            stage_combine(nc, T, keep, plan, shared_w, last)


def lay_out(inputs):
    x = np.ascontiguousarray(inputs["x"])
    B, S, D = x.shape

    def by_chunk(w):
        w = np.asarray(w)
        w = np.swapaxes(w, -1, -2)
        w = w.reshape(*w.shape[:-2], w.shape[-2] // P, P, w.shape[-1])
        return np.ascontiguousarray(np.swapaxes(w, -3, -2))

    wkv = np.asarray(inputs["L0_xattn_Wkv"])
    w1, w3, w2 = (np.asarray(inputs[f"L0_ffn_w{n}_e"]) for n in (1, 3, 2))
    E = w1.shape[0]
    up = by_chunk(np.concatenate([w1, w3], axis=1)).reshape(E, P, -1)
    down = by_chunk(w2).reshape(E, P, -1)
    shared = np.concatenate([by_chunk(inputs[f"L0_ffn_w{n}_s"]).reshape(P, -1) for n in (1, 3, 2)], axis=1)
    shared = shared.reshape(P, SHARED_PARTS, -1).swapaxes(0, 1)
    return {
        "x": x,
        "ctx_t": by_chunk(inputs["ctx_1024"]),
        "mask_t": by_chunk(inputs["mask_BxSxS2_bk0"]),
        "wq": by_chunk(inputs["L0_xattn_Wq"]),
        "wk": by_chunk(wkv[:D]),
        "wv": by_chunk(wkv[D:]),
        "wo": by_chunk(inputs["L0_xattn_Wo"]),
        "nbias": np.ascontiguousarray(inputs["L0_xattn_nbias"]),
        "wg": by_chunk(inputs["L0_ffn_w_gate"]),
        "w_experts": np.ascontiguousarray(np.concatenate([np.concatenate([up, down], axis=2), shared])),
    }


def kernel(**inputs):
    import concourse.bacc as bacc
    from concourse.bass_utils import run_bass_kernel_spmd

    arrays = {f"in_{name}": a for name, a in lay_out(inputs).items()}
    nc = bacc.Bacc("TRN2", target_bir_lowering=False, num_devices=1)
    T = {name[3:]: nc.dram_tensor(name, a.shape, mybir.dt.from_np(a.dtype), kind="ExternalInput").ap()
         for name, a in arrays.items()}
    T["out"] = nc.dram_tensor("out_rows", inputs["x"].shape, F32, kind="ExternalOutput").ap()
    program(nc, T)
    result = run_bass_kernel_spmd(nc, [arrays], core_ids=[0])
    return result.results[0]["out_rows"]
```
